# Optimizing a Trainium2 kernel written in Bass

```python
import numpy as np
import jax
import jax.numpy as jnp

def _softmax(x, axis=-1):
    return jax.nn.softmax(x, axis=axis)

def _gelu(x):
    return jax.nn.gelu(x, approximate=True)

def _silu(x):
    return jax.nn.silu(x)

def _sigmoid(x):
    return jax.nn.sigmoid(x)

def _layernorm(x, axis=-1, eps=1e-05):
    m = jnp.mean(x, axis=axis, keepdims=True)
    v = jnp.var(x, axis=axis, keepdims=True)
    return (x - m) / jnp.sqrt(v + eps)

def _scatter_add(tgt, idx, src, axis=0):
    return tgt.at[idx].add(src)

def _segment_sum(src, seg, n):
    return jax.ops.segment_sum(src, seg, n)
kernel_name = 'mk_xattn_ffn_d1_seqx_r8_02c0a2'

def setup_inputs(seed: int=0):
    np.random.seed(seed)
    _w = jnp.asarray

    def _rec_inputs():
        import jax
        import jax.numpy as jnp
        _rk = jax.random.key(seed)
        x = -0.0002928 + 1 * jax.random.normal(jax.random.fold_in(_rk, 1), (4, 256, 128), jnp.float32)
        _lenS = 256 - jax.random.randint(jax.random.fold_in(_rk, 7), (4,), 0, max(1, 256 // 4) + 1, jnp.int32)
        _lenS2 = 64 - jax.random.randint(jax.random.fold_in(_rk, 8), (4,), 0, max(1, 64 // 4) + 1, jnp.int32)
        _ctx_512P = jax.random.normal(jax.random.fold_in(_rk, 11), (4, 16, 64), jnp.float32)
        _ctx_512c = jax.random.dirichlet(jax.random.fold_in(_rk, 511), 0.3 * jnp.ones((16,), jnp.float32), (4, 64))
        _ctx_512t = jnp.einsum('bsk,bkd->bsd', _ctx_512c, _ctx_512P)
        _ctx_512t = _ctx_512t * jax.lax.rsqrt(jnp.mean(jnp.square(_ctx_512t)) + 1e-12) * 0.953939
        ctx_512 = 0.00222621 + 0.99962 * (_ctx_512t + 0.3 * jax.random.normal(jax.random.fold_in(_rk, 611), (4, 64, 64), jnp.float32))
        return (x, ctx_512)
    x, ctx_512 = _rec_inputs()

    def _L0_xattn_setup():
        import jax, jax.numpy as jnp
        import numpy as np
        B, T, TC, C, CC, H = (2, 256, 64, 128, 64, 16)
        D = C // H

        def _heads(t):
            b, l, _ = t.shape
            return t.reshape(b, l, H, D).transpose(0, 2, 1, 3)
        key = jax.random.key(seed)
        ks = jax.random.split(key, 18)
        w = lambda k, i, o: jax.random.normal(k, (i, o), jnp.float32) / np.sqrt(i).astype(np.float32)
        return {'x': jax.random.normal(ks[0], (B, T, C), jnp.float32), 'cross_input': jax.random.normal(ks[1], (B, TC, CC), jnp.float32), 'Wk': w(ks[2], C, C), 'bk': jnp.zeros((C,), jnp.float32), 'Wq': w(ks[3], C, C), 'bq': jnp.zeros((C,), jnp.float32), 'Wv': w(ks[4], C, C), 'bv': jnp.zeros((C,), jnp.float32), 'Wck': w(ks[5], CC, C), 'bck': jnp.zeros((C,), jnp.float32), 'Wcq': w(ks[6], C, C), 'bcq': jnp.zeros((C,), jnp.float32), 'Wcv': w(ks[7], CC, C), 'bcv': jnp.zeros((C,), jnp.float32), 'Wp': w(ks[8], C, C), 'bp': jnp.zeros((C,), jnp.float32)}
    _L0_xattn_all = _L0_xattn_setup()
    _L0_xattn_in = {k: v for k, v in _L0_xattn_all.items() if k in ('Wk', 'bk', 'Wq', 'bq', 'Wv', 'bv', 'Wck', 'bck', 'Wcq', 'bcq', 'Wcv', 'bcv', 'Wp', 'bp')}
    del _L0_xattn_all

    def _L0_ffn_setup():
        import jax, jax.numpy as jnp
        import numpy as np
        H, I, E, K = (128, 64, 32, 8)
        B, S = (4, 128)

        def silu(x):
            return x * jax.nn.sigmoid(x)
        key = jax.random.key(seed)
        ks = jax.random.split(key, 14)

        def w(k, shape, fan_in):
            return jax.random.normal(k, shape, jnp.float32) / np.float32(np.sqrt(fan_in))
        return {'hidden_states': jax.random.normal(ks[0], (B, S, H), jnp.float32), 'Wr': w(ks[1], (H, E), H), 'br': jnp.zeros((E,), jnp.float32), 'Wg_s': w(ks[2], (H, I), H), 'bg_s': jnp.zeros((I,), jnp.float32), 'Wu_s': w(ks[3], (H, I), H), 'bu_s': jnp.zeros((I,), jnp.float32), 'Wd_s': w(ks[4], (I, H), I), 'bd_s': jnp.zeros((H,), jnp.float32), 'Wg': w(ks[5], (E, H, I), H), 'bg': jnp.zeros((E, I), jnp.float32), 'Wu': w(ks[6], (E, H, I), H), 'bu': jnp.zeros((E, I), jnp.float32), 'Wd': w(ks[7], (E, I, H), I), 'bd': jnp.zeros((E, H), jnp.float32)}
    _L0_ffn_all = _L0_ffn_setup()
    _L0_ffn_in = {k: v for k, v in _L0_ffn_all.items() if k in ('Wr', 'br', 'Wg_s', 'bg_s', 'Wu_s', 'bu_s', 'Wd_s', 'bd_s', 'Wg', 'bg', 'Wu', 'bu', 'Wd', 'bd')}
    del _L0_ffn_all
    return {'x': x, 'ctx_512': ctx_512, 'L0_xattn_Wk': _L0_xattn_in['Wk'], 'L0_xattn_bk': _L0_xattn_in['bk'], 'L0_xattn_Wq': _L0_xattn_in['Wq'], 'L0_xattn_bq': _L0_xattn_in['bq'], 'L0_xattn_Wv': _L0_xattn_in['Wv'], 'L0_xattn_bv': _L0_xattn_in['bv'], 'L0_xattn_Wck': _L0_xattn_in['Wck'], 'L0_xattn_bck': _L0_xattn_in['bck'], 'L0_xattn_Wcq': _L0_xattn_in['Wcq'], 'L0_xattn_bcq': _L0_xattn_in['bcq'], 'L0_xattn_Wcv': _L0_xattn_in['Wcv'], 'L0_xattn_bcv': _L0_xattn_in['bcv'], 'L0_xattn_Wp': _L0_xattn_in['Wp'], 'L0_xattn_bp': _L0_xattn_in['bp'], 'L0_ffn_Wr': _L0_ffn_in['Wr'], 'L0_ffn_br': _L0_ffn_in['br'], 'L0_ffn_Wg_s': _L0_ffn_in['Wg_s'], 'L0_ffn_bg_s': _L0_ffn_in['bg_s'], 'L0_ffn_Wu_s': _L0_ffn_in['Wu_s'], 'L0_ffn_bu_s': _L0_ffn_in['bu_s'], 'L0_ffn_Wd_s': _L0_ffn_in['Wd_s'], 'L0_ffn_bd_s': _L0_ffn_in['bd_s'], 'L0_ffn_Wg': _L0_ffn_in['Wg'], 'L0_ffn_bg': _L0_ffn_in['bg'], 'L0_ffn_Wu': _L0_ffn_in['Wu'], 'L0_ffn_bu': _L0_ffn_in['bu'], 'L0_ffn_Wd': _L0_ffn_in['Wd'], 'L0_ffn_bd': _L0_ffn_in['bd']}

def reference(x, ctx_512, L0_xattn_Wk, L0_xattn_bk, L0_xattn_Wq, L0_xattn_bq, L0_xattn_Wv, L0_xattn_bv, L0_xattn_Wck, L0_xattn_bck, L0_xattn_Wcq, L0_xattn_bcq, L0_xattn_Wcv, L0_xattn_bcv, L0_xattn_Wp, L0_xattn_bp, L0_ffn_Wr, L0_ffn_br, L0_ffn_Wg_s, L0_ffn_bg_s, L0_ffn_Wu_s, L0_ffn_bu_s, L0_ffn_Wd_s, L0_ffn_bd_s, L0_ffn_Wg, L0_ffn_bg, L0_ffn_Wu, L0_ffn_bu, L0_ffn_Wd, L0_ffn_bd):
    import jax
    import jax.numpy as jnp

    def _L0_xattn_ref(x, cross_input, Wk, bk, Wq, bq, Wv, bv, Wck, bck, Wcq, bcq, Wcv, bcv, Wp, bp):
        import jax, jax.numpy as jnp
        import numpy as np
        B, T, TC, C, CC, H = (2, 256, 64, 128, 64, 16)
        D = C // H

        def _heads(t):
            b, l, _ = t.shape
            return t.reshape(b, l, H, D).transpose(0, 2, 1, 3)
        scale = np.float32(1.0 / np.sqrt(D))
        q = _heads(x @ Wq + bq)
        k = _heads(x @ Wk + bk)
        v = _heads(x @ Wv + bv)
        att = jnp.einsum('bhqd,bhkd->bhqk', q, k) * scale
        causal = jnp.tril(jnp.ones((T, T), bool))
        att = jnp.where(causal[None, None], att, -jnp.inf)
        y = jnp.einsum('bhqk,bhkd->bhqd', jax.nn.softmax(att, axis=-1), v)
        qc = _heads(x @ Wcq + bcq)
        kc = _heads(cross_input @ Wck + bck)
        vc = _heads(cross_input @ Wcv + bcv)
        attc = jnp.einsum('bhqd,bhkd->bhqk', qc, kc) * scale
        y = y + jnp.einsum('bhqk,bhkd->bhqd', jax.nn.softmax(attc, axis=-1), vc)
        y = y.transpose(0, 2, 1, 3).reshape(x.shape[0], T, C)
        return y @ Wp + bp

    def _L0_ffn_ref(hidden_states, Wr, br, Wg_s, bg_s, Wu_s, bu_s, Wd_s, bd_s, Wg, bg, Wu, bu, Wd, bd):
        import jax, jax.numpy as jnp
        import numpy as np
        H, I, E, K = (128, 64, 32, 8)
        B, S = (4, 128)

        def silu(x):
            return x * jax.nn.sigmoid(x)
        b, s, h = hidden_states.shape
        T = b * s
        x = hidden_states.reshape(T, h)
        logits = jnp.dot(x.astype(jnp.float32), Wr) + br
        aff = jax.nn.sigmoid(logits)
        top_v, top_i = jax.lax.top_k(aff, K)
        top_w = top_v / (jnp.sum(top_v, axis=-1, keepdims=True) + 1e-09)
        top_w = top_w.astype(hidden_states.dtype)
        e_total = Wr.shape[1]
        w_full = jnp.zeros((T, e_total), hidden_states.dtype)
        w_full = w_full.at[jnp.arange(T)[:, None], top_i].set(top_w)
        shared = jnp.dot(silu(jnp.dot(x, Wg_s) + bg_s) * (jnp.dot(x, Wu_s) + bu_s), Wd_s) + bd_s
        gate = silu(jnp.einsum('th,ehi->eti', x, Wg) + bg[:, None, :])
        up = jnp.einsum('th,ehi->eti', x, Wu) + bu[:, None, :]
        down = jnp.einsum('eti,eih->eth', gate * up, Wd) + bd[:, None, :]
        routed = jnp.einsum('te,eth->th', w_full, down)
        return (shared + routed).reshape(b, s, h)
    x = x + _L0_xattn_ref(_layernorm(x, axis=-1), ctx_512, L0_xattn_Wk, L0_xattn_bk, L0_xattn_Wq, L0_xattn_bq, L0_xattn_Wv, L0_xattn_bv, L0_xattn_Wck, L0_xattn_bck, L0_xattn_Wcq, L0_xattn_bcq, L0_xattn_Wcv, L0_xattn_bcv, L0_xattn_Wp, L0_xattn_bp)
    x = x + _L0_ffn_ref(_layernorm(x, axis=-1), L0_ffn_Wr, L0_ffn_br, L0_ffn_Wg_s, L0_ffn_bg_s, L0_ffn_Wu_s, L0_ffn_bu_s, L0_ffn_Wd_s, L0_ffn_bd_s, L0_ffn_Wg, L0_ffn_bg, L0_ffn_Wu, L0_ffn_bu, L0_ffn_Wd, L0_ffn_bd)
    return x

_drawn_inputs = setup_inputs


def setup_inputs(seed=0):
    import zlib

    import numpy as np

    out = dict(_drawn_inputs(seed))
    spreads = {'L0_xattn_bk': (0.0, 0.8),
     'L0_xattn_bq': (0.0, 0.282),
     'L0_xattn_bv': (0.0, 0.1),
     'L0_xattn_bck': (0.0, 0.8),
     'L0_xattn_bcq': (0.0, 0.1),
     'L0_xattn_bcv': (0.0, 0.1),
     'L0_xattn_bp': (0.0, 0.1),
     'L0_ffn_br': (0.0, 0.1),
     'L0_ffn_bg_s': (0.0, 0.1),
     'L0_ffn_bu_s': (0.0, 0.1),
     'L0_ffn_bd_s': (0.0, 0.1),
     'L0_ffn_bg': (0.0, 0.495),
     'L0_ffn_bu': (0.0, 0.511),
     'L0_ffn_bd': (0.0, 0.304)}
    factors = {}
    for name, (base, spread) in spreads.items():
        noise = np.random.default_rng([zlib.crc32(name.encode()), seed]).standard_normal(out[name].shape)
        drawn = base * np.exp(spread * noise) if base else spread * noise
        out[name] = jnp.asarray(drawn.astype(out[name].dtype))
    for name, factor in factors.items():
        out[name] = (out[name] * factor).astype(out[name].dtype)
    return out
```

```python
from contextlib import ExitStack

import concourse.bass as bass
from concourse import mybir

F32 = mybir.dt.float32
F32R = mybir.dt.float32r
BF16 = mybir.dt.bfloat16
ACT = mybir.ActivationFunctionType
ALU = mybir.AluOpType
AX = mybir.AxisListType

P = 128
BATCH, SEQ, C = 4, 256, 128
CTX, CTX_C = 64, 64
HEADS, D = 16, 8
GROUP = 4
GROUPS = HEADS // GROUP
STEPS = BATCH * GROUPS
TOKENS = BATCH * SEQ
TILES = TOKENS // P
CHUNK = 512
CHUNKS = TOKENS // CHUNK
PARTS = 3
SHIFT_ROW = PARTS * GROUP * D
PART = GROUP * D
EXPERTS, TOP, INNER = 32, 8, 64
SPREADS = 5
SPREAD_UNITS = 4
PAIRS = EXPERTS // 2
UNITS = PAIRS + 1
SCALE = float(1.0 / D ** 0.5)
LN_EPS = 1e-5
MASKED = -1e30

BIAS_GATE, BIAS_UP = 0, UNITS
BIAS_Q, BIAS_K, BIAS_CQ, BIAS_CK = range(2 * UNITS, 2 * UNITS + 4)
BIAS_ROWS = 2 * UNITS + 4

LEAD = 4
WORK = ([(u, c) for c in range(CHUNKS) for u in range(LEAD)]
        + [(u, c) for u in range(LEAD, UNITS - LEAD) for c in range(CHUNKS)]
        + [(u, c) for c in range(CHUNKS) for u in range(UNITS - LEAD, UNITS)])
ITEMS = len(WORK)
SLOTS = 6
ROUND_STEP = STEPS - SLOTS
LAST_USE = {u: max(n for n, e in enumerate(WORK) if e[0] == u) for u in range(UNITS)}
FIRST_USE = {u: min(n for n, e in enumerate(WORK) if e[0] == u) for u in range(UNITS)}
SPLIT_AT = {LAST_USE[u - SLOTS] + 4: u for u in range(SLOTS, UNITS)}
CHUNK_DONE = [max(n for n, e in enumerate(WORK) if e[1] == c) for c in range(CHUNKS)]
assert all(n < FIRST_USE[u] for n, u in SPLIT_AT.items()) and len(SPLIT_AT) == UNITS - SLOTS

B_NAT0, B_NATC, B_NAT1, B_ST, B_OUT, B_MISC = 0, 1, 2, 4, 6, 7
B_GATE, B_UP, B_WIDE = 0, 2, 4


def build(nc, x, ctx, w, out):
    with ExitStack() as stack:
        def sb(name, shape, dt=F32, until=None):
            return (until or stack).enter_context(nc.sbuf_tensor(name, shape, dt))

        def sem(name):
            return stack.enter_context(nc.semaphore(name))

        rows_dram = [nc.dram_tensor(f"rows_{n}", (GROUP, PARTS * D, GROUPS, TOKENS), F32, kind="Internal").ap()
                     for n in ("q", "k", "cq")]
        crows_dram = nc.dram_tensor("rows_ck", (GROUP, PARTS * D, GROUPS, BATCH * CTX), F32, kind="Internal").ap()
        psum = stack.enter_context(nc.psum_tensor("psum", [P, 8, CHUNK], F32))

        ident = sb("ident", [P, P])
        ident_bf = sb("ident_bf", [P, P], BF16)
        causal = sb("causal", [P, GROUP, P], BF16)
        key_const = sb("key_const", [P, GROUP, SEQ])
        minus_half = sb("minus_half", [P, TILES])
        spread = sb("spread", [P, UNITS, P], F32R)
        x_sb = sb("x_sb", [P, TILES, C])
        ctx_sb = sb("ctx_sb", [P, 2, CTX_C])
        w_qkv = sb("w_qkv", [P, 5, C])
        w_qkv_hi = sb("w_qkv_hi", [P, 5, C], F32R)
        w_qkv_lo = sb("w_qkv_lo", [P, 5, C], F32R)
        w_ctx = sb("w_ctx", [CTX_C, 3, C])
        w_r = sb("w_r", [P, EXPERTS])
        w_r_hi = sb("w_r_hi", [P, EXPERTS], F32R)
        w_r_lo = sb("w_r_lo", [P, EXPERTS], F32R)
        bias_rows = sb("bias_rows", [2 * UNITS, P])
        qkc_bias = sb("qkc_bias", [4, 2, C])
        bias_cols = sb("bias_cols", [P, BIAS_ROWS])
        b_wide = sb("b_wide", [P, 3, C])
        b_r = sb("b_r", [P, EXPERTS])
        b_down = sb("b_down", [P, C])
        b_down_hi = sb("b_down_hi", [P, C], F32R)
        b_down_lo = sb("b_down_lo", [P, C], F32R)
        w_ffn = sb("w_ffn", [P, SLOTS, 3, P])
        w_ffn_hi = sb("w_ffn_hi", [P, SLOTS, 3, P], F32R)
        w_ffn_lo = sb("w_ffn_lo", [P, SLOTS, 3, P], F32R)
        stats = sb("stats", [P, TILES, 6])
        moments = sb("moments", [P, TILES, 2])
        var_eps = sb("var_eps", [P, TILES])
        rstd = sb("rstd", [P, TILES])
        x1 = sb("x1", [P, TILES, C])
        xT_hi = sb("xT_hi", [P, TOKENS], F32R)
        xT_lo = sb("xT_lo", [P, TOKENS], F32R)
        ctxT = sb("ctxT", [CTX_C, BATCH, 2, CTX])
        ck_hi = sb("ck_hi", [P, BATCH * CTX], F32R)
        ck_lo = sb("ck_lo", [P, BATCH * CTX], F32R)
        value = sb("value", [P, TILES, HEADS, D + 1])
        cvalue = sb("cvalue", [P, BATCH, HEADS // 2, 32 + D + 1])
        row_max = sb("row_max", [P, 2, 4, P])
        probs = sb("probs", [P, 4, CHUNK])
        o_sb = sb("o_sb", [P, 2, CHUNK])
        r_den = sb("r_den", [P, 16])
        o_norm = sb("o_norm", [P, 2, 4 * PART])
        y_nat = sb("y_nat", [P, 2, 2, C])
        yT_hi = sb("yT_hi", [P, SEQ], F32R)
        yT_lo = sb("yT_lo", [P, SEQ], F32R)
        x2_norm = sb("x2_norm", [P, 2, C])
        logits = sb("logits", [P, 2, EXPERTS])
        exp_neg = sb("exp_neg", [P, 2, EXPERTS])
        affinity = sb("affinity", [P, 2, EXPERTS])
        top = sb("top", [P, 2, TOP])
        not_top = sb("not_top", [P, 2, EXPERTS])
        top_sum = sb("top_sum", [P, 2])
        r_top = sb("r_top", [P, 2])
        route = sb("route", [P, 2, 2, P])
        routeT = sb("routeT", [P, TOKENS], F32R)

        with ExitStack() as attention:
            spread_f = sb("spread_f", [P, SPREAD_UNITS, P], until=attention)
            qkc_hi = sb("qkc_hi", [P, 3, TOKENS], F32R, until=attention)
            qkc_lo = sb("qkc_lo", [P, 3, TOKENS], F32R, until=attention)
            query_rows = sb("query_rows", [P, 2, GROUPS, 2, SEQ], F32R, until=attention)
            key_blocks = sb("key_blocks", [P, 2, GROUPS, GROUP, SEQ], F32R, until=attention)
            ckey_blocks = sb("ckey_blocks", [P, GROUPS, BATCH, GROUP, CTX], F32R, until=attention)
        gate = sb("gate", [P, 3, CHUNK])
        gated = sb("gated", [P, 3, CHUNK])
        hid = sb("hid", [P, 3, CHUNK])
        hid_hi = sb("hid_hi", [P, 3, CHUNK], F32R)
        hid_lo = sb("hid_lo", [P, 3, CHUNK], F32R)
        ffnT = sb("ffnT", [P, CHUNK])
        result = sb("result", [P, TILES, C])

        in_x = [sem(f"in_x{c}") for c in range(CHUNKS)]
        in_small = sem("in_small")
        in_qkc_bias = sem("in_qkc_bias")
        in_ctx = sem("in_ctx")
        in_w_ctx = sem("in_w_ctx")
        in_w_qkv = sem("in_w_qkv")
        in_wide = sem("in_wide")
        in_router = sem("in_router")
        in_down_bias = sem("in_down_bias")
        in_ffn = [sem(f"in_ffn{k}") for k in range(SLOTS)]
        placed_q = [sem(f"placed_q{k}") for k in range(2)]
        wrote = [[sem(f"wrote_{n}{c}") for n in ("q", "k", "cq")] for c in range(CHUNKS)]
        wrote_ck = sem("wrote_ck")
        placed_k = [sem(f"placed_k{s}") for s in range(2)]
        placed_ck = sem("placed_ck")
        stored = sem("stored")
        zeroed = sem("zeroed")
        slot_zeroed = sem("slot_zeroed")
        have_ident = sem("have_ident")
        have_causal = sem("have_causal")
        have_key_const = sem("have_key_const")
        have_spread = sem("have_spread")
        g_chain = sem("g_chain")
        have_rstd = sem("have_rstd")
        have_x_bp = sem("have_x_bp")
        selected = sem("selected")
        y_added = sem("y_added")
        ffn_lo = sem("ffn_lo")
        v_chain = sem("v_chain")
        var_ready = sem("var_ready")
        x_normed = sem("x_normed")
        have_ident_bf = sem("have_ident_bf")
        w_qkv_split = sem("w_qkv_split")
        qkc_bias_stacked = sem("qkc_bias_stacked")
        have_bias_cols = sem("have_bias_cols")
        have_ctxT = sem("have_ctxT")
        ck_split = sem("ck_split")
        xT_split = sem("xT_split")
        qkc_split = sem("qkc_split")
        have_value = sem("have_value")
        have_cvalue = sem("have_cvalue")
        key_blocks_set = sem("key_blocks_set")
        key_blocks1_set = sem("key_blocks1_set")
        ckey_blocks_set = sem("ckey_blocks_set")
        out_zeroed = sem("out_zeroed")
        max_zeroed = sem("max_zeroed")
        max_done = sem("max_done")
        normalized = sem("normalized")
        yT_split = sem("yT_split")
        x1_ready = sem("x1_ready")
        var2_ready = sem("var2_ready")
        x2_normed = sem("x2_normed")
        x2T_split = sem("x2T_split")
        w_r_split = sem("w_r_split")
        b_down_split = sem("b_down_split")
        logits_ready = sem("logits_ready")
        route_ready = sem("route_ready")
        gated_done = sem("gated_done")
        hid_done = sem("hid_done")
        hid_lo_done = sem("hid_lo_done")
        result_ready = sem("result_ready")
        w_qkv_rounded = sem("w_qkv_rounded")
        ck_rounded = sem("ck_rounded")
        xT_rounded = sem("xT_rounded")
        qkc_rounded = sem("qkc_rounded")
        w_r_rounded = sem("w_r_rounded")
        b_down_rounded = sem("b_down_rounded")
        spread_copied = sem("spread_copied")
        ffn_rounded = sem("ffn_rounded")
        shift_placed = sem("shift_placed")
        exp_done = sem("exp_done")
        o_copied = sem("o_copied")
        yT_rounded = sem("yT_rounded")
        x2T_rounded = sem("x2T_rounded")
        exp_neg_ready = sem("exp_neg_ready")
        routeT_ready = sem("routeT_ready")
        gate_done = sem("gate_done")
        hid_rounded = sem("hid_rounded")
        ffnT_copied = sem("ffnT_copied")
        t_bias = sem("t_bias")
        t_ctx = sem("t_ctx")
        m_ck = sem("m_ck")
        m_cv = sem("m_cv")
        t_x = sem("t_x")
        m_qkc = sem("m_qkc")
        m_v = sem("m_v")
        m_nat = sem("m_nat")
        t_max = sem("t_max")
        m_st = sem("m_st")
        m_out = sem("m_out")
        t_out = sem("t_out")
        t_y = sem("t_y")
        m_proj = sem("m_proj")
        t_x2 = sem("t_x2")
        m_router = sem("m_router")
        t_route = sem("t_route")
        m_gate = sem("m_gate")
        m_up = sem("m_up")
        m_wide = sem("m_wide")
        m_down = sem("m_down")
        t_ffn = sem("t_ffn")

        x_t = x.rearrange("a s c -> (a s) c").rearrange("(t p) c -> p t c", p=P)
        out_t = out.rearrange("a s c -> (a s) c").rearrange("(t p) c -> p t c", p=P)

        def row(v):
            return v.rearrange("(o n) -> o n", o=1)

        def bank(n, cols=CHUNK):
            return psum[:, n, 0:cols]

        def grouped(v):
            return v.rearrange("p (g j d) -> p j d g", j=GROUP, d=D)

        def stacked(v):
            return v.rearrange("p (j d g) -> p j d g", j=GROUP, d=D)

        def tokens(b, tile=None):
            lo = b * SEQ + (tile or 0) * P
            return slice(lo, lo + (SEQ if tile is None else P))

        TAIL = ("y_turn", "project", "x2_turn", "router", "route_turn")
        tail_at = {}
        for b in range(BATCH):
            for n, name in enumerate(TAIL):
                tail_at.setdefault(4 * b + 4 + n, []).append((name, b))
        for s in tail_at:
            tail_at[s].sort(key=lambda e: e[1])
        LAST_TAILS = [e for s in sorted(tail_at) if s >= STEPS for e in tail_at[s]]

        block = stack.enter_context(nc.Block())

        def write_rows(sp, c, tensor):
            cols = slice(c * CHUNK, (c + 1) * CHUNK)
            sp.wait_ge(qkc_split, 3 * c + 1 + (1, 0, 2).index(tensor))
            for part in range(PARTS):
                half = qkc_lo if part == (1 if tensor == 1 else 2) else qkc_hi
                sp.dma_start(rows_dram[tensor][:, D * part:D * (part + 1), :, cols]
                             .rearrange("j d g n -> j (d g) n"), half[:, tensor, cols].bitcast(F32)
                             ).then_inc(wrote[c][tensor], 16)

        def read_rows(sp, b):
            if b == 0:
                sp.wait_ge(key_blocks_set, 1)
            if b == 1:
                sp.wait_ge(key_blocks1_set, 1)
            if b >= 2:
                sp.wait_ge(m_st, 16 * (b - 1))
            sp.wait_ge(wrote[b // 2][1], 48)
            for j in range(GROUP):
                sp.dma_start(key_blocks[24 * j:24 * (j + 1), b % 2, :, j, :].bitcast(F32),
                             rows_dram[1][j][:, :, tokens(b)]).then_inc(placed_k[b % 2], 16)
            for n, tensor in enumerate((0, 2)):
                sp.wait_ge(wrote[b // 2][tensor], 48)
                sp.dma_start(query_rows[0:SHIFT_ROW, b % 2, :, n, :].bitcast(F32),
                             rows_dram[tensor].rearrange("j r g n -> (j r) g n")[:, :, tokens(b)]
                             ).then_inc(placed_q[b % 2], 16)

        def load_unit(sp, u):
            slot = u % SLOTS
            if u >= SLOTS:
                sp.wait_ge(ffn_lo, u - SLOTS + 1)
            if u == PAIRS:
                sp.wait_ge(slot_zeroed, 1)
                sp.dma_start(w_ffn[:, slot, 0, 0:INNER], w["Wg_s"]).then_inc(in_ffn[slot], 16)
                sp.dma_start(w_ffn[:, slot, 1, 0:INNER], w["Wu_s"]).then_inc(in_ffn[slot], 16)
                sp.dma_start(w_ffn[0:INNER, slot, 2, :], w["Wd_s"]).then_inc(in_ffn[slot], 16)
                return
            for n, name in enumerate(("Wg", "Wu")):
                sp.dma_start(w_ffn[:, slot, n, :].rearrange("h (e i) -> h e i", e=2),
                             w[name][2 * u:2 * u + 2].rearrange("e h i -> h e i")).then_inc(in_ffn[slot], 16)
            sp.dma_start(w_ffn[:, slot, 2, :],
                         w["Wd"][2 * u:2 * u + 2].rearrange("e i h -> (e i) h")).then_inc(in_ffn[slot], 16)

        @block.sync
        def _(sp):
            for c in range(CHUNKS):
                sp.dma_start(x_sb[:, 4 * c:4 * c + 4, :], x_t[:, 4 * c:4 * c + 4, :]).then_inc(in_x[c], 16)
            sp.dma_start(w_qkv[:, 0, :], w["Wq"]).then_inc(in_w_qkv, 16)
            sp.dma_start(w_qkv[:, 1, :], w["Wk"]).then_inc(in_w_qkv, 16)
            sp.dma_start(w_qkv[:, 2, :], w["Wcq"]).then_inc(in_w_qkv, 16)
            sp.dma_start(w_qkv[:, 3, :], w["Wv"]).then_inc(in_w_qkv, 16)
            sp.dma_start(w_qkv[:, 4, :], w["Wp"]).then_inc(in_w_qkv, 16)
            sp.dma_start(w_ctx[:, 0, :], w["Wck"]).then_inc(in_w_ctx, 16)
            sp.dma_start(w_ctx[:, 1, :], w["Wcv"]).then_inc(in_w_ctx, 16)
            sp.dma_start(ctx_sb[:, :, :], ctx.rearrange("(h a) k c -> (a k) h c", a=2)).then_inc(in_ctx, 16)
            write_rows(sp, 0, 1)
            write_rows(sp, 0, 0)
            write_rows(sp, 0, 2)
            read_rows(sp, 0)
            sp.wait_ge(ck_split, 1)
            for part, half in enumerate((ck_hi, ck_lo, ck_hi)):
                sp.dma_start(crows_dram[:, D * part:D * (part + 1), :, :].rearrange("j d g n -> j (d g) n"),
                             half[:, :].bitcast(F32)).then_inc(wrote_ck, 16)
            sp.wait_ge(ckey_blocks_set, 1)
            sp.wait_ge(wrote_ck, 48)
            for j in range(GROUP):
                sp.dma_start(ckey_blocks[24 * j:24 * (j + 1), :, :, j, :].rearrange("r g b k -> r (g b) k").bitcast(F32),
                             crows_dram[j].rearrange("r g (b k) -> r (g b) k", b=BATCH)).then_inc(placed_ck, 16)
            read_rows(sp, 1)
            for tensor in (1, 0, 2):
                write_rows(sp, 1, tensor)
            for u in range(SLOTS):
                load_unit(sp, u)
            read_rows(sp, 2)
            read_rows(sp, 3)
            for u in range(SLOTS, UNITS):
                load_unit(sp, u)
            for c in range(CHUNKS):
                sp.wait_ge(result_ready, c + 1)
                sp.dma_start(out_t[:, 4 * c:4 * c + 4, :], result[:, 4 * c:4 * c + 4, :]).then_inc(stored, 16)
            sp.wait_ge(stored, 16 * CHUNKS)

        @block.gpsimd
        def _(pool):
            chained = [0]

            def chain(ins):
                chained[0] += 1
                ins.then_inc(g_chain, 1)
                pool.wait_ge(g_chain, chained[0])

            chain(pool.memset(ident[:, :], 0.0))
            pool.affine_select(out=ident[:, :], in_=ident[:, :], compare_op=ALU.not_equal, fill=1.0, base=0,
                               pattern=[[-1, P]], channel_multiplier=1).then_inc(have_ident, 1)
            pool.memset(bias_rows[:, :], 0.0).then_inc(zeroed, 1)
            pool.memset(minus_half[:, :], -0.5).then_inc(g_chain, 1)
            chained[0] += 1
            pool.wait_ge(g_chain, chained[0])
            for c in range(CHUNKS):
                pool.wait_ge(var_ready, c + 1)
                pool.tensor_tensor(rstd[:, 4 * c:4 * c + 4], var_eps[:, 4 * c:4 * c + 4],
                                   minus_half[:, 0:4], ALU.pow).then_inc(have_rstd, 1)
                if c == 0:
                    chain(pool.memset(key_const[:, :, :], 0.0))
                    pool.affine_select(out=key_const[:, :, :], in_=key_const[:, :, :], compare_op=ALU.not_equal,
                                       fill=-1.0, base=-SHIFT_ROW, pattern=[[-1, GROUP], [0, SEQ]],
                                       channel_multiplier=1).then_inc(have_key_const, 1)
            chain(pool.memset(causal[:, :, :], 0.0))
            pool.affine_select(out=causal[:, :, :], in_=causal[:, :, :], compare_op=ALU.is_ge, fill=MASKED, base=0,
                               pattern=[[0, GROUP], [-1, P]], channel_multiplier=1).then_inc(have_causal, 1)
            pool.memset(value[:, :, :, :], 1.0).then_inc(zeroed, 1)
            pool.memset(cvalue[:, :, :, :], 0.0).then_inc(g_chain, 1)
            chained[0] += 1
            pool.wait_ge(g_chain, chained[0])
            pool.memset(cvalue[0:CTX, :, :, D:D + 1], 1.0).then_inc(zeroed, 1)
            pool.wait_ge(zeroed, 3)
            pool.memset(cvalue[CTX:P, :, :, 32 + D:32 + D + 1], 1.0).then_inc(zeroed, 1)
            pool.wait_ge(zeroed, 4)
            pool.memset(b_down[:, :], 0.0).then_inc(zeroed, 1)
            chain(pool.memset(route[:, :, :, :], 0.0))
            pool.memset(route[:, :, :, 2 * EXPERTS:2 * EXPERTS + 1], 1.0).then_inc(zeroed, 1)
            pool.wait_ge(in_wide, 48)
            pool.wait_ge(x_normed, TILES)
            for t in range(TILES):
                ins = pool.tensor_tensor(x_sb[:, t, :], x_sb[:, t, :], b_wide[:, 2, :], ALU.add)
            ins.then_inc(have_x_bp, 1)

            def make_spread(k):
                if k:
                    pool.wait_ge(spread_copied, k)
                body = spread_f[:, :, :].rearrange("p u (e i) -> p u e i", e=2)
                chain(pool.memset(spread_f[:, :, :], 0.0))
                if k < PAIRS // SPREAD_UNITS:
                    for half in range(2):
                        ins = pool.affine_select(out=body, in_=body, compare_op=ALU.not_equal, fill=1.0,
                                                 base=-EXPERTS * half - 2 * SPREAD_UNITS * k,
                                                 pattern=[[-2, SPREAD_UNITS], [-1, 2], [0, INNER]],
                                                 channel_multiplier=1)
                        if half == 0:
                            chain(ins)
                else:
                    ins = pool.affine_select(out=spread_f[:, 0, :], in_=spread_f[:, 0, :],
                                             compare_op=ALU.not_equal, fill=1.0, base=-2 * EXPERTS,
                                             pattern=[[0, P]], channel_multiplier=1)
                ins.then_inc(have_spread, 1)

            def split_unit(u):
                k = u % SLOTS
                pool.wait_ge(ffn_rounded, u + 1)
                ins = pool.tensor_tensor(w_ffn_lo[:, k, :, :], w_ffn[:, k, :, :], w_ffn_hi[:, k, :, :].bitcast(F32),
                                         ALU.subtract).then_inc(ffn_lo, 1)
                if u == PAIRS - SLOTS:
                    pool.wait_ge(ffn_lo, u + 1)
                    pool.memset(w_ffn[:, k, :, :], 0.0).then_inc(slot_zeroed, 1)

            def add_y(i):
                b, g = divmod(i, GROUPS)
                pool.wait_ge(normalized, i + 1)
                if g == 0 and b >= 2:
                    pool.wait_ge(t_y, b - 1)
                pool.tensor_tensor(y_nat[:, b % 2, :, PART * g:PART * (g + 1)],
                                   o_norm[:, i % 2, 0:2 * PART].rearrange("p (t c) -> p t c", t=2),
                                   o_norm[:, i % 2, 2 * PART:4 * PART].rearrange("p (t c) -> p t c", t=2),
                                   ALU.add).then_inc(y_added, 1)

            def tail(name, b):
                if name == "project":
                    pool.wait_ge(var2_ready, b + 1)
                    pool.tensor_tensor(rstd[:, 2 * b:2 * b + 2], var_eps[:, 2 * b:2 * b + 2], minus_half[:, 0:2],
                                       ALU.pow).then_inc(have_rstd, 1)

            for i in range(STEPS):
                pool.wait_ge(exp_done, 4 * i + 2)
                for_k0 = probs[:, 0:2, :].rearrange("p c (j q) -> p (c j) q", j=2)[:, :, 0:P]
                pool.affine_select(out=for_k0, in_=for_k0, compare_op=ALU.is_ge, fill=0.0, base=0,
                                   pattern=[[0, GROUP], [1, P]], channel_multiplier=-1).then_inc(selected, 1)
                pool.wait_ge(exp_done, 4 * i + 3)
                for_k1 = probs[:, 2, :].rearrange("p (j q) -> p j q", j=GROUP)
                pool.affine_select(out=for_k1, in_=for_k1, compare_op=ALU.is_ge, fill=0.0, base=0,
                                   pattern=[[0, GROUP], [1, P]], channel_multiplier=-1).then_inc(selected, 1)
                if i:
                    add_y(i - 1)
                for name, b in tail_at.get(i, ()):
                    tail(name, b)
                if i < SPREADS:
                    make_spread(i)
                if ROUND_STEP <= i < ROUND_STEP + SLOTS:
                    split_unit(i - ROUND_STEP)
            add_y(STEPS - 1)
            for name, b in LAST_TAILS:
                tail(name, b)
            for u in range(SLOTS, UNITS):
                split_unit(u)

        @block.scalar
        def _(act):
            act.wait_ge(zeroed, 1)
            for u, name, r0 in ((0, "bg", BIAS_GATE), (0, "bu", BIAS_UP)):
                act.dma_start(bias_rows[r0:r0 + PAIRS, :],
                              w[name].rearrange("(p e) i -> p (e i)", e=2)).then_inc(in_small, 16)
            act.dma_start(bias_rows[PAIRS:PAIRS + 1, 0:INNER], row(w["bg_s"])).then_inc(in_small, 16)
            act.dma_start(bias_rows[BIAS_UP + PAIRS:BIAS_UP + UNITS, 0:INNER], row(w["bu_s"])).then_inc(in_small, 16)
            for name, r0 in (("bq", BIAS_Q), ("bk", BIAS_K), ("bcq", BIAS_CQ), ("bck", BIAS_CK)):
                act.dma_start(qkc_bias[r0 - BIAS_Q:r0 - BIAS_Q + 1, 0, :], row(w[name])).then_inc(in_qkc_bias, 16)
            for n, name in enumerate(("bv", "bcv", "bp")):
                act.dma_start(b_wide[:, n, :], row(w[name]).to_broadcast([P, C])).then_inc(in_wide, 16)
            act.wait_ge(in_w_qkv, 80)
            for n in range(3):
                act.copy(stacked(w_qkv_hi[:, n, :]), grouped(w_qkv[:, n, :]))
            act.copy(w_qkv_hi[:, 3:5, :], w_qkv[:, 3:5, :]).then_inc(w_qkv_rounded, 1)

            def copy_hi(dst, src, done):
                act.copy(dst, src).then_inc(done, 1)

            act.wait_ge(have_bias_cols, 1)
            for c in range(CHUNKS):
                cols = slice(c * CHUNK, (c + 1) * CHUNK)
                if c == 1:
                    act.wait_ge(m_ck, 1)
                    act.activation(ck_hi[:, :], psum[:, 6, SEQ:2 * SEQ], ACT.Identity,
                                   bias=bias_cols[:, BIAS_CK:BIAS_CK + 1]).then_inc(ck_rounded, 1)
                act.wait_ge(t_x, c + 1)
                copy_hi(xT_hi[:, cols], bank(c), xT_rounded)
                for n, (tensor, bias) in enumerate(((1, BIAS_K), (0, BIAS_Q), (2, BIAS_CQ))):
                    act.wait_ge(m_qkc, 3 * c + n + 1)
                    act.activation(qkc_hi[:, tensor, cols], bank(2 + n), ACT.Identity,
                                   bias=bias_cols[:, bias:bias + 1]).then_inc(qkc_rounded, 1)
            act.wait_ge(have_key_const, 1)
            for g in range(GROUPS):
                ins = act.copy(key_blocks[:, 1, g, :, :], key_const[:, :, :])
            ins.then_inc(key_blocks1_set, 1)
            act.dma_start(w_r[:, :], w["Wr"]).then_inc(in_router, 16)
            act.dma_start(b_r[:, :], row(w["br"]).to_broadcast([P, EXPERTS])).then_inc(in_router, 16)
            act.wait_ge(zeroed, 5)
            act.dma_start(b_down[0:EXPERTS, :], w["bd"]).then_inc(in_down_bias, 16)
            act.dma_start(b_down[EXPERTS:2 * EXPERTS, :], w["bd"]).then_inc(in_down_bias, 16)
            act.dma_start(b_down[2 * EXPERTS:2 * EXPERTS + 1, :], row(w["bd_s"])).then_inc(in_down_bias, 16)

            def shift(i):
                b, g = divmod(i, GROUPS)
                act.wait_ge(t_max, i + 1)
                act.copy(query_rows[SHIFT_ROW:P, b % 2, g, :, :],
                         psum[SHIFT_ROW:P, B_MISC, :].rearrange("p (s n) -> p s n", s=2)).then_inc(shift_placed, 1)

            def exps(i):
                for c in range(4):
                    act.wait_ge(m_st, 4 * i + c + 1)
                    act.activation(probs[:, c, :], bank(B_ST + c % 2), ACT.Exp,
                                   scale=SCALE).then_inc(exp_done, 1)

            def copy_out(i):
                act.wait_ge(m_out, i + 1)
                if i >= 2:
                    act.wait_ge(t_out, i - 1)
                act.copy(o_sb[:, i % 2, :], bank(B_OUT)).then_inc(o_copied, 1)

            def round_unit(u):
                k = u % SLOTS
                act.wait_ge(in_ffn[k], 48 * (u // SLOTS + 1))
                if u >= SLOTS:
                    act.wait_ge(m_down, LAST_USE[u - SLOTS] + 1)
                act.copy(w_ffn_hi[:, k, :, :], w_ffn[:, k, :, :]).then_inc(ffn_rounded, 1)

            def tail(name, b):
                if name == "y_turn":
                    act.wait_ge(t_y, b + 1)
                    copy_hi(yT_hi[:, :], bank(B_MISC, SEQ), yT_rounded)
                if name == "x2_turn":
                    act.wait_ge(t_x2, b + 1)
                    copy_hi(xT_hi[:, tokens(b)], bank(B_MISC, SEQ), x2T_rounded)
                if name == "router":
                    act.wait_ge(logits_ready, b + 1)
                    act.activation(exp_neg[:, :, :], logits[:, :, :], ACT.Exp, scale=-1.0).then_inc(exp_neg_ready, 1)
                if name == "route_turn":
                    act.wait_ge(t_route, b + 1)
                    act.copy(routeT[:, tokens(b)], bank(B_MISC, SEQ)).then_inc(routeT_ready, 1)

            shift(0)
            for i in range(STEPS):
                exps(i)
                if i == 1:
                    act.wait_ge(in_router, 32)
                    copy_hi(w_r_hi[:, :], w_r[:, :], w_r_rounded)
                    act.wait_ge(in_down_bias, 48)
                    copy_hi(b_down_hi[:, :], b_down[:, :], b_down_rounded)
                if i < SPREADS:
                    act.wait_ge(have_spread, i + 1)
                    n = min(SPREAD_UNITS, UNITS - SPREAD_UNITS * i)
                    act.copy(spread[:, SPREAD_UNITS * i:SPREAD_UNITS * i + n, :],
                             spread_f[:, 0:n, :]).then_inc(spread_copied, 1)
                for name, b in tail_at.get(i, ()):
                    tail(name, b)
                if ROUND_STEP <= i < ROUND_STEP + SLOTS:
                    round_unit(i - ROUND_STEP)
                if i + 1 < STEPS:
                    shift(i + 1)
                copy_out(i)
            for name, b in LAST_TAILS:
                tail(name, b)

            for n in range(ITEMS + 1):
                if n < ITEMS:
                    u, _ = WORK[n]
                    act.wait_ge(m_gate, n + 1)
                    if n >= 3:
                        act.wait_ge(gated_done, n - 2)
                    act.activation(gate[:, n % 3, :], bank(B_GATE + n % 2), ACT.Silu,
                                   bias=bias_cols[:, BIAS_GATE + u:BIAS_GATE + u + 1]).then_inc(gate_done, 1)
                if n >= 1:
                    act.wait_ge(hid_done, n)
                    if n >= 4:
                        act.wait_ge(m_down, n - 3)
                    act.copy(hid_hi[:, (n - 1) % 3, :], hid[:, (n - 1) % 3, :]).then_inc(hid_rounded, 1)
                if n in SPLIT_AT:
                    round_unit(SPLIT_AT[n])
                if n == CHUNK_DONE[0] + 4:
                    act.wait_ge(m_down, CHUNK_DONE[0] + 1)
                    act.copy(ffnT[:, :], bank(6)).then_inc(ffnT_copied, 1)
            act.wait_ge(m_down, ITEMS)
            act.wait_ge(t_ffn, 1)
            act.copy(ffnT[:, :], bank(7)).then_inc(ffnT_copied, 1)

        @block.vector
        def _(dve):
            chained = [0]

            def chain(ins):
                chained[0] += 1
                ins.then_inc(v_chain, 1)
                dve.wait_ge(v_chain, chained[0])

            dve.memset(bank(B_OUT), 0.0).then_inc(out_zeroed, 1)
            dve.memset(row_max[:, :, :, :], 0.0).then_inc(max_zeroed, 1)

            def norm_stats(src, tiles, done):
                for k in range(tiles.start, tiles.stop):
                    ins = dve.bn_stats(stats[:, k, :], src[:, k, :])
                chain(ins)
                for k in range(tiles.start, tiles.stop):
                    ins = dve.bn_aggr(moments[:, k, :], stats[:, k, :])
                chain(ins)
                dve.tensor_scalar(var_eps[:, tiles], moments[:, tiles, 1], LN_EPS, None, ALU.add).then_inc(done, 1)

            def lo_half(dst, src, hi, done):
                return dve.tensor_tensor(dst, src, hi.bitcast(F32), ALU.subtract).then_inc(done, 1)

            for c in range(CHUNKS):
                dve.wait_ge(in_x[c], 16)
                norm_stats(x_sb, slice(4 * c, 4 * c + 4), var_ready)
            dve.wait_ge(in_qkc_bias, 64)
            dve.tensor_copy(stacked(qkc_bias[:, 1, :]), grouped(qkc_bias[:, 0, :])).then_inc(qkc_bias_stacked, 1)
            dve.wait_ge(have_ident, 1)
            dve.tensor_copy(ident_bf[:, :], ident[:, :]).then_inc(have_ident_bf, 1)
            for c in range(CHUNKS):
                dve.wait_ge(have_rstd, c + 1)
                for t in range(4 * c, 4 * c + 4):
                    dve.tensor_scalar(x1[:, t, :], x_sb[:, t, :], moments[:, t, 0:1], rstd[:, t:t + 1],
                                      ALU.subtract, ALU.mult).then_inc(x_normed, 1)
            dve.wait_ge(w_qkv_rounded, 1)
            for n in range(3):
                dve.tensor_tensor(stacked(w_qkv_lo[:, n, :]), grouped(w_qkv[:, n, :]),
                                  stacked(w_qkv_hi[:, n, :]).bitcast(F32), ALU.subtract)
            lo_half(w_qkv_lo[:, 3:5, :], w_qkv[:, 3:5, :], w_qkv_hi[:, 3:5, :], w_qkv_split)
            dve.wait_ge(t_bias, 1)
            dve.tensor_copy(bias_cols[:, :], psum[:, 7, 0:BIAS_ROWS]).then_inc(have_bias_cols, 1)
            dve.wait_ge(t_ctx, 1)
            for k in range(2):
                dve.tensor_copy(ctxT[:, :, k, :],
                                psum[0:CTX_C, 6, 0:BATCH * CTX].rearrange("p (b k) -> p b k", b=BATCH))
            dve.wait_ge(in_w_ctx, 32)
            dve.tensor_copy(stacked(w_ctx[:, 2, :]), grouped(w_ctx[:, 0, :])).then_inc(have_ctxT, 1)

            def value_add(dst, src, which, done):
                dve.tensor_tensor(dst, src, which, ALU.add).then_inc(done, 1)

            def chunk(c):
                cols = slice(c * CHUNK, (c + 1) * CHUNK)
                dve.wait_ge(xT_rounded, c + 1)
                lo_half(xT_lo[:, cols], bank(c), xT_hi[:, cols], xT_split)
                for n, (tensor, bias) in enumerate(((1, BIAS_K), (0, BIAS_Q), (2, BIAS_CQ))):
                    dve.wait_ge(qkc_rounded, 3 * c + n + 1)
                    dve.scalar_tensor_tensor(out=qkc_lo[:, tensor, cols], in0=bank(2 + n),
                                             scalar=bias_cols[:, bias:bias + 1],
                                             in1=qkc_hi[:, tensor, cols].bitcast(F32),
                                             op0=ALU.add, op1=ALU.subtract).then_inc(qkc_split, 1)
                if c == 0:
                    dve.wait_ge(have_bias_cols, 1)
                dve.wait_ge(m_v, c + 1)
                if c == 0:
                    dve.wait_ge(in_wide, 48)
                    dve.wait_ge(zeroed, 2)
                value_add(value[:, 4 * c:4 * c + 4, :, 0:D],
                          bank(5).rearrange("p (t h d) -> p t h d", t=4, h=HEADS),
                          b_wide[:, 0, :].rearrange("p (h d) -> p h d", h=HEADS).unsqueeze(1)
                          .to_broadcast([P, 4, HEADS, D]), have_value)

            dve.wait_ge(have_bias_cols, 1)
            chunk(0)
            dve.wait_ge(have_key_const, 1)
            for g in range(GROUPS):
                ins = dve.tensor_copy(key_blocks[:, 0, g, :, :], key_const[:, :, :])
            ins.then_inc(key_blocks_set, 1)
            for g in range(GROUPS):
                ins = dve.tensor_copy(ckey_blocks[:, g, :, :, :],
                                      key_const[:, :, 0:CTX].unsqueeze(1).to_broadcast([P, BATCH, GROUP, CTX]))
            ins.then_inc(ckey_blocks_set, 1)
            dve.wait_ge(ck_rounded, 1)
            dve.scalar_tensor_tensor(out=ck_lo[:, :], in0=psum[:, 6, SEQ:2 * SEQ],
                                     scalar=bias_cols[:, BIAS_CK:BIAS_CK + 1], in1=ck_hi[:, :].bitcast(F32),
                                     op0=ALU.add, op1=ALU.subtract).then_inc(ck_split, 1)
            dve.wait_ge(m_cv, 1)
            dve.wait_ge(zeroed, 4)
            for half in range(2):
                rows = slice(CTX * half, CTX * (half + 1))
                src = psum[rows, 7, :].rearrange("p (b q e d) -> p b q e d", b=BATCH, e=2, d=D)[:, :, :, half, :]
                wide = b_wide[rows, 1, :].rearrange("p (q e d) -> p q e d", e=2, d=D)[:, :, half, :]
                value_add(cvalue[rows, :, :, 32 * half:32 * half + D], src,
                          wide.unsqueeze(1).to_broadcast([CTX, BATCH, HEADS // 2, D]), have_cvalue)
            chunk(1)

            def maxima(i):
                to = row_max[:, i % 2, :, :]
                if i >= 2:
                    dve.wait_ge(t_max, i - 1)
                dve.wait_ge(m_nat, 3 * i + 1)
                dve.tensor_reduce(to[:, 0, SHIFT_ROW:SHIFT_ROW + GROUP], bank(B_NAT0).rearrange("p (j k) -> p j k", j=GROUP),
                                  AX.X, ALU.max).then_inc(max_done, 1)
                dve.wait_ge(m_nat, 3 * i + 2)
                dve.tensor_reduce(to[:, 2:4, SHIFT_ROW:SHIFT_ROW + GROUP],
                                  bank(B_NATC).rearrange("p (t j k) -> p t j k", t=2, j=GROUP),
                                  AX.X, ALU.max).then_inc(max_done, 1)
                dve.wait_ge(m_nat, 3 * i + 3)
                dve.tensor_reduce(to[:, 1, SHIFT_ROW:SHIFT_ROW + GROUP],
                                  psum[:, B_NAT1:B_NAT1 + 2, :].rearrange("p k (j c) -> p j k c", j=GROUP),
                                  AX.XY, ALU.max).then_inc(max_done, 1)

            def normalize(i):
                turned = bank(B_MISC).rearrange("p (j d) -> p j d", d=32)
                dve.wait_ge(t_out, i + 1)
                chain(dve.reciprocal(r_den[:, :].unsqueeze(2), turned[:, :, D:D + 1]))
                if i >= 2:
                    dve.wait_ge(y_added, i - 1)
                dve.tensor_tensor(o_norm[:, i % 2, :].rearrange("p (j d) -> p j d", d=D), turned[:, :, 0:D],
                                  r_den[:, :].unsqueeze(2).to_broadcast([P, 16, D]), ALU.mult)\
                   .then_inc(normalized, 1)

            def tail(name, b):
                mine = slice(2 * b, 2 * b + 2)
                if name == "y_turn":
                    dve.wait_ge(yT_rounded, b + 1)
                    lo_half(yT_lo[:, :], bank(B_MISC, SEQ), yT_hi[:, :], yT_split)
                if name == "project":
                    dve.wait_ge(m_proj, b + 1)
                    if b == 0:
                        dve.wait_ge(have_x_bp, 1)
                    dve.tensor_tensor(x1[:, mine, :], bank(B_MISC, SEQ).rearrange("p (t c) -> p t c", t=2),
                                      x_sb[:, mine, :], ALU.add).then_inc(x1_ready, 1)
                    dve.wait_ge(x1_ready, b + 1)
                    norm_stats(x1, mine, var2_ready)
                    dve.wait_ge(have_rstd, CHUNKS + b + 1)
                    for t in range(2):
                        k = 2 * b + t
                        dve.tensor_scalar(x2_norm[:, t, :], x1[:, k, :], moments[:, k, 0:1], rstd[:, k:k + 1],
                                          ALU.subtract, ALU.mult).then_inc(x2_normed, 1)
                if name == "x2_turn":
                    dve.wait_ge(x2T_rounded, b + 1)
                    lo_half(xT_lo[:, tokens(b)], bank(B_MISC, SEQ), xT_hi[:, tokens(b)],
                            x2T_split)
                if name == "router":
                    dve.wait_ge(m_router, b + 1)
                    dve.tensor_tensor(logits[:, :, :], bank(B_MISC, 2 * EXPERTS).rearrange("p (t e) -> p t e", t=2),
                                      b_r[:, :].unsqueeze(1).to_broadcast([P, 2, EXPERTS]),
                                      ALU.add).then_inc(logits_ready, 1)
                    dve.wait_ge(exp_neg_ready, b + 1)
                    chain(dve.tensor_scalar(exp_neg[:, :, :], exp_neg[:, :, :], 1.0, None, ALU.add))
                    chain(dve.reciprocal(affinity[:, :, :], exp_neg[:, :, :]))
                    for t in range(2):
                        ins = dve.max(top[:, t, :], affinity[:, t, :])
                    chain(ins)
                    for t in range(2):
                        dve.match_replace(not_top[:, t, :], top[:, t, :], affinity[:, t, :], -1.0)
                    chain(dve.tensor_reduce(top_sum[:, :], top[:, :, :], AX.X, ALU.add))
                    dve.scalar_tensor_tensor(out=affinity[:, :, :], in0=not_top[:, :, :], scalar=0.0,
                                             in1=affinity[:, :, :], op0=ALU.is_lt, op1=ALU.mult)
                    chain(dve.tensor_scalar(top_sum[:, :], top_sum[:, :], 1e-9, None, ALU.add))
                    chain(dve.reciprocal(r_top[:, :], top_sum[:, :]))
                    chain(dve.tensor_tensor(affinity[:, :, :], affinity[:, :, :],
                                            r_top[:, :].unsqueeze(2).to_broadcast([P, 2, EXPERTS]), ALU.mult))
                    if b >= 2:
                        dve.wait_ge(t_route, b - 1)
                    if b == 0:
                        dve.wait_ge(zeroed, 6)
                    to = route[:, b % 2, :, :]
                    chain(dve.tensor_copy(to[:, :, 0:EXPERTS].bitcast(F32R), affinity[:, :, :]))
                    dve.tensor_tensor(to[:, :, EXPERTS:2 * EXPERTS], affinity[:, :, :], to[:, :, 0:EXPERTS],
                                      ALU.subtract).then_inc(route_ready, 1)

            maxima(0)
            for i in range(STEPS):
                if i:
                    normalize(i - 1)
                if i + 1 < STEPS:
                    maxima(i + 1)
                if i == 1:
                    dve.wait_ge(w_r_rounded, 1)
                    lo_half(w_r_lo[:, :], w_r[:, :], w_r_hi[:, :], w_r_split)
                    dve.wait_ge(b_down_rounded, 1)
                    lo_half(b_down_lo[:, :], b_down[:, :], b_down_hi[:, :], b_down_split)
                for name, b in tail_at.get(i, ()):
                    tail(name, b)
            normalize(STEPS - 1)
            for name, b in LAST_TAILS:
                tail(name, b)

            def residual(c):
                dve.wait_ge(t_ffn, c + 1)
                dve.tensor_tensor(result[:, 4 * c:4 * c + 4, :], bank(6).rearrange("p (t h) -> p t h", t=4),
                                  x1[:, 4 * c:4 * c + 4, :], ALU.add).then_inc(result_ready, 1)

            for n in range(ITEMS + 1):
                if n < ITEMS:
                    u, _ = WORK[n]
                    dve.wait_ge(m_up, n + 1)
                    dve.wait_ge(gate_done, n + 1)
                    dve.scalar_tensor_tensor(out=gated[:, n % 3, :], in0=bank(B_UP + n % 2),
                                             scalar=bias_cols[:, BIAS_UP + u:BIAS_UP + u + 1],
                                             in1=gate[:, n % 3, :], op0=ALU.add, op1=ALU.mult).then_inc(gated_done, 1)
                if n >= 1:
                    dve.wait_ge(hid_rounded, n)
                    if n >= 4:
                        dve.wait_ge(m_down, n - 3)
                    k = (n - 1) % 3
                    lo_half(hid_lo[:, k, :], hid[:, k, :], hid_hi[:, k, :], hid_lo_done)
                if n < ITEMS:
                    dve.wait_ge(m_wide, n + 1)
                    dve.wait_ge(gated_done, n + 1)
                    if n >= 3:
                        dve.wait_ge(hid_rounded, n - 2)
                        dve.wait_ge(hid_lo_done, n - 2)
                    dve.tensor_tensor(hid[:, n % 3, :], gated[:, n % 3, :], bank(B_WIDE + n % 2),
                                      ALU.mult).then_inc(hid_done, 1)
            residual(0)
            residual(1)

        def turn_ffn(pe, c):
            pe.wait_ge(ffnT_copied, c + 1)
            if c:
                pe.wait_ge(result_ready, c)
            for k in range(4):
                ins = pe.transpose(psum[:, 6, P * k:P * (k + 1)], ffnT[:, P * k:P * (k + 1)], ident[:, :])
            ins.then_inc(t_ffn, 1)

        @block.tensor
        def _(pe):
            misc_read = []

            def take_misc(reader, count):
                if misc_read:
                    pe.wait_ge(*misc_read.pop())
                misc_read.append((reader, count))

            def product3(dst, w_hi, w_lo, x_hi, x_lo, start=True, stop=True):
                pe.matmul(dst, w_hi, x_hi, start=start, stop=False, skip_group_check=True)
                pe.matmul(dst, w_hi, x_lo, start=False, stop=False, skip_group_check=True)
                return pe.matmul(dst, w_lo, x_hi, start=False, stop=stop, skip_group_check=True)

            pe.wait_ge(have_ident, 1)
            pe.wait_ge(in_small, 64)
            pe.transpose(psum[:, 7, 0:2 * UNITS], bias_rows[:, :], ident[0:2 * UNITS, 0:2 * UNITS])
            pe.wait_ge(qkc_bias_stacked, 1)
            pe.transpose(psum[:, 7, 2 * UNITS:BIAS_ROWS], qkc_bias[:, 1, :], ident[0:4, 0:4]).then_inc(t_bias, 1)
            pe.wait_ge(in_ctx, 16)
            for h in range(2):
                ins = pe.transpose(psum[0:CTX_C, 6, P * h:P * (h + 1)], ctx_sb[:, h, :], ident[:, :])
            ins.then_inc(t_ctx, 1)

            def turn_x(c):
                pe.wait_ge(x_normed, 4 * c + 4)
                for k in range(4):
                    ins = pe.transpose(psum[:, c, P * k:P * (k + 1)], x1[:, 4 * c + k, :], ident[:, :])
                ins.then_inc(t_x, 1)

            def project(c):
                cols = slice(c * CHUNK, (c + 1) * CHUNK)
                pe.wait_ge(xT_split, c + 1)
                if c == 0:
                    pe.wait_ge(w_qkv_split, 1)
                for n, tensor in enumerate((1, 0, 2)):
                    if c:
                        pe.wait_ge(qkc_split, n + 1)
                    product3(bank(2 + n), w_qkv_hi[:, tensor, :], w_qkv_lo[:, tensor, :], xT_hi[:, cols],
                             xT_lo[:, cols]).then_inc(m_qkc, 1)
                if c:
                    pe.wait_ge(have_value, 1)
                for k in range(4):
                    t = slice(c * CHUNK + k * P, c * CHUNK + (k + 1) * P)
                    ins = product3(psum[:, 5, P * k:P * (k + 1)], xT_hi[:, t], xT_lo[:, t], w_qkv_hi[:, 3, :],
                                   w_qkv_lo[:, 3, :])
                ins.then_inc(m_v, 1)

            turn_x(0)
            project(0)
            turn_x(1)
            pe.wait_ge(in_w_ctx, 32)
            pe.wait_ge(have_ctxT, 1)
            pe.matmul(psum[:, 6, SEQ:2 * SEQ], w_ctx[:, 2, :], ctxT[:, :, 0, :], start=True,
                      stop=True).then_inc(m_ck, 1)
            pe.wait_ge(have_bias_cols, 1)
            for b in range(BATCH):
                ins = pe.matmul(psum[:, 7, C * b:C * (b + 1)], ctxT[:, b, :, :], w_ctx[:, 1, :], start=True, stop=True)
            ins.then_inc(m_cv, 1)
            project(1)

            def natural(i):
                b, g = divmod(i, GROUPS)
                KR = SHIFT_ROW
                if i:
                    pe.wait_ge(max_done, 3 * i)
                else:
                    pe.wait_ge(xT_split, 2)
                    pe.wait_ge(qkc_split, 6)
                    pe.wait_ge(have_value, 2)
                    pe.wait_ge(have_cvalue, 2)
                    pe.wait_ge(ck_split, 1)
                    pe.wait_ge(have_causal, 1)
                    pe.wait_ge(have_ident_bf, 1)
                if g == 0:
                    pe.wait_ge(placed_k[b % 2], 64 * (b // 2 + 1))
                    pe.wait_ge(placed_q[b % 2], 32 * (b // 2 + 1))
                    if b == 0:
                        pe.wait_ge(placed_ck, 64)
                keys = key_blocks[0:KR, b % 2, g, :, :]

                def masked(to, q, k):
                    diagonal = q == k
                    if diagonal:
                        pe.matmul(to, ident_bf[:, :], causal[:, :, :], start=True, stop=False, skip_group_check=True)
                    return pe.matmul(to, query_rows[0:KR, b % 2, g, 0, P * q:P * (q + 1)], keys[:, :, P * k:P * (k + 1)],
                                     start=not diagonal, stop=True, skip_group_check=True)

                masked(bank(B_NAT0), 0, 0).then_inc(m_nat, 1)
                for t in range(2):
                    ins = pe.matmul(psum[:, B_NATC, SEQ * t:SEQ * (t + 1)], query_rows[0:KR, b % 2, g, 1, P * t:P * (t + 1)],
                                    ckey_blocks[0:KR, g, b, :, :], start=True, stop=True)
                ins.then_inc(m_nat, 1)
                masked(bank(B_NAT1), 1, 0)
                masked(bank(B_NAT1 + 1), 1, 1).then_inc(m_nat, 1)

            def turn_max(i):
                if i == 0:
                    pe.wait_ge(max_zeroed, 1)
                pe.wait_ge(max_done, 3 * i + 3)
                take_misc(shift_placed, i + 1)
                for n in range(4):
                    ins = pe.transpose(psum[:, B_MISC, P * n:P * (n + 1)], row_max[:, i % 2, n, :], ident[:, :])
                ins.then_inc(t_max, 1)

            def scores(i, c):
                b, g = divmod(i, GROUPS)
                if c == 0:
                    pe.wait_ge(shift_placed, i + 1)
                if i or c >= 2:
                    pe.wait_ge(exp_done, 4 * i + c - 1)
                to = B_ST + c % 2
                if c < 2:
                    for j in range(2):
                        ins = pe.matmul(psum[:, to, SEQ * j:SEQ * (j + 1)], key_blocks[:, b % 2, g, 2 * c + j, 0:P],
                                        query_rows[:, b % 2, g, 0, :], start=True, stop=True)
                if c == 2:
                    for j in range(GROUP):
                        ins = pe.matmul(psum[:, to, P * j:P * (j + 1)], key_blocks[:, b % 2, g, j, P:SEQ],
                                        query_rows[:, b % 2, g, 0, P:SEQ], start=True, stop=True)
                if c == 3:
                    for j in range(2):
                        ins = pe.matmul(psum[:, to, SEQ * j:SEQ * (j + 1)],
                                        ckey_blocks[:, g, b, 2 * j:2 * j + 2, :].rearrange("p j k -> p (j k)"),
                                        query_rows[:, b % 2, g, 1, :], start=True, stop=True)
                ins.then_inc(m_st, 1)

            def attend_self(i):
                b, g = divmod(i, GROUPS)
                if i:
                    pe.wait_ge(o_copied, i)
                else:
                    pe.wait_ge(out_zeroed, 1)
                pe.wait_ge(selected, 2 * i + 1)
                for j in range(GROUP):
                    pe.matmul(psum[32 * j:32 * j + D + 1, B_OUT, 0:SEQ], value[:, 2 * b, GROUP * g + j, :],
                              probs[:, j // 2, SEQ * (j % 2):SEQ * (j % 2 + 1)], start=True, stop=False,
                              skip_group_check=True)
                pe.wait_ge(selected, 2 * i + 2)
                for j in range(GROUP):
                    pe.matmul(psum[32 * j:32 * j + D + 1, B_OUT, P:SEQ], value[:, 2 * b + 1, GROUP * g + j, :],
                              probs[:, 2, P * j:P * (j + 1)], start=False, stop=True, skip_group_check=True)

            def attend_context(i):
                b, g = divmod(i, GROUPS)
                pe.wait_ge(exp_done, 4 * i + 4)
                for j in range(2):
                    ins = pe.matmul(psum[64 * j:64 * j + 32 + D + 1, B_OUT, SEQ:2 * SEQ],
                                    cvalue[:, b, 2 * g + j, :], probs[:, 3, SEQ * j:SEQ * (j + 1)],
                                    start=False, stop=True, skip_group_check=True)
                ins.then_inc(m_out, 1)

            def turn_out(i):
                pe.wait_ge(o_copied, i + 1)
                take_misc(normalized, i + 1)
                for n in range(4):
                    ins = pe.transpose(psum[:, B_MISC, P * n:P * (n + 1)], o_sb[:, i % 2, P * n:P * (n + 1)],
                                       ident[:, :])
                ins.then_inc(t_out, 1)

            def tail(name, b):
                take_misc({"y_turn": yT_split, "project": x1_ready, "x2_turn": x2T_split, "router": logits_ready,
                           "route_turn": routeT_ready}[name], b + 1)
                if name == "y_turn":
                    pe.wait_ge(y_added, 4 * b + 4)
                    for t in range(2):
                        ins = pe.transpose(psum[:, B_MISC, P * t:P * (t + 1)], y_nat[:, b % 2, t, :], ident[:, :])
                    ins.then_inc(t_y, 1)
                if name == "project":
                    pe.wait_ge(yT_split, b + 1)
                    for t in range(2):
                        mine = slice(P * t, P * (t + 1))
                        ins = product3(psum[:, B_MISC, mine], yT_hi[:, mine], yT_lo[:, mine], w_qkv_hi[:, 4, :],
                                       w_qkv_lo[:, 4, :])
                    ins.then_inc(m_proj, 1)
                if name == "x2_turn":
                    pe.wait_ge(x2_normed, 2 * b + 2)
                    for t in range(2):
                        ins = pe.transpose(psum[:, B_MISC, P * t:P * (t + 1)], x2_norm[:, t, :], ident[:, :])
                    ins.then_inc(t_x2, 1)
                if name == "router":
                    pe.wait_ge(x2T_split, b + 1)
                    pe.wait_ge(w_r_split, 1)
                    for t in range(2):
                        ins = product3(psum[:, B_MISC, EXPERTS * t:EXPERTS * (t + 1)], xT_hi[:, tokens(b, t)],
                                       xT_lo[:, tokens(b, t)], w_r_hi[:, :], w_r_lo[:, :])
                    ins.then_inc(m_router, 1)
                if name == "route_turn":
                    pe.wait_ge(route_ready, b + 1)
                    for t in range(2):
                        ins = pe.transpose(psum[:, B_MISC, P * t:P * (t + 1)], route[:, b % 2, t, :], ident[:, :])
                    ins.then_inc(t_route, 1)

            natural(0)
            turn_max(0)
            for i in range(STEPS):
                scores(i, 0)
                scores(i, 1)
                if i:
                    turn_out(i - 1)
                if i + 1 < STEPS:
                    natural(i + 1)
                scores(i, 2)
                scores(i, 3)
                for name, b in tail_at.get(i, ()):
                    tail(name, b)
                attend_self(i)
                if i + 1 < STEPS:
                    turn_max(i + 1)
                attend_context(i)
            turn_out(STEPS - 1)
            for name, b in LAST_TAILS:
                tail(name, b)

            pe.wait_ge(b_down_split, 1)
            for n in range(ITEMS + 2):
                if n < ITEMS:
                    u, c = WORK[n]
                    k = u % SLOTS
                    cols = slice(c * CHUNK, (c + 1) * CHUNK)
                    if u == 0:
                        pe.wait_ge(routeT_ready, 2 * c + 2)
                    pe.wait_ge(ffn_lo, u + 1)
                    if n >= 2:
                        pe.wait_ge(gate_done, n - 1)
                    product3(bank(B_GATE + n % 2), w_ffn_hi[:, k, 0, :], w_ffn_lo[:, k, 0, :], xT_hi[:, cols],
                             xT_lo[:, cols]).then_inc(m_gate, 1)
                    if n >= 2:
                        pe.wait_ge(gated_done, n - 1)
                    product3(bank(B_UP + n % 2), w_ffn_hi[:, k, 1, :], w_ffn_lo[:, k, 1, :], xT_hi[:, cols],
                             xT_lo[:, cols]).then_inc(m_up, 1)
                    if n >= 2:
                        pe.wait_ge(hid_done, n - 1)
                    pe.matmul(bank(B_WIDE + n % 2), spread[:, u, :], routeT[:, cols], start=True,
                              stop=True).then_inc(m_wide, 1)
                if n >= 2:
                    m = n - 2
                    u, c = WORK[m]
                    k = u % SLOTS
                    cols = slice(c * CHUNK, (c + 1) * CHUNK)
                    y = bank(6 + c)
                    if u == 0:
                        pe.matmul(y, b_down_hi[:, :], routeT[:, cols], start=True, stop=False, skip_group_check=True)
                        pe.matmul(y, b_down_lo[:, :], routeT[:, cols], start=False, stop=False, skip_group_check=True)
                    pe.wait_ge(hid_lo_done, m + 1)
                    product3(y, w_ffn_hi[:, k, 2, :], w_ffn_lo[:, k, 2, :], hid_hi[:, m % 3, :], hid_lo[:, m % 3, :],
                             start=False, stop=u == UNITS - 1).then_inc(m_down, 1)
                if n == CHUNK_DONE[0] + 6:
                    turn_ffn(pe, 0)
            turn_ffn(pe, 1)


NAMES = {
    "L0_xattn_": ("Wk", "bk", "Wq", "bq", "Wv", "bv", "Wck", "bck", "Wcq", "bcq", "Wcv", "bcv", "Wp", "bp"),
    "L0_ffn_": ("Wr", "br", "Wg_s", "bg_s", "Wu_s", "bu_s", "Wd_s", "bd_s", "Wg", "bg", "Wu", "bu", "Wd", "bd"),
}


def kernel(**inputs):
    import concourse.bacc as bacc
    import numpy as np
    from concourse.bass_utils import run_bass_kernel_spmd

    nc = bacc.Bacc("TRN2", target_bir_lowering=False, num_devices=1)
    arrays = {}

    def declare(name):
        a = np.ascontiguousarray(inputs[name])
        arrays[f"in_{name}"] = a
        return nc.dram_tensor(f"in_{name}", a.shape, mybir.dt.from_np(a.dtype), kind="ExternalInput").ap()

    x = declare("x")
    ctx = declare("ctx_512")
    w = {short: declare(prefix + short) for prefix, shorts in NAMES.items() for short in shorts}
    out = nc.dram_tensor("out_x", (BATCH, SEQ, C), F32, kind="ExternalOutput").ap()
    build(nc, x, ctx, w, out)
    r = run_bass_kernel_spmd(nc, [arrays], core_ids=[0])
    return r.results[0]["out_x"]
```

```python
from contextlib import ExitStack

import concourse.bass as bass
from concourse import mybir

F32 = mybir.dt.float32
F32R = mybir.dt.float32r
BF16 = mybir.dt.bfloat16
ACT = mybir.ActivationFunctionType
ALU = mybir.AluOpType
AX = mybir.AxisListType

P = 128
BATCH, SEQ, C = 4, 256, 128
CTX, CTX_C = 64, 64
HEADS, D = 16, 8
GROUP = 4
GROUPS = HEADS // GROUP
STEPS = BATCH * GROUPS
TOKENS = BATCH * SEQ
CTX_KEYS = BATCH * CTX
TILES = TOKENS // P
CHUNK = 512
CHUNKS = TOKENS // CHUNK
PARTS = 3
QUERY_PARTS, KEY_PARTS = (0, 1, 0), (0, 0, 1)
WRITES = ((0, 1), (1, 2), (2, 4))
NORM_GROUPS = ((0, 2), (2, 4), (4, 8))
SHIFT_ROW = PARTS * GROUP * D
PART = GROUP * D
EXPERTS, TOP, INNER = 32, 8, 64
SPREADS = 5
SPREAD_UNITS = 4
PAIRS = EXPERTS // 2
UNITS = PAIRS + 1
SCALE = float(1.0 / D ** 0.5)
LN_EPS = 1e-5
MASKED = -1e30

BIAS_GATE, BIAS_UP = 0, UNITS
BIAS_Q, BIAS_K, BIAS_CQ, BIAS_CK = range(2 * UNITS, 2 * UNITS + 4)
BIAS_ROWS = 2 * UNITS + 4
ORDER = ((1, BIAS_K), (0, BIAS_Q), (2, BIAS_CQ))

LEAD = 6
LAST = 4
WORK = ([(u, c) for c in range(CHUNKS) for u in range(LEAD)]
        + [(u, c) for u in range(LEAD, UNITS - LAST) for c in range(CHUNKS)]
        + [(u, c) for c in range(CHUNKS) for u in range(UNITS - LAST, UNITS)])
ITEMS = len(WORK)
SLOTS = 6
ROUND_STEP = STEPS - SLOTS
LAST_USE = {u: max(n for n, e in enumerate(WORK) if e[0] == u) for u in range(UNITS)}
FIRST_USE = {u: min(n for n, e in enumerate(WORK) if e[0] == u) for u in range(UNITS)}
SPLIT_AT = {LAST_USE[u - SLOTS] + 4: u for u in range(SLOTS, UNITS)}
CHUNK_DONE = [max(n for n, e in enumerate(WORK) if e[1] == c) for c in range(CHUNKS)]
assert all(n < FIRST_USE[u] for n, u in SPLIT_AT.items()) and len(SPLIT_AT) == UNITS - SLOTS

B_NAT0, B_NATC, B_NAT1, B_ST, B_OUT, B_MISC = 0, 1, 2, 4, 6, 7
B_GATE, B_UP, B_WIDE = 0, 2, 4
B_QKC, B_VALUE, B_CV, B_CK = 4, 7, 2, 3


def build(nc, x, ctx, w, out):
    with ExitStack() as stack:
        def sb(name, shape, dt=F32, until=None):
            return (until or stack).enter_context(nc.sbuf_tensor(name, shape, dt))

        def sem(name):
            return stack.enter_context(nc.semaphore(name))

        key_dram = nc.dram_tensor("key_dram", (GROUP, PARTS * D, GROUPS, TOKENS), F32, kind="Internal").ap()
        ckey_dram = nc.dram_tensor("ckey_dram", (GROUP, PARTS * D, GROUPS, CTX_KEYS), F32, kind="Internal").ap()
        query_dram = nc.dram_tensor("query_dram", (GROUP, PARTS * D, GROUPS, 2, TOKENS), F32, kind="Internal").ap()
        psum = stack.enter_context(nc.psum_tensor("psum", [P, 8, CHUNK], F32))

        ident = sb("ident", [P, P])
        ident_bf = sb("ident_bf", [P, P], BF16)
        causal = sb("causal", [P, GROUP, P], BF16)
        key_const = sb("key_const", [P, GROUP, CTX])
        minus_half = sb("minus_half", [P, TILES])
        spread = sb("spread", [P, UNITS, P], F32R)
        x_sb = sb("x_sb", [P, TILES, C])
        ctx_sb = sb("ctx_sb", [P, 2, CTX_C])
        w_qkv = sb("w_qkv", [P, 5, C])
        w_qkv_hi = sb("w_qkv_hi", [P, 5, C], F32R)
        w_qkv_lo = sb("w_qkv_lo", [P, 5, C], F32R)
        w_ctx = sb("w_ctx", [CTX_C, 3, C])
        w_r = sb("w_r", [P, EXPERTS])
        w_r_hi = sb("w_r_hi", [P, EXPERTS], F32R)
        w_r_lo = sb("w_r_lo", [P, EXPERTS], F32R)
        bias_rows = sb("bias_rows", [2 * UNITS, P])
        qkc_bias = sb("qkc_bias", [4, 2, C])
        bias_cols = sb("bias_cols", [P, BIAS_ROWS])
        b_wide = sb("b_wide", [P, 3, C])
        b_r = sb("b_r", [P, EXPERTS])
        b_down = sb("b_down", [P, C])
        b_down_hi = sb("b_down_hi", [P, C], F32R)
        b_down_lo = sb("b_down_lo", [P, C], F32R)
        w_ffn = sb("w_ffn", [P, SLOTS, 3, P])
        w_ffn_hi = sb("w_ffn_hi", [P, SLOTS, 3, P], F32R)
        w_ffn_lo = sb("w_ffn_lo", [P, SLOTS, 3, P], F32R)
        stats = sb("stats", [P, TILES, 6])
        moments = sb("moments", [P, TILES, 2])
        var_eps = sb("var_eps", [P, TILES])
        rstd = sb("rstd", [P, TILES])
        x1 = sb("x1", [P, TILES, C])
        xT_hi = sb("xT_hi", [P, TOKENS], F32R)
        xT_lo = sb("xT_lo", [P, TOKENS], F32R)
        ctxT = sb("ctxT", [CTX_C, BATCH, 2, CTX])
        value = sb("value", [P, TILES, HEADS, D + 1])
        cvalue = sb("cvalue", [P, BATCH, HEADS // 2, 32 + D + 1])
        row_max = sb("row_max", [P, 2, 4, P - SHIFT_ROW])
        probs_even = sb("probs_even", [P, 4, CHUNK])
        o_sb = sb("o_sb", [P, 2, CHUNK])
        r_den = sb("r_den", [P, 16])
        o_norm = sb("o_norm", [P, 2, 4 * PART])
        y_nat = sb("y_nat", [P, 2, 2, C])
        yT_hi = sb("yT_hi", [P, SEQ], F32R)
        yT_lo = sb("yT_lo", [P, SEQ], F32R)
        x2_norm = sb("x2_norm", [P, 2, C])
        logits = sb("logits", [P, 2, EXPERTS])
        exp_neg = sb("exp_neg", [P, 2, EXPERTS])
        affinity = sb("affinity", [P, 2, EXPERTS])
        top = sb("top", [P, 2, TOP])
        not_top = sb("not_top", [P, 2, EXPERTS])
        top_sum = sb("top_sum", [P, 2])
        r_top = sb("r_top", [P, 2])
        route = sb("route", [P, 2, 2, P])
        routeT = sb("routeT", [P, TOKENS], F32R)

        with ExitStack() as attention:
            queries = sb("queries", [P, 2, 2, TOKENS], F32R, until=attention)
            ckeys = sb("ckeys", [P, 2, CTX_KEYS], F32R, until=attention)
            query_rows = sb("query_rows", [P, 2, GROUPS, 2, SEQ], F32R, until=attention)
            key_blocks = sb("key_blocks", [P, 2, GROUPS, GROUP, SEQ], F32R, until=attention)
            ckey_blocks = sb("ckey_blocks", [P, GROUPS, BATCH, GROUP, CTX], F32R, until=attention)
            spread_f = sb("spread_f", [P, SPREAD_UNITS, P], until=attention)
            keys = sb("keys", [P, 2, TOKENS], F32R, until=attention)
        probs = [probs_even[:, :, :],
                 keys[:, :, :].rearrange("p h (c n) -> p (h c) n", n=CHUNK).bitcast(F32)]
        gate = sb("gate", [P, 3, CHUNK])
        gated = sb("gated", [P, 3, CHUNK])
        hid = sb("hid", [P, 3, CHUNK])
        hid_hi = sb("hid_hi", [P, 3, CHUNK], F32R)
        hid_lo = sb("hid_lo", [P, 3, CHUNK], F32R)
        ffnT = sb("ffnT", [P, CHUNK])
        result = sb("result", [P, TILES, C])

        in_x = [sem(f"in_x{k}") for k in range(len(NORM_GROUPS))]
        in_small = sem("in_small")
        in_q_bias = sem("in_q_bias")
        in_k_bias = sem("in_k_bias")
        in_ctx = sem("in_ctx")
        in_w_ck = sem("in_w_ck")
        in_w_cv = sem("in_w_cv")
        in_w_kq = sem("in_w_kq")
        in_w_cqv = sem("in_w_cqv")
        in_w_p = sem("in_w_p")
        in_wide = sem("in_wide")
        in_bp = sem("in_bp")
        in_router = sem("in_router")
        in_down_bias = sem("in_down_bias")
        in_ffn = [sem(f"in_ffn{k}") for k in range(SLOTS)]
        placed_q = [sem(f"placed_q{k}") for k in range(2)]
        wrote_k = [sem(f"wrote_k{n}") for n in range(len(WRITES))]
        wrote_ck = sem("wrote_ck")
        wrote_q = [sem(f"wrote_q{n}") for n in range(len(WRITES))]
        placed_k = [sem(f"placed_k{s}") for s in range(2)]
        placed_ck = sem("placed_ck")
        stored = sem("stored")
        zeroed = sem("zeroed")
        slot_zeroed = sem("slot_zeroed")
        have_ident = sem("have_ident")
        have_causal = sem("have_causal")
        have_key_const = sem("have_key_const")
        have_spread = sem("have_spread")
        g_chain = sem("g_chain")
        have_rstd = sem("have_rstd")
        have_x_bp = sem("have_x_bp")
        late_x_normed = sem("late_x_normed")
        selected = sem("selected")
        y_added = sem("y_added")
        ffn_lo = sem("ffn_lo")
        pool_lo_done = sem("pool_lo_done")
        v_chain = sem("v_chain")
        var_ready = sem("var_ready")
        x_normed = sem("x_normed")
        have_ident_bf = sem("have_ident_bf")
        max_zeroed = sem("max_zeroed")
        w_qkv_split = sem("w_qkv_split")
        qkc_bias_stacked = sem("qkc_bias_stacked")
        have_bias_cols = sem("have_bias_cols")
        have_ffn_bias = sem("have_ffn_bias")
        have_ctxT = sem("have_ctxT")
        have_w_ck = sem("have_w_ck")
        ck_split = sem("ck_split")
        xT_split = sem("xT_split")
        qkc_split = sem("qkc_split")
        have_value = sem("have_value")
        have_cvalue = sem("have_cvalue")
        key_blocks_set = sem("key_blocks_set")
        key_blocks1_set = sem("key_blocks1_set")
        ckey_blocks_set = sem("ckey_blocks_set")
        out_zeroed = sem("out_zeroed")
        max_done = sem("max_done")
        normalized = sem("normalized")
        yT_split = sem("yT_split")
        x1_ready = sem("x1_ready")
        var2_ready = sem("var2_ready")
        x2_normed = sem("x2_normed")
        x2T_split = sem("x2T_split")
        w_r_split = sem("w_r_split")
        b_down_split = sem("b_down_split")
        logits_ready = sem("logits_ready")
        route_ready = sem("route_ready")
        gated_done = sem("gated_done")
        hid_done = sem("hid_done")
        hid_lo_done = sem("hid_lo_done")
        result_ready = sem("result_ready")
        have_ctxT2 = sem("have_ctxT2")
        w_qkv_rounded = sem("w_qkv_rounded")
        ck_rounded = sem("ck_rounded")
        xT_rounded = sem("xT_rounded")
        qkc_rounded = sem("qkc_rounded")
        w_r_rounded = sem("w_r_rounded")
        b_down_rounded = sem("b_down_rounded")
        spread_copied = sem("spread_copied")
        ffn_rounded = sem("ffn_rounded")
        shift_placed = sem("shift_placed")
        exp_done = sem("exp_done")
        o_copied = sem("o_copied")
        yT_rounded = sem("yT_rounded")
        x2T_rounded = sem("x2T_rounded")
        exp_neg_ready = sem("exp_neg_ready")
        routeT_ready = sem("routeT_ready")
        gate_done = sem("gate_done")
        hid_rounded = sem("hid_rounded")
        ffnT_copied = sem("ffnT_copied")
        t_bias = sem("t_bias")
        t_ffn_bias = sem("t_ffn_bias")
        t_ctx = sem("t_ctx")
        m_ck = sem("m_ck")
        m_cv = sem("m_cv")
        t_x = sem("t_x")
        m_qkc = sem("m_qkc")
        m_v = sem("m_v")
        m_nat = sem("m_nat")
        t_max = sem("t_max")
        m_st = sem("m_st")
        m_out = sem("m_out")
        t_out = sem("t_out")
        t_y = sem("t_y")
        m_proj = sem("m_proj")
        t_x2 = sem("t_x2")
        m_router = sem("m_router")
        t_route = sem("t_route")
        m_gate = sem("m_gate")
        m_up = sem("m_up")
        m_wide = sem("m_wide")
        m_down = sem("m_down")
        t_ffn = sem("t_ffn")

        x_t = x.rearrange("a s c -> (a s) c").rearrange("(t p) c -> p t c", p=P)
        out_t = out.rearrange("a s c -> (a s) c").rearrange("(t p) c -> p t c", p=P)

        def row(v):
            return v.rearrange("(o n) -> o n", o=1)

        def bank(n, cols=CHUNK):
            return psum[:, n, 0:cols]

        def grouped(v):
            return v.rearrange("p (g j d) -> p j d g", j=GROUP, d=D)

        def stacked(v):
            return v.rearrange("p (j d g) -> p j d g", j=GROUP, d=D)

        def tokens(b, tile=None):
            lo = b * SEQ + (tile or 0) * P
            return slice(lo, lo + (SEQ if tile is None else P))

        TAIL = ("y_turn", "project", "x2_turn", "router")
        tail_at = {2: [("ffn_bias", 0)]}
        late_at = {}
        between_at = {}
        for b in range(BATCH - 1):
            for n, name in enumerate(TAIL):
                tail_at.setdefault(4 * b + 6 + n, []).append((name, b))
            between_at[4 * b + 8] = [("norm", b)]
            between_at[4 * b + 10] = [("weights", b)]
            late_at[4 * b + 10] = [("route_turn", b)]
        beside = {(0, "A"): ("attend", STEPS - 1), (0, "B"): ("turn_out", STEPS - 2), (0, "C"): ("x2_turn", BATCH - 2),
                  (1, "A"): ("turn_out", STEPS - 1), (1, "B"): ("router", BATCH - 2), (2, "A"): ("y_turn", BATCH - 1),
                  (2, "C"): ("project", BATCH - 1), (3, "B"): ("route_turn", BATCH - 2),
                  (4, "A"): ("x2_turn", BATCH - 1), (4, "C"): ("router", BATCH - 1),
                  (6, "A"): ("route_turn", BATCH - 1)}
        v_beside = {(0, "A"): ("norm", BATCH - 2), (1, "C"): ("router", BATCH - 2), (2, "B"): ("weights", BATCH - 2),
                    (2, "C"): ("project", BATCH - 1), (4, "A"): ("norm", BATCH - 1), (4, "C"): ("router", BATCH - 1),
                    (5, "B"): ("weights", BATCH - 1)}
        assert max(beside) <= (LEAD, "A")
        POOL_LO = 8

        def projected(b, n, half):
            if n == 0:
                return keys[:, half, tokens(b)]
            return queries[:, half, n - 1, tokens(b)]

        block = stack.enter_context(nc.Block())

        def write_keys(sp, dram, parts, rounded, split, done):
            sp.wait_ge(*rounded)
            for part, half in enumerate(KEY_PARTS):
                if half:
                    sp.wait_ge(*split)
                sp.dma_start(dram[:, D * part:D * (part + 1), :, :].rearrange("j d g n -> j (d g) n"),
                             parts[:, half, :].bitcast(F32)).then_inc(done, 16)

        def write_token_keys(sp, n):
            first, end = WRITES[n]
            cols = slice(first * SEQ, end * SEQ)
            write_keys(sp, key_dram[:, :, :, cols], keys[:, :, cols], (qkc_rounded, 3 * end - 2),
                       (qkc_split, 3 * end - 2), wrote_k[n])

        def write_queries(sp, n):
            first, end = WRITES[n]
            cols = slice(first * SEQ, end * SEQ)
            sp.wait_ge(qkc_rounded, 3 * end)
            for part in (0, 2, 1):
                half = QUERY_PARTS[part]
                if half:
                    sp.wait_ge(qkc_split, 3 * end)
                sp.dma_start(query_dram[:, D * part:D * (part + 1), :, :, cols].rearrange("j d g s n -> j (d g) s n"),
                             queries[:, half, :, cols].bitcast(F32)).then_inc(wrote_q[n], 16)

        def read_keys(sp, b):
            if b == 0:
                sp.wait_ge(key_blocks_set, 1)
            if b == 1:
                sp.wait_ge(key_blocks1_set, 1)
            if b >= 2:
                sp.wait_ge(m_st, 16 * (b - 1))
            sp.wait_ge(wrote_k[min(b, 2)], 48)
            for j in range(GROUP):
                sp.dma_start(key_blocks[24 * j:24 * (j + 1), b % 2, :, j, :].bitcast(F32),
                             key_dram[j][:, :, tokens(b)]).then_inc(placed_k[b % 2], 16)

        def read_queries(sp, b):
            sp.wait_ge(wrote_q[min(b, 2)], 48)
            sp.dma_start(query_rows[0:SHIFT_ROW, b % 2, :, :, :].rearrange("p g s n -> p (g s) n").bitcast(F32),
                         query_dram.rearrange("j r g s n -> (j r) (g s) n")[:, :, tokens(b)]
                         ).then_inc(placed_q[b % 2], 16)

        def load_unit(sp, u):
            slot = u % SLOTS
            if u >= SLOTS:
                sp.wait_ge(ffn_lo, u - SLOTS + 1)
            if u == PAIRS:
                sp.wait_ge(slot_zeroed, 1)
                sp.dma_start(w_ffn[:, slot, 0, 0:INNER], w["Wg_s"]).then_inc(in_ffn[slot], 16)
                sp.dma_start(w_ffn[:, slot, 1, 0:INNER], w["Wu_s"]).then_inc(in_ffn[slot], 16)
                sp.dma_start(w_ffn[0:INNER, slot, 2, :], w["Wd_s"]).then_inc(in_ffn[slot], 16)
                return
            for n, name in enumerate(("Wg", "Wu")):
                sp.dma_start(w_ffn[:, slot, n, :].rearrange("h (e i) -> h e i", e=2),
                             w[name][2 * u:2 * u + 2].rearrange("e h i -> h e i")).then_inc(in_ffn[slot], 16)
            sp.dma_start(w_ffn[:, slot, 2, :],
                         w["Wd"][2 * u:2 * u + 2].rearrange("e i h -> (e i) h")).then_inc(in_ffn[slot], 16)

        @block.sync
        def _(sp):
            def load_x(k):
                lo, hi = NORM_GROUPS[k]
                sp.dma_start(x_sb[:, lo:hi, :], x_t[:, lo:hi, :]).then_inc(in_x[k], 16)

            load_x(0)
            sp.dma_start(w_qkv[:, 1, :], w["Wk"]).then_inc(in_w_kq, 16)
            load_x(1)
            sp.dma_start(w_qkv[:, 0, :], w["Wq"]).then_inc(in_w_kq, 16)
            for name, r0 in (("bk", BIAS_K), ("bck", BIAS_CK)):
                sp.dma_start(qkc_bias[r0 - BIAS_Q:r0 - BIAS_Q + 1, 0, :], row(w[name])).then_inc(in_k_bias, 16)
            sp.dma_start(w_qkv[:, 2, :], w["Wcq"]).then_inc(in_w_cqv, 16)
            sp.dma_start(w_qkv[:, 3, :], w["Wv"]).then_inc(in_w_cqv, 16)
            load_x(2)
            sp.dma_start(w_ctx[:, 1, :], w["Wcv"]).then_inc(in_w_cv, 16)
            for n, name in enumerate(("bv", "bcv")):
                sp.dma_start(b_wide[:, n, :], row(w[name]).to_broadcast([P, C])).then_inc(in_wide, 16)
            write_keys(sp, ckey_dram, ckeys, (ck_rounded, 1), (ck_split, 1), wrote_ck)
            write_token_keys(sp, 0)
            write_queries(sp, 0)
            read_keys(sp, 0)
            read_queries(sp, 0)
            sp.wait_ge(ckey_blocks_set, 1)
            sp.wait_ge(wrote_ck, 48)
            for j in range(GROUP):
                sp.dma_start(ckey_blocks[24 * j:24 * (j + 1), :, :, j, :].rearrange("r g b k -> r (g b) k").bitcast(F32),
                             ckey_dram[j].rearrange("r g (b k) -> r (g b) k", b=BATCH)).then_inc(placed_ck, 16)
            for n in (1, 2):
                write_token_keys(sp, n)
                write_queries(sp, n)
            read_keys(sp, 1)
            read_queries(sp, 1)
            sp.dma_start(b_wide[:, 2, :], row(w["bp"]).to_broadcast([P, C])).then_inc(in_bp, 16)
            sp.dma_start(w_qkv[:, 4, :], w["Wp"]).then_inc(in_w_p, 16)
            sp.wait_ge(zeroed, 4)
            for name, r0 in (("bg", BIAS_GATE), ("bu", BIAS_UP)):
                sp.dma_start(bias_rows[r0:r0 + PAIRS, :],
                              w[name].rearrange("(p e) i -> p (e i)", e=2)).then_inc(in_small, 16)
            sp.dma_start(bias_rows[PAIRS:PAIRS + 1, 0:INNER], row(w["bg_s"])).then_inc(in_small, 16)
            sp.dma_start(bias_rows[BIAS_UP + PAIRS:BIAS_UP + UNITS, 0:INNER], row(w["bu_s"])).then_inc(in_small, 16)
            sp.dma_start(w_r[:, :], w["Wr"]).then_inc(in_router, 16)
            sp.dma_start(b_r[:, :], row(w["br"]).to_broadcast([P, EXPERTS])).then_inc(in_router, 16)
            sp.wait_ge(zeroed, 5)
            sp.dma_start(b_down[0:EXPERTS, :], w["bd"]).then_inc(in_down_bias, 16)
            sp.dma_start(b_down[EXPERTS:2 * EXPERTS, :], w["bd"]).then_inc(in_down_bias, 16)
            sp.dma_start(b_down[2 * EXPERTS:2 * EXPERTS + 1, :], row(w["bd_s"])).then_inc(in_down_bias, 16)
            for u in range(SLOTS):
                load_unit(sp, u)
            read_keys(sp, 2)
            read_queries(sp, 2)
            read_keys(sp, 3)
            read_queries(sp, 3)
            for u in range(SLOTS, UNITS):
                load_unit(sp, u)
            for c in range(CHUNKS):
                sp.wait_ge(result_ready, c + 1)
                sp.dma_start(out_t[:, 4 * c:4 * c + 4, :], result[:, 4 * c:4 * c + 4, :]).then_inc(stored, 16)
            sp.wait_ge(stored, 16 * CHUNKS)

        @block.gpsimd
        def _(pool):
            chained = [0]

            def chain(ins):
                chained[0] += 1
                ins.then_inc(g_chain, 1)
                pool.wait_ge(g_chain, chained[0])

            chain(pool.memset(key_const[:, :, :], 0.0))
            pool.affine_select(out=key_const[:, :, :], in_=key_const[:, :, :], compare_op=ALU.not_equal,
                               fill=-1.0, base=-SHIFT_ROW, pattern=[[-1, GROUP], [0, CTX]],
                               channel_multiplier=1).then_inc(have_key_const, 1)
            chain(pool.memset(ident[:, :], 0.0))
            pool.affine_select(out=ident[:, :], in_=ident[:, :], compare_op=ALU.not_equal, fill=1.0, base=0,
                               pattern=[[-1, P]], channel_multiplier=1).then_inc(have_ident, 1)
            chain(pool.memset(minus_half[:, :], -0.5))
            for name, r0 in (("bq", BIAS_Q), ("bcq", BIAS_CQ)):
                pool.dma_start(qkc_bias[r0 - BIAS_Q:r0 - BIAS_Q + 1, 0, :], row(w[name])).then_inc(in_q_bias, 16)

            def first_rstd(k):
                lo, hi = NORM_GROUPS[k]
                pool.wait_ge(var_ready, k + 1)
                pool.tensor_tensor(rstd[:, lo:hi], var_eps[:, lo:hi], minus_half[:, 0:hi - lo],
                                   ALU.pow).then_inc(have_rstd, 1)

            first_rstd(0)
            pool.memset(value[:, :, :, :], 1.0).then_inc(zeroed, 1)
            pool.memset(cvalue[:, :, :, :], 0.0).then_inc(g_chain, 1)
            chained[0] += 1
            pool.wait_ge(g_chain, chained[0])
            pool.memset(cvalue[0:CTX, :, :, D:D + 1], 1.0).then_inc(zeroed, 1)
            pool.wait_ge(zeroed, 2)
            pool.memset(cvalue[CTX:P, :, :, 32 + D:32 + D + 1], 1.0).then_inc(zeroed, 1)
            pool.wait_ge(zeroed, 3)
            first_rstd(1)
            first_rstd(2)
            pool.wait_ge(have_rstd, 3)
            for t in range(*NORM_GROUPS[2]):
                pool.tensor_scalar(x1[:, t, :], x_sb[:, t, :], moments[:, t, 0:1], rstd[:, t:t + 1],
                                   ALU.subtract, ALU.mult).then_inc(late_x_normed, 1)
            chain(pool.memset(causal[:, :, :], 0.0))
            pool.affine_select(out=causal[:, :, :], in_=causal[:, :, :], compare_op=ALU.is_ge, fill=MASKED, base=0,
                               pattern=[[0, GROUP], [-1, P]], channel_multiplier=1).then_inc(have_causal, 1)
            pool.wait_ge(zeroed, 3)
            pool.memset(bias_rows[:, :], 0.0).then_inc(zeroed, 1)
            pool.memset(b_down[:, :], 0.0).then_inc(zeroed, 1)
            chain(pool.memset(route[:, :, :, :], 0.0))
            pool.memset(route[:, :, :, 2 * EXPERTS:2 * EXPERTS + 1], 1.0).then_inc(zeroed, 1)
            def add_bp(b):
                for t in (2 * b, 2 * b + 1):
                    ins = pool.tensor_tensor(x_sb[:, t, :], x_sb[:, t, :], b_wide[:, 2, :], ALU.add)
                ins.then_inc(have_x_bp, 1)

            def make_spread(k):
                if k:
                    pool.wait_ge(spread_copied, k)
                body = spread_f[:, :, :].rearrange("p u (e i) -> p u e i", e=2)
                chain(pool.memset(spread_f[:, :, :], 0.0))
                if k < PAIRS // SPREAD_UNITS:
                    for half in range(2):
                        ins = pool.affine_select(out=body, in_=body, compare_op=ALU.not_equal, fill=1.0,
                                                 base=-EXPERTS * half - 2 * SPREAD_UNITS * k,
                                                 pattern=[[-2, SPREAD_UNITS], [-1, 2], [0, INNER]],
                                                 channel_multiplier=1)
                        if half == 0:
                            chain(ins)
                else:
                    ins = pool.affine_select(out=spread_f[:, 0, :], in_=spread_f[:, 0, :],
                                             compare_op=ALU.not_equal, fill=1.0, base=-2 * EXPERTS,
                                             pattern=[[0, P]], channel_multiplier=1)
                ins.then_inc(have_spread, 1)

            def split_unit(u):
                k = u % SLOTS
                pool.wait_ge(ffn_rounded, u + 1)
                ins = pool.tensor_tensor(w_ffn_lo[:, k, :, :], w_ffn[:, k, :, :], w_ffn_hi[:, k, :, :].bitcast(F32),
                                         ALU.subtract).then_inc(ffn_lo, 1)
                if u == PAIRS - SLOTS:
                    pool.wait_ge(ffn_lo, u + 1)
                    pool.memset(w_ffn[:, k, :, :], 0.0).then_inc(slot_zeroed, 1)

            def add_y(i):
                b, g = divmod(i, GROUPS)
                pool.wait_ge(normalized, i + 1)
                if g == 0 and b >= 2:
                    pool.wait_ge(t_y, b - 1)
                pool.tensor_tensor(y_nat[:, b % 2, :, PART * g:PART * (g + 1)],
                                   o_norm[:, i % 2, 0:2 * PART].rearrange("p (t c) -> p t c", t=2),
                                   o_norm[:, i % 2, 2 * PART:4 * PART].rearrange("p (t c) -> p t c", t=2),
                                   ALU.add).then_inc(y_added, 1)

            def tail(name, b):
                if name == "project":
                    pool.wait_ge(var2_ready, b + 1)
                    pool.tensor_tensor(rstd[:, 2 * b:2 * b + 2], var_eps[:, 2 * b:2 * b + 2], minus_half[:, 0:2],
                                       ALU.pow).then_inc(have_rstd, 1)

            for i in range(STEPS):
                pool.wait_ge(exp_done, 4 * i + 2)
                for_k0 = probs[i % 2][:, 0:2, :].rearrange("p c (j q) -> p (c j) q", j=2)[:, :, 0:P]
                pool.affine_select(out=for_k0, in_=for_k0, compare_op=ALU.is_ge, fill=0.0, base=0,
                                   pattern=[[0, GROUP], [1, P]], channel_multiplier=-1).then_inc(selected, 1)
                pool.wait_ge(exp_done, 4 * i + 3)
                for_k1 = probs[i % 2][:, 2, :].rearrange("p (j q) -> p j q", j=GROUP)
                pool.affine_select(out=for_k1, in_=for_k1, compare_op=ALU.is_ge, fill=0.0, base=0,
                                   pattern=[[0, GROUP], [1, P]], channel_multiplier=-1).then_inc(selected, 1)
                if i >= 2:
                    add_y(i - 2)
                for name, b in tail_at.get(i, ()):
                    tail(name, b)
                if i < BATCH:
                    if i == 0:
                        pool.wait_ge(in_bp, 16)
                        pool.wait_ge(x_normed, NORM_GROUPS[2][0])
                        pool.wait_ge(late_x_normed, TILES - NORM_GROUPS[2][0])
                    add_bp(i)
                elif i % 2 and i // 2 - 2 < SPREADS:
                    make_spread(i // 2 - 2)
                if ROUND_STEP <= i < ROUND_STEP + SLOTS:
                    split_unit(i - ROUND_STEP)
            add_y(STEPS - 2)
            add_y(STEPS - 1)
            for n in range(POOL_LO):
                if beside.get((n, "C"), ("", 0))[0] == "project":
                    tail("project", BATCH - 1)
                pool.wait_ge(hid_rounded, n + 1)
                if n >= 3:
                    pool.wait_ge(m_down, n - 2)
                pool.tensor_tensor(hid_lo[:, n % 3, :], hid[:, n % 3, :], hid_hi[:, n % 3, :].bitcast(F32),
                                   ALU.subtract).then_inc(pool_lo_done, 1)
            for u in range(SLOTS, UNITS):
                split_unit(u)

        @block.scalar
        def _(act):
            act.dma_start(ctx_sb[:, :, :], ctx.rearrange("(h a) k c -> (a k) h c", a=2)).then_inc(in_ctx, 16)
            act.dma_start(w_ctx[:, 0, :], w["Wck"]).then_inc(in_w_ck, 16)

            def blocks_const(dst):
                return act.copy(dst, key_const[:, :, :].unsqueeze(2).to_broadcast([P, GROUP, SEQ // CTX, CTX]))

            def copy_hi(dst, src, done):
                act.copy(dst, src).then_inc(done, 1)

            def ckey_const(g):
                return act.copy(ckey_blocks[:, g, :, :, :],
                                key_const[:, :, :].unsqueeze(1).to_broadcast([P, BATCH, GROUP, CTX]))

            act.wait_ge(have_key_const, 1)
            ckey_const(0)
            act.wait_ge(t_ctx, 1)
            act.copy(ctxT[:, :, 1, :], psum[0:CTX_C, B_VALUE, 0:CTX_KEYS]
                     .rearrange("p (b k) -> p b k", b=BATCH)).then_inc(have_ctxT2, 1)
            act.wait_ge(in_w_kq, 32)
            for n in (1, 0):
                ins = act.copy(stacked(w_qkv_hi[:, n, :]), grouped(w_qkv[:, n, :]))
            ins.then_inc(w_qkv_rounded, 1)

            def round_x(b):
                act.wait_ge(t_x, b + 1)
                copy_hi(xT_hi[:, tokens(b)], bank(b % 2, SEQ), xT_rounded)

            for b in range(BATCH):
                if b < 2:
                    round_x(b)
                if b == 0:
                    act.wait_ge(in_w_cqv, 32)
                    act.copy(stacked(w_qkv_hi[:, 2, :]), grouped(w_qkv[:, 2, :]))
                    act.copy(w_qkv_hi[:, 3, :], w_qkv[:, 3, :]).then_inc(w_qkv_rounded, 1)
                    act.wait_ge(have_bias_cols, 1)
                    act.wait_ge(m_ck, 1)
                    act.activation(ckeys[:, 0, :], bank(B_CK, CTX_KEYS), ACT.Identity,
                                   bias=bias_cols[:, BIAS_CK:BIAS_CK + 1]).then_inc(ck_rounded, 1)
                for n, (tensor, bias) in enumerate(ORDER):
                    act.wait_ge(m_qkc, 3 * b + n + 1)
                    act.activation(projected(b, n, 0), bank(B_QKC + n, SEQ), ACT.Identity,
                                   bias=bias_cols[:, bias:bias + 1]).then_inc(qkc_rounded, 1)
                if b == 0:
                    for g in range(1, GROUPS):
                        ins = ckey_const(g)
                    ins.then_inc(ckey_blocks_set, 1)
                if b == 1:
                    round_x(2)
                    round_x(3)
            for g in range(GROUPS):
                ins = blocks_const(key_blocks[:, 1, g, :, :].rearrange("p j (r k) -> p j r k", k=CTX))
            ins.then_inc(key_blocks1_set, 1)
            def shift(i):
                b, g = divmod(i, GROUPS)
                act.wait_ge(t_max, i + 1)
                act.copy(query_rows[SHIFT_ROW:P, b % 2, g, :, :],
                         psum[0:P - SHIFT_ROW, B_MISC, :].rearrange("p (s n) -> p s n", s=2)).then_inc(shift_placed, 1)

            def exps(i, parts):
                if i == 1:
                    for done in wrote_k:
                        act.wait_ge(done, 48)
                if i >= 2:
                    act.wait_ge(m_out, i - 1)
                for c in parts:
                    act.wait_ge(m_st, 4 * i + c + 1)
                    act.activation(probs[i % 2][:, c, :], bank(B_ST + c % 2), ACT.Exp,
                                   scale=SCALE).then_inc(exp_done, 1)

            def copy_out(i):
                act.wait_ge(m_out, i + 1)
                if i >= 2:
                    act.wait_ge(t_out, i - 1)
                act.copy(o_sb[:, i % 2, :], bank(B_OUT)).then_inc(o_copied, 1)

            def round_unit(u):
                k = u % SLOTS
                act.wait_ge(in_ffn[k], 48 * (u // SLOTS + 1))
                if u >= SLOTS:
                    act.wait_ge(m_down, LAST_USE[u - SLOTS] + 1)
                act.copy(w_ffn_hi[:, k, :, :], w_ffn[:, k, :, :]).then_inc(ffn_rounded, 1)

            def tail(name, b):
                if name == "y_turn":
                    act.wait_ge(t_y, b + 1)
                    copy_hi(yT_hi[:, :], bank(B_MISC, SEQ), yT_rounded)
                if name == "x2_turn":
                    act.wait_ge(t_x2, b + 1)
                    copy_hi(xT_hi[:, tokens(b)], bank(B_MISC, SEQ), x2T_rounded)
                if name == "route_turn":
                    act.wait_ge(t_route, b + 1)
                    act.copy(routeT[:, tokens(b)], bank(B_MISC, SEQ)).then_inc(routeT_ready, 1)

            def tail_rest(name, b):
                if name == "router":
                    act.wait_ge(logits_ready, b + 1)
                    act.activation(exp_neg[:, :, :], logits[:, :, :], ACT.Exp, scale=-1.0).then_inc(exp_neg_ready, 1)

            shift(0)
            for i in range(STEPS):
                exps(i, (0, 1))
                if i + 1 < STEPS:
                    shift(i + 1)
                if i == 2:
                    act.wait_ge(in_w_p, 16)
                    act.copy(w_qkv_hi[:, 4, :], w_qkv[:, 4, :]).then_inc(w_qkv_rounded, 1)
                    act.wait_ge(in_router, 32)
                    copy_hi(w_r_hi[:, :], w_r[:, :], w_r_rounded)
                    act.wait_ge(in_down_bias, 48)
                    copy_hi(b_down_hi[:, :], b_down[:, :], b_down_rounded)
                if ROUND_STEP <= i < ROUND_STEP + SLOTS:
                    round_unit(i - ROUND_STEP)
                if i % 2 and 0 <= i // 2 - 3 < SPREADS:
                    k = i // 2 - 3
                    act.wait_ge(have_spread, k + 1)
                    n = min(SPREAD_UNITS, UNITS - SPREAD_UNITS * k)
                    act.copy(spread[:, SPREAD_UNITS * k:SPREAD_UNITS * k + n, :],
                             spread_f[:, 0:n, :]).then_inc(spread_copied, 1)
                exps(i, (2, 3))
                for name, b in tail_at.get(i, ()):
                    tail(name, b)
                if i:
                    copy_out(i - 1)
                for name, b in tail_at.get(i, ()):
                    tail_rest(name, b)
                for name, b in late_at.get(i, ()):
                    tail(name, b)

            def left_over(n, slot):
                name, b = beside.get((n, slot), ("", 0))
                if name == "attend":
                    copy_out(b)
                tail(name, b)
                name, b = v_beside.get((n, slot), ("", 0))
                if name == "router":
                    tail_rest(name, b)

            act.wait_ge(have_ffn_bias, 1)
            for done in wrote_q:
                act.wait_ge(done, 48)
            act.wait_ge(wrote_ck, 48)
            for n in range(ITEMS + 1):
                if n < ITEMS:
                    u, _ = WORK[n]
                    act.wait_ge(m_gate, n + 1)
                    if n >= 3:
                        act.wait_ge(gated_done, n - 2)
                    act.activation(gate[:, n % 3, :], bank(B_GATE + n % 2), ACT.Silu,
                                   bias=bias_cols[:, BIAS_GATE + u:BIAS_GATE + u + 1]).then_inc(gate_done, 1)
                left_over(n, "A")
                if n >= 1:
                    act.wait_ge(hid_done, n)
                    if n >= 4:
                        act.wait_ge(m_down, n - 3)
                    act.copy(hid_hi[:, (n - 1) % 3, :], hid[:, (n - 1) % 3, :]).then_inc(hid_rounded, 1)
                left_over(n, "B")
                left_over(n, "C")
                if n in SPLIT_AT:
                    round_unit(SPLIT_AT[n])
                if n == CHUNK_DONE[0] + 4:
                    act.wait_ge(m_down, CHUNK_DONE[0] + 1)
                    act.copy(ffnT[:, :], bank(6)).then_inc(ffnT_copied, 1)
            act.wait_ge(m_down, ITEMS)
            act.wait_ge(t_ffn, 1)
            act.copy(ffnT[:, :], bank(7)).then_inc(ffnT_copied, 1)

        @block.vector
        def _(dve):
            chained = [0]

            def chain(ins):
                chained[0] += 1
                ins.then_inc(v_chain, 1)
                dve.wait_ge(v_chain, chained[0])

            def norm_stats(src, tiles, done):
                for k in range(tiles.start, tiles.stop):
                    ins = dve.bn_stats(stats[:, k, :], src[:, k, :])
                chain(ins)
                for k in range(tiles.start, tiles.stop):
                    ins = dve.bn_aggr(moments[:, k, :], stats[:, k, :])
                chain(ins)
                dve.tensor_scalar(var_eps[:, tiles], moments[:, tiles, 1], LN_EPS, None, ALU.add).then_inc(done, 1)

            def lo_half(dst, src, hi, done):
                return dve.tensor_tensor(dst, src, hi.bitcast(F32), ALU.subtract).then_inc(done, 1)

            def stats_of(k):
                dve.wait_ge(in_x[k], 16)
                norm_stats(x_sb, slice(*NORM_GROUPS[k]), var_ready)

            def norm(k):
                dve.wait_ge(have_rstd, k + 1)
                for t in range(*NORM_GROUPS[k]):
                    dve.tensor_scalar(x1[:, t, :], x_sb[:, t, :], moments[:, t, 0:1], rstd[:, t:t + 1],
                                      ALU.subtract, ALU.mult).then_inc(x_normed, 1)

            def blocks_const(g):
                return dve.tensor_copy(key_blocks[:, 0, g, :, :].rearrange("p j (r k) -> p j r k", k=CTX),
                                       key_const[:, :, :].unsqueeze(2).to_broadcast([P, GROUP, SEQ // CTX, CTX]))

            def lo_weights(n):
                return dve.tensor_tensor(stacked(w_qkv_lo[:, n, :]), grouped(w_qkv[:, n, :]),
                                         stacked(w_qkv_hi[:, n, :]).bitcast(F32), ALU.subtract)

            dve.memset(bank(B_OUT), 0.0).then_inc(out_zeroed, 1)
            dve.wait_ge(have_key_const, 1)
            for g in range(2):
                blocks_const(g)
            stats_of(0)
            dve.wait_ge(have_ctxT2, 1)
            dve.tensor_copy(ctxT[:, :, 0, :],
                            psum[0:CTX_C, B_VALUE, 0:CTX_KEYS].rearrange("p (b k) -> p b k", b=BATCH)
                            ).then_inc(have_ctxT, 1)
            dve.wait_ge(in_w_ck, 16)
            dve.tensor_copy(stacked(w_ctx[:, 2, :]), grouped(w_ctx[:, 0, :])).then_inc(have_w_ck, 1)
            norm(0)
            stats_of(1)
            dve.wait_ge(in_q_bias, 32)
            dve.wait_ge(in_k_bias, 32)
            dve.tensor_copy(stacked(qkc_bias[:, 1, :]), grouped(qkc_bias[:, 0, :])).then_inc(qkc_bias_stacked, 1)
            dve.wait_ge(w_qkv_rounded, 1)
            lo_weights(1)
            lo_weights(0).then_inc(w_qkv_split, 1)

            def value_add(dst, src, which, done):
                dve.tensor_tensor(dst, src, which, ALU.add).then_inc(done, 1)

            def split_x(b):
                dve.wait_ge(xT_rounded, b + 1)
                lo_half(xT_lo[:, tokens(b)], bank(b % 2, SEQ), xT_hi[:, tokens(b)], xT_split)

            def split_qkc(b, n):
                bias = ORDER[n][1]
                dve.wait_ge(qkc_rounded, 3 * b + n + 1)
                dve.scalar_tensor_tensor(out=projected(b, n, 1), in0=bank(B_QKC + n, SEQ),
                                         scalar=bias_cols[:, bias:bias + 1],
                                         in1=projected(b, n, 0).bitcast(F32),
                                         op0=ALU.add, op1=ALU.subtract).then_inc(qkc_split, 1)

            def values(b):
                dve.wait_ge(m_v, b + 1)
                if b == 0:
                    dve.wait_ge(in_wide, 32)
                    dve.wait_ge(zeroed, 1)
                value_add(value[:, 2 * b:2 * b + 2, :, 0:D],
                          bank(B_VALUE, SEQ).rearrange("p (t h d) -> p t h d", t=2, h=HEADS),
                          b_wide[:, 0, :].rearrange("p (h d) -> p h d", h=HEADS).unsqueeze(1)
                          .to_broadcast([P, 2, HEADS, D]), have_value)

            split_x(0)
            dve.wait_ge(t_bias, 1)
            dve.tensor_copy(bias_cols[:, BIAS_Q:BIAS_ROWS],
                            bank(B_CV, 4)).then_inc(have_bias_cols, 1)
            dve.wait_ge(ck_rounded, 1)
            dve.scalar_tensor_tensor(out=ckeys[:, 1, :], in0=bank(B_CK, CTX_KEYS),
                                     scalar=bias_cols[:, BIAS_CK:BIAS_CK + 1], in1=ckeys[:, 0, :].bitcast(F32),
                                     op0=ALU.add, op1=ALU.subtract).then_inc(ck_split, 1)
            dve.wait_ge(w_qkv_rounded, 2)
            lo_weights(2)
            lo_half(w_qkv_lo[:, 3, :], w_qkv[:, 3, :], w_qkv_hi[:, 3, :], w_qkv_split)
            stats_of(2)
            norm(1)
            split_qkc(0, 0)
            split_qkc(0, 1)
            split_qkc(0, 2)
            blocks_const(2)
            blocks_const(3).then_inc(key_blocks_set, 1)
            split_x(1)
            values(0)
            dve.tensor_copy(ident_bf[:, :], ident[:, :]).then_inc(have_ident_bf, 1)
            dve.memset(row_max[:, :, :, :], 0.0).then_inc(max_zeroed, 1)
            for n in range(3):
                split_qkc(1, n)
            split_x(2)
            split_x(3)
            values(1)
            dve.wait_ge(m_cv, 1)
            dve.wait_ge(zeroed, 3)
            for h in range(2):
                rows = slice(CTX * h, CTX * (h + 1))
                src = psum[rows, B_CV, :].rearrange("p (b q e d) -> p b q e d", b=BATCH, e=2, d=D)[:, :, :, h, :]
                wide = b_wide[rows, 1, :].rearrange("p (q e d) -> p q e d", e=2, d=D)[:, :, h, :]
                value_add(cvalue[rows, :, :, 32 * h:32 * h + D], src,
                          wide.unsqueeze(1).to_broadcast([CTX, BATCH, HEADS // 2, D]), have_cvalue)

            def maxima(i, outputs=-1):
                to = row_max[:, i % 2, :, :]
                if i >= 2:
                    dve.wait_ge(t_max, i - 1)
                dve.wait_ge(m_nat, 3 * i + 1)
                dve.tensor_reduce(to[:, 0, 0:GROUP], bank(B_NAT0).rearrange("p (j k) -> p j k", j=GROUP),
                                  AX.X, ALU.max).then_inc(max_done, 1)
                dve.wait_ge(m_nat, 3 * i + 2)
                dve.tensor_reduce(to[:, 2:4, 0:GROUP],
                                  bank(B_NATC).rearrange("p (t j k) -> p t j k", t=2, j=GROUP),
                                  AX.X, ALU.max).then_inc(max_done, 1)
                if outputs >= 0:
                    normalize(outputs)
                for name, b in between_at.get(i - 2, ()):
                    long_part(name, b)
                dve.wait_ge(m_nat, 3 * i + 3)
                dve.tensor_reduce(to[:, 1, 0:GROUP],
                                  psum[:, B_NAT1:B_NAT1 + 2, :].rearrange("p k (j c) -> p j k c", j=GROUP),
                                  AX.XY, ALU.max).then_inc(max_done, 1)

            def normalize(i):
                turned = bank(B_MISC).rearrange("p (j d) -> p j d", d=32)
                dve.wait_ge(t_out, i + 1)
                chain(dve.reciprocal(r_den[:, :].unsqueeze(2), turned[:, :, D:D + 1]))
                if i >= 2:
                    dve.wait_ge(y_added, i - 1)
                dve.tensor_tensor(o_norm[:, i % 2, :].rearrange("p (j d) -> p j d", d=D), turned[:, :, 0:D],
                                  r_den[:, :].unsqueeze(2).to_broadcast([P, 16, D]), ALU.mult)\
                   .then_inc(normalized, 1)

            def tail(name, b):
                mine = slice(2 * b, 2 * b + 2)
                if name == "ffn_bias":
                    dve.wait_ge(t_ffn_bias, 1)
                    dve.tensor_copy(bias_cols[:, 0:2 * UNITS], bank(B_MISC, 2 * UNITS)).then_inc(have_ffn_bias, 1)
                if name == "y_turn":
                    dve.wait_ge(yT_rounded, b + 1)
                    lo_half(yT_lo[:, :], bank(B_MISC, SEQ), yT_hi[:, :], yT_split)
                if name == "project":
                    dve.wait_ge(m_proj, b + 1)
                    dve.wait_ge(have_x_bp, b + 1)
                    dve.tensor_tensor(x1[:, mine, :], bank(B_MISC, SEQ).rearrange("p (t c) -> p t c", t=2),
                                      x_sb[:, mine, :], ALU.add).then_inc(x1_ready, 1)
                if name == "x2_turn":
                    dve.wait_ge(x2T_rounded, b + 1)
                    lo_half(xT_lo[:, tokens(b)], bank(B_MISC, SEQ), xT_hi[:, tokens(b)],
                            x2T_split)
                if name == "router":
                    dve.wait_ge(m_router, b + 1)
                    dve.tensor_tensor(logits[:, :, :], bank(B_MISC, 2 * EXPERTS).rearrange("p (t e) -> p t e", t=2),
                                      b_r[:, :].unsqueeze(1).to_broadcast([P, 2, EXPERTS]),
                                      ALU.add).then_inc(logits_ready, 1)

            def tail_rest(name, b):
                mine = slice(2 * b, 2 * b + 2)
                if name == "project":
                    dve.wait_ge(x1_ready, b + 1)
                    norm_stats(x1, mine, var2_ready)

                if name == "router":
                    dve.wait_ge(exp_neg_ready, b + 1)
                    chain(dve.tensor_scalar(exp_neg[:, :, :], exp_neg[:, :, :], 1.0, None, ALU.add))
                    chain(dve.reciprocal(affinity[:, :, :], exp_neg[:, :, :]))
                    for t in range(2):
                        ins = dve.max(top[:, t, :], affinity[:, t, :])
                    chain(ins)
                    for t in range(2):
                        dve.match_replace(not_top[:, t, :], top[:, t, :], affinity[:, t, :], -1.0)
            def long_part(name, b):
                mine = slice(2 * b, 2 * b + 2)
                if name == "norm":
                    dve.wait_ge(have_rstd, len(NORM_GROUPS) + b + 1)
                    for t in range(2):
                        k = 2 * b + t
                        dve.tensor_scalar(x2_norm[:, t, :], x1[:, k, :], moments[:, k, 0:1], rstd[:, k:k + 1],
                                          ALU.subtract, ALU.mult).then_inc(x2_normed, 1)
                if name == "weights":
                    chain(dve.tensor_reduce(top_sum[:, :], top[:, :, :], AX.X, ALU.add))
                    dve.scalar_tensor_tensor(out=affinity[:, :, :], in0=not_top[:, :, :], scalar=0.0,
                                             in1=affinity[:, :, :], op0=ALU.is_lt, op1=ALU.mult)
                    chain(dve.tensor_scalar(top_sum[:, :], top_sum[:, :], 1e-9, None, ALU.add))
                    chain(dve.reciprocal(r_top[:, :], top_sum[:, :]))
                    chain(dve.tensor_tensor(affinity[:, :, :], affinity[:, :, :],
                                            r_top[:, :].unsqueeze(2).to_broadcast([P, 2, EXPERTS]), ALU.mult))
                    if b >= 2:
                        dve.wait_ge(t_route, b - 1)
                    if b == 0:
                        dve.wait_ge(zeroed, 6)
                    to = route[:, b % 2, :, :]
                    chain(dve.tensor_copy(to[:, :, 0:EXPERTS].bitcast(F32R), affinity[:, :, :]))
                    dve.tensor_tensor(to[:, :, EXPERTS:2 * EXPERTS], affinity[:, :, :], to[:, :, 0:EXPERTS],
                                      ALU.subtract).then_inc(route_ready, 1)

            for b in (2, 3):
                for n in range(3):
                    split_qkc(b, n)
                values(b)
            dve.wait_ge(max_zeroed, 1)
            maxima(0)
            maxima(1)
            for i in range(STEPS):
                if i + 2 < STEPS:
                    maxima(i + 2, i - 2)
                else:
                    normalize(i - 2)
                    for name, b in between_at.get(i, ()):
                        long_part(name, b)
                for name, b in tail_at.get(i, ()):
                    tail(name, b)
                for name, b in tail_at.get(i, ()):
                    tail_rest(name, b)
                if i == 2:
                    dve.wait_ge(w_qkv_rounded, 3)
                    lo_half(w_qkv_lo[:, 4, :], w_qkv[:, 4, :], w_qkv_hi[:, 4, :], w_qkv_split)
                    dve.wait_ge(w_r_rounded, 1)
                    lo_half(w_r_lo[:, :], w_r[:, :], w_r_hi[:, :], w_r_split)
                    dve.wait_ge(b_down_rounded, 1)
                    lo_half(b_down_lo[:, :], b_down[:, :], b_down_hi[:, :], b_down_split)

            def residual(c):
                dve.wait_ge(t_ffn, c + 1)
                dve.tensor_tensor(result[:, 4 * c:4 * c + 4, :], bank(6).rearrange("p (t h) -> p t h", t=4),
                                  x1[:, 4 * c:4 * c + 4, :], ALU.add).then_inc(result_ready, 1)

            def left_over(n, slot):
                name, b = v_beside.get((n, slot), ("", 0))
                if name == "norm":
                    long_part(name, b)
                name, b = beside.get((n, slot), ("", 0))
                if name == "turn_out":
                    normalize(b)
                tail(name, b)
                name, b = v_beside.get((n, slot), ("", 0))
                if name == "weights":
                    long_part(name, b)
                tail_rest(name, b)

            for n in range(ITEMS + 1):
                left_over(n, "A")
                if n == 0:
                    left_over(n, "B")
                if n < ITEMS:
                    u, _ = WORK[n]
                    dve.wait_ge(m_up, n + 1)
                    dve.wait_ge(gate_done, n + 1)
                    dve.scalar_tensor_tensor(out=gated[:, n % 3, :], in0=bank(B_UP + n % 2),
                                             scalar=bias_cols[:, BIAS_UP + u:BIAS_UP + u + 1],
                                             in1=gate[:, n % 3, :], op0=ALU.add, op1=ALU.mult).then_inc(gated_done, 1)
                if n:
                    left_over(n, "B")
                if n >= POOL_LO + 1:
                    dve.wait_ge(hid_rounded, n)
                    dve.wait_ge(m_down, n - 3)
                    k = (n - 1) % 3
                    lo_half(hid_lo[:, k, :], hid[:, k, :], hid_hi[:, k, :], hid_lo_done)
                if n < ITEMS:
                    dve.wait_ge(m_wide, n + 1)
                    dve.wait_ge(gated_done, n + 1)
                    if n >= 3:
                        dve.wait_ge(hid_rounded, n - 2)
                        if n - 3 < POOL_LO:
                            dve.wait_ge(pool_lo_done, n - 2)
                        else:
                            dve.wait_ge(hid_lo_done, n - 2 - POOL_LO)
                    dve.tensor_tensor(hid[:, n % 3, :], gated[:, n % 3, :], bank(B_WIDE + n % 2),
                                      ALU.mult).then_inc(hid_done, 1)
                left_over(n, "C")
            residual(0)
            residual(1)

        def turn_ffn(pe, c):
            pe.wait_ge(ffnT_copied, c + 1)
            if c:
                pe.wait_ge(result_ready, c)
            for k in range(4):
                ins = pe.transpose(psum[:, 6, P * k:P * (k + 1)], ffnT[:, P * k:P * (k + 1)], ident[:, :])
            ins.then_inc(t_ffn, 1)

        @block.tensor
        def _(pe):
            misc_read = []

            def take_misc(reader, count):
                if misc_read:
                    pe.wait_ge(*misc_read.pop())
                if reader:
                    misc_read.append((reader, count))

            def product3(dst, w_hi, w_lo, x_hi, x_lo, start=True, stop=True):
                pe.matmul(dst, w_hi, x_hi, start=start, stop=False, skip_group_check=True)
                pe.matmul(dst, w_hi, x_lo, start=False, stop=False, skip_group_check=True)
                return pe.matmul(dst, w_lo, x_hi, start=False, stop=stop, skip_group_check=True)

            def turn_x(b):
                if b >= 2:
                    pe.wait_ge(xT_split, b - 1)
                for k in range(2):
                    if b < 2:
                        pe.wait_ge(x_normed, 2 * b + k + 1)
                    else:
                        pe.wait_ge(late_x_normed, 2 * (b - 2) + k + 1)
                    ins = pe.transpose(psum[:, b % 2, P * k:P * (k + 1)], x1[:, 2 * b + k, :], ident[:, :])
                ins.then_inc(t_x, 1)

            def project(b):
                pe.wait_ge(xT_split, b + 1)
                if b == 0:
                    pe.wait_ge(w_qkv_split, 1)
                for n, (tensor, _) in enumerate(ORDER):
                    if b:
                        pe.wait_ge(qkc_split, 3 * (b - 1) + n + 1)
                    if b == 0 and n == 2:
                        pe.wait_ge(w_qkv_split, 2)
                    product3(bank(B_QKC + n, SEQ), w_qkv_hi[:, tensor, :], w_qkv_lo[:, tensor, :],
                             xT_hi[:, tokens(b)], xT_lo[:, tokens(b)]).then_inc(m_qkc, 1)
                if b:
                    pe.wait_ge(have_value, b)
                for k in range(2):
                    t = tokens(b, k)
                    ins = product3(psum[:, B_VALUE, P * k:P * (k + 1)], xT_hi[:, t], xT_lo[:, t], w_qkv_hi[:, 3, :],
                                   w_qkv_lo[:, 3, :])
                ins.then_inc(m_v, 1)

            pe.wait_ge(have_ident, 1)
            pe.wait_ge(in_ctx, 16)
            for h in range(2):
                ins = pe.transpose(psum[0:CTX_C, B_VALUE, P * h:P * (h + 1)], ctx_sb[:, h, :], ident[:, :])
            ins.then_inc(t_ctx, 1)
            turn_x(0)
            pe.wait_ge(have_ctxT, 1)
            pe.wait_ge(have_w_ck, 1)
            pe.matmul(bank(B_CK, CTX_KEYS), w_ctx[:, 2, :], ctxT[:, :, 0, :], start=True,
                      stop=True).then_inc(m_ck, 1)
            pe.wait_ge(qkc_bias_stacked, 1)
            pe.transpose(bank(B_CV, 4), qkc_bias[:, 1, :], ident[0:4, 0:4]).then_inc(t_bias, 1)
            pe.wait_ge(out_zeroed, 1)
            project(0)
            turn_x(1)
            pe.wait_ge(in_w_cv, 16)
            pe.wait_ge(have_bias_cols, 1)
            for b in range(BATCH):
                ins = pe.matmul(psum[:, B_CV, C * b:C * (b + 1)], ctxT[:, b, :, :], w_ctx[:, 1, :], start=True,
                                stop=True)
            ins.then_inc(m_cv, 1)
            project(1)
            turn_x(2)
            turn_x(3)

            def natural(i):
                b, g = divmod(i, GROUPS)
                KR = SHIFT_ROW
                if i:
                    pe.wait_ge(max_done, 3 * i)
                else:
                    pe.wait_ge(xT_split, BATCH)
                    pe.wait_ge(have_cvalue, 2)
                    pe.wait_ge(ck_split, 1)
                    pe.wait_ge(have_causal, 1)
                    pe.wait_ge(have_ident_bf, 1)
                if g == 0:
                    pe.wait_ge(placed_k[b % 2], 64 * (b // 2 + 1))
                    pe.wait_ge(placed_q[b % 2], 16 * (b // 2 + 1))
                blocks = key_blocks[0:KR, b % 2, g, :, :]

                def masked(to, q, k):
                    diagonal = q == k
                    if diagonal:
                        pe.matmul(to, ident_bf[:, :], causal[:, :, :], start=True, stop=False, skip_group_check=True)
                    return pe.matmul(to, query_rows[0:KR, b % 2, g, 0, P * q:P * (q + 1)], blocks[:, :, P * k:P * (k + 1)],
                                     start=not diagonal, stop=True, skip_group_check=True)

                masked(bank(B_NAT0), 0, 0).then_inc(m_nat, 1)
                if i == 0:
                    pe.wait_ge(placed_ck, 64)
                for t in range(2):
                    ins = pe.matmul(psum[:, B_NATC, SEQ * t:SEQ * (t + 1)], query_rows[0:KR, b % 2, g, 1, P * t:P * (t + 1)],
                                    ckey_blocks[0:KR, g, b, :, :], start=True, stop=True)
                ins.then_inc(m_nat, 1)
                masked(bank(B_NAT1), 1, 0)
                masked(bank(B_NAT1 + 1), 1, 1).then_inc(m_nat, 1)

            def turn_max(i):
                pe.wait_ge(max_done, 3 * i + 3)
                take_misc(shift_placed, i + 1)
                for n in range(4):
                    ins = pe.transpose(psum[0:P - SHIFT_ROW, B_MISC, P * n:P * (n + 1)], row_max[:, i % 2, n, :],
                                       ident[:, :])
                ins.then_inc(t_max, 1)

            def scores(i, c):
                b, g = divmod(i, GROUPS)
                if c == 0:
                    pe.wait_ge(shift_placed, i + 1)
                if i or c >= 2:
                    pe.wait_ge(exp_done, 4 * i + c - 1)
                to = B_ST + c % 2
                if c < 2:
                    for j in range(2):
                        ins = pe.matmul(psum[:, to, SEQ * j:SEQ * (j + 1)], key_blocks[:, b % 2, g, 2 * c + j, 0:P],
                                        query_rows[:, b % 2, g, 0, :], start=True, stop=True)
                if c == 2:
                    for j in range(GROUP):
                        ins = pe.matmul(psum[:, to, P * j:P * (j + 1)], key_blocks[:, b % 2, g, j, P:SEQ],
                                        query_rows[:, b % 2, g, 0, P:SEQ], start=True, stop=True)
                if c == 3:
                    for j in range(2):
                        ins = pe.matmul(psum[:, to, SEQ * j:SEQ * (j + 1)],
                                        ckey_blocks[:, g, b, 2 * j:2 * j + 2, :].rearrange("p j k -> p (j k)"),
                                        query_rows[:, b % 2, g, 1, :], start=True, stop=True)
                ins.then_inc(m_st, 1)

            def attend_self(i):
                b, g = divmod(i, GROUPS)
                if i:
                    pe.wait_ge(o_copied, i)
                else:
                    pe.wait_ge(out_zeroed, 1)
                pe.wait_ge(selected, 2 * i + 1)
                for j in range(GROUP):
                    pe.matmul(psum[32 * j:32 * j + D + 1, B_OUT, 0:SEQ], value[:, 2 * b, GROUP * g + j, :],
                              probs[i % 2][:, j // 2, SEQ * (j % 2):SEQ * (j % 2 + 1)], start=True, stop=False,
                              skip_group_check=True)
                pe.wait_ge(selected, 2 * i + 2)
                for j in range(GROUP):
                    pe.matmul(psum[32 * j:32 * j + D + 1, B_OUT, P:SEQ], value[:, 2 * b + 1, GROUP * g + j, :],
                              probs[i % 2][:, 2, P * j:P * (j + 1)], start=False, stop=True, skip_group_check=True)

            def attend_context(i):
                b, g = divmod(i, GROUPS)
                pe.wait_ge(exp_done, 4 * i + 4)
                for j in range(2):
                    ins = pe.matmul(psum[64 * j:64 * j + 32 + D + 1, B_OUT, SEQ:2 * SEQ],
                                    cvalue[:, b, 2 * g + j, :], probs[i % 2][:, 3, SEQ * j:SEQ * (j + 1)],
                                    start=False, stop=True, skip_group_check=True)
                ins.then_inc(m_out, 1)

            def turn_out(i):
                pe.wait_ge(o_copied, i + 1)
                take_misc(normalized, i + 1)
                for n in range(4):
                    ins = pe.transpose(psum[:, B_MISC, P * n:P * (n + 1)], o_sb[:, i % 2, P * n:P * (n + 1)],
                                       ident[:, :])
                ins.then_inc(t_out, 1)

            def tail(name, b):
                take_misc({"ffn_bias": have_ffn_bias, "y_turn": yT_split, "project": x1_ready, "x2_turn": x2T_split, "router": logits_ready,
                           "route_turn": routeT_ready}[name], b + 1)
                if name == "ffn_bias":
                    pe.wait_ge(in_small, 64)
                    pe.transpose(bank(B_MISC, 2 * UNITS), bias_rows[:, :],
                                 ident[0:2 * UNITS, 0:2 * UNITS]).then_inc(t_ffn_bias, 1)
                if name == "y_turn":
                    pe.wait_ge(y_added, 4 * b + 4)
                    for t in range(2):
                        ins = pe.transpose(psum[:, B_MISC, P * t:P * (t + 1)], y_nat[:, b % 2, t, :], ident[:, :])
                    ins.then_inc(t_y, 1)
                if name == "project":
                    pe.wait_ge(yT_split, b + 1)
                    pe.wait_ge(w_qkv_split, 3)
                    for t in range(2):
                        mine = slice(P * t, P * (t + 1))
                        ins = product3(psum[:, B_MISC, mine], yT_hi[:, mine], yT_lo[:, mine], w_qkv_hi[:, 4, :],
                                       w_qkv_lo[:, 4, :])
                    ins.then_inc(m_proj, 1)
                if name == "x2_turn":
                    pe.wait_ge(x2_normed, 2 * b + 2)
                    for t in range(2):
                        ins = pe.transpose(psum[:, B_MISC, P * t:P * (t + 1)], x2_norm[:, t, :], ident[:, :])
                    ins.then_inc(t_x2, 1)
                if name == "router":
                    pe.wait_ge(x2T_split, b + 1)
                    pe.wait_ge(w_r_split, 1)
                    for t in range(2):
                        ins = product3(psum[:, B_MISC, EXPERTS * t:EXPERTS * (t + 1)], xT_hi[:, tokens(b, t)],
                                       xT_lo[:, tokens(b, t)], w_r_hi[:, :], w_r_lo[:, :])
                    ins.then_inc(m_router, 1)
                if name == "route_turn":
                    pe.wait_ge(route_ready, b + 1)
                    for t in range(2):
                        ins = pe.transpose(psum[:, B_MISC, P * t:P * (t + 1)], route[:, b % 2, t, :], ident[:, :])
                    ins.then_inc(t_route, 1)

            project(2)
            project(3)
            natural(0)
            pe.wait_ge(qkc_split, 3 * BATCH)
            pe.wait_ge(have_value, BATCH)
            turn_max(0)
            natural(1)
            for i in range(STEPS):
                scores(i, 0)
                scores(i, 1)
                if i + 1 < STEPS:
                    turn_max(i + 1)
                if i + 2 < STEPS:
                    natural(i + 2)
                scores(i, 2)
                scores(i, 3)
                if i >= 2:
                    turn_out(i - 2)
                if i:
                    attend_self(i - 1)
                for name, b in tail_at.get(i, ()):
                    tail(name, b)
                if i:
                    attend_context(i - 1)
                for name, b in late_at.get(i, ()):
                    tail(name, b)

            def left_over(n, slot):
                name, b = beside.get((n, slot), ("", 0))
                if name == "attend":
                    attend_self(b)
                    attend_context(b)
                elif name == "turn_out":
                    turn_out(b)
                elif name:
                    tail(name, b)

            pe.wait_ge(b_down_split, 1)
            for n in range(ITEMS + 2):
                if n < ITEMS:
                    u, c = WORK[n]
                    k = u % SLOTS
                    cols = slice(c * CHUNK, (c + 1) * CHUNK)
                    if u == 0:
                        pe.wait_ge(x2T_split, 2 * c + 2)
                    pe.wait_ge(ffn_lo, u + 1)
                    if n >= 2:
                        pe.wait_ge(gate_done, n - 1)
                    product3(bank(B_GATE + n % 2), w_ffn_hi[:, k, 0, :], w_ffn_lo[:, k, 0, :], xT_hi[:, cols],
                             xT_lo[:, cols]).then_inc(m_gate, 1)
                    left_over(n, "A")
                    if n >= 2:
                        pe.wait_ge(gated_done, n - 1)
                    product3(bank(B_UP + n % 2), w_ffn_hi[:, k, 1, :], w_ffn_lo[:, k, 1, :], xT_hi[:, cols],
                             xT_lo[:, cols]).then_inc(m_up, 1)
                    left_over(n, "B")
                    if u == 0:
                        pe.wait_ge(routeT_ready, 2 * c + 2)
                    if n >= 2:
                        pe.wait_ge(hid_done, n - 1)
                    pe.matmul(bank(B_WIDE + n % 2), spread[:, u, :], routeT[:, cols], start=True,
                              stop=True).then_inc(m_wide, 1)
                if n >= 2:
                    m = n - 2
                    u, c = WORK[m]
                    k = u % SLOTS
                    cols = slice(c * CHUNK, (c + 1) * CHUNK)
                    y = bank(6 + c)
                    if u == 0:
                        if c:
                            take_misc(None, 0)
                        pe.matmul(y, b_down_hi[:, :], routeT[:, cols], start=True, stop=False, skip_group_check=True)
                        pe.matmul(y, b_down_lo[:, :], routeT[:, cols], start=False, stop=False, skip_group_check=True)
                    if m < POOL_LO:
                        pe.wait_ge(pool_lo_done, m + 1)
                    else:
                        pe.wait_ge(hid_lo_done, m + 1 - POOL_LO)
                    product3(y, w_ffn_hi[:, k, 2, :], w_ffn_lo[:, k, 2, :], hid_hi[:, m % 3, :], hid_lo[:, m % 3, :],
                             start=False, stop=u == UNITS - 1).then_inc(m_down, 1)
                left_over(n, "C")
                if n == CHUNK_DONE[0] + 6:
                    turn_ffn(pe, 0)
            turn_ffn(pe, 1)


NAMES = {
    "L0_xattn_": ("Wk", "bk", "Wq", "bq", "Wv", "bv", "Wck", "bck", "Wcq", "bcq", "Wcv", "bcv", "Wp", "bp"),
    "L0_ffn_": ("Wr", "br", "Wg_s", "bg_s", "Wu_s", "bu_s", "Wd_s", "bd_s", "Wg", "bg", "Wu", "bu", "Wd", "bd"),
}


def kernel(**inputs):
    import concourse.bacc as bacc
    import numpy as np
    from concourse.bass_utils import run_bass_kernel_spmd

    nc = bacc.Bacc("TRN2", target_bir_lowering=False, num_devices=1)
    arrays = {}

    def declare(name):
        a = np.ascontiguousarray(inputs[name])
        arrays[f"in_{name}"] = a
        return nc.dram_tensor(f"in_{name}", a.shape, mybir.dt.from_np(a.dtype), kind="ExternalInput").ap()

    x = declare("x")
    ctx = declare("ctx_512")
    w = {short: declare(prefix + short) for prefix, shorts in NAMES.items() for short in shorts}
    out = nc.dram_tensor("out_x", (BATCH, SEQ, C), F32, kind="ExternalOutput").ap()
    build(nc, x, ctx, w, out)
    r = run_bass_kernel_spmd(nc, [arrays], core_ids=[0])
    return r.results[0]["out_x"]
```

```python
from contextlib import ExitStack

import concourse.bass as bass
from concourse import mybir

F32 = mybir.dt.float32
F32R = mybir.dt.float32r
BF16 = mybir.dt.bfloat16
ACT = mybir.ActivationFunctionType
ALU = mybir.AluOpType
AX = mybir.AxisListType

P = 128
BATCH, SEQ, C = 4, 256, 128
CTX, CTX_C = 64, 64
HEADS, D = 16, 8
GROUP = 4
GROUPS = HEADS // GROUP
STEPS = BATCH * GROUPS
TOKENS = BATCH * SEQ
CTX_KEYS = BATCH * CTX
TILES = TOKENS // P
CHUNK = 512
CHUNKS = TOKENS // CHUNK
PARTS = 3
QUERY_PARTS, KEY_PARTS = (0, 1, 0), (0, 0, 1)
WRITES = ((0, 1), (1, 2), (2, 4))
NORM_GROUPS = ((0, 2), (2, 4), (4, 8))
SHIFT_ROW = PARTS * GROUP * D
ROWS = SHIFT_ROW + GROUP
PART = GROUP * D
EXPERTS, TOP, INNER = 32, 8, 64
SPREADS = 4
SPREAD_UNITS = 4
PAIRS = EXPERTS // 2
UNITS = PAIRS + 1
SHARED = PAIRS
SCALE = float(1.0 / D ** 0.5)
LN_EPS = 1e-5
MASKED = -1e30

BIAS_GATE, BIAS_UP = 0, UNITS
BIAS_Q, BIAS_K, BIAS_CQ, BIAS_CK = range(2 * UNITS, 2 * UNITS + 4)
BIAS_ROWS = 2 * UNITS + 4
ORDER = ((1, BIAS_K), (0, BIAS_Q), (2, BIAS_CQ))

LEAD = 6
LAST = 4
WORK = ([(u, c) for c in range(CHUNKS) for u in range(LEAD)]
        + [(u, c) for u in range(LEAD, UNITS - LAST) for c in range(CHUNKS)]
        + [(u, c) for c in range(CHUNKS) for u in range(UNITS - LAST, UNITS)])
ITEMS = len(WORK)
assert WORK[-1][0] == SHARED
SLOTS = 6
ROUND_STEP = STEPS - SLOTS
LAST_USE = {u: max(n for n, e in enumerate(WORK) if e[0] == u) for u in range(UNITS)}
FIRST_USE = {u: min(n for n, e in enumerate(WORK) if e[0] == u) for u in range(UNITS)}
SPLIT_AT = {LAST_USE[u - SLOTS] + 4: u for u in range(SLOTS, UNITS)}
CHUNK_DONE = [max(n for n, e in enumerate(WORK) if e[1] == c) for c in range(CHUNKS)]
assert all(n < FIRST_USE[u] for n, u in SPLIT_AT.items()) and len(SPLIT_AT) == UNITS - SLOTS

B_NAT0, B_NATC, B_NAT1, B_ST, B_OUT, B_MISC = 0, 1, 2, 4, 6, 7
B_GATE, B_UP, B_WIDE = 0, 2, 4
B_QKC, B_VALUE, B_CV, B_CK = 4, 7, 2, 3


def build(nc, x, ctx, w, out):
    with ExitStack() as stack:
        def sb(name, shape, dt=F32, until=None):
            return (until or stack).enter_context(nc.sbuf_tensor(name, shape, dt))

        def sem(name):
            return stack.enter_context(nc.semaphore(name))

        key_dram = nc.dram_tensor("key_dram", (GROUP, PARTS * D, GROUPS, TOKENS), F32, kind="Internal").ap()
        ckey_dram = nc.dram_tensor("ckey_dram", (GROUP, PARTS * D, GROUPS, CTX_KEYS), F32, kind="Internal").ap()
        query_dram = nc.dram_tensor("query_dram", (GROUP, PARTS * D, GROUPS, 2, TOKENS), F32, kind="Internal").ap()
        psum = stack.enter_context(nc.psum_tensor("psum", [P, 8, CHUNK], F32))

        ident = sb("ident", [P, P])
        ident_bf = sb("ident_bf", [P, P], BF16)
        ident_r = sb("ident_r", [P, P], F32R)
        causal = sb("causal", [P, GROUP, P], BF16)
        key_const = sb("key_const", [P, GROUP, CTX])
        minus_half = sb("minus_half", [P, TILES])
        spread = sb("spread", [P, PAIRS, P], F32R)
        x_sb = sb("x_sb", [P, TILES, C])
        ctx_sb = sb("ctx_sb", [P, 2, CTX_C])
        w_qkv = sb("w_qkv", [P, 5, C])
        w_qkv_hi = sb("w_qkv_hi", [P, 5, C], F32R)
        w_qkv_lo = sb("w_qkv_lo", [P, 5, C], F32R)
        w_ctx = sb("w_ctx", [CTX_C, 3, C])
        w_r = sb("w_r", [P, EXPERTS])
        w_r_hi = sb("w_r_hi", [P, EXPERTS], F32R)
        w_r_lo = sb("w_r_lo", [P, EXPERTS], F32R)
        bias_rows = sb("bias_rows", [2 * UNITS, P])
        qkc_bias = sb("qkc_bias", [4, 2, C])
        bias_cols = sb("bias_cols", [P, BIAS_ROWS])
        b_wide = sb("b_wide", [P, 3, C])
        b_r = sb("b_r", [P, EXPERTS])
        b_down = sb("b_down", [P, C])
        b_down_hi = sb("b_down_hi", [P, C], F32R)
        b_down_lo = sb("b_down_lo", [P, C], F32R)
        w_ffn = sb("w_ffn", [P, SLOTS, 3, P])
        w_ffn_hi = sb("w_ffn_hi", [P, SLOTS, 3, P], F32R)
        w_ffn_lo = sb("w_ffn_lo", [P, SLOTS, 3, P], F32R)
        stats = sb("stats", [P, TILES, 6])
        moments = sb("moments", [P, TILES, 2])
        var_eps = sb("var_eps", [P, TILES])
        rstd = sb("rstd", [P, TILES])
        x1 = sb("x1", [P, TILES, C])
        xT_hi = sb("xT_hi", [P, TOKENS], F32R)
        xT_lo = sb("xT_lo", [P, TOKENS], F32R)
        ctxT = sb("ctxT", [CTX_C, BATCH, 2, CTX])
        value = sb("value", [P, TILES, HEADS, D + 1])
        cvalue = sb("cvalue", [P, BATCH, HEADS // 2, 32 + D + 1])
        row_max = sb("row_max", [P, 2, 4, GROUP], F32R)
        probs_even = sb("probs_even", [P, 4, CHUNK])
        o_sb = sb("o_sb", [P, 2, CHUNK])
        r_den = sb("r_den", [P, 16])
        o_norm = sb("o_norm", [P, 2, 4 * PART])
        y_nat = sb("y_nat", [P, 2, 2, C])
        yT_hi = sb("yT_hi", [P, SEQ], F32R)
        yT_lo = sb("yT_lo", [P, SEQ], F32R)
        x2_norm = sb("x2_norm", [P, 2, C])
        logits = sb("logits", [P, 2, EXPERTS])
        exp_neg = sb("exp_neg", [P, 2, EXPERTS])
        affinity = sb("affinity", [P, 2, EXPERTS])
        top = sb("top", [P, 2, TOP])
        not_top = sb("not_top", [P, 2, EXPERTS])
        top_sum = sb("top_sum", [P, 2])
        r_top = sb("r_top", [P, 2])
        route = sb("route", [P, 2, 2, P])
        routeT = sb("routeT", [P, TOKENS], F32R)

        with ExitStack() as attention:
            queries = sb("queries", [P, 2, 2, TOKENS], F32R, until=attention)
            ckeys = sb("ckeys", [P, 2, CTX_KEYS], F32R, until=attention)
            query_rows = sb("query_rows", [P, 2, GROUPS, 2, SEQ], F32R, until=attention)
            key_blocks = sb("key_blocks", [P, 2, GROUPS, GROUP, SEQ], F32R, until=attention)
            ckey_blocks = sb("ckey_blocks", [P, GROUPS, BATCH, GROUP, CTX], F32R, until=attention)
            spread_f = sb("spread_f", [P, SPREAD_UNITS, P], until=attention)
            keys = sb("keys", [P, 2, TOKENS], F32R, until=attention)
        probs = [probs_even[:, :, :],
                 keys[:, :, :].rearrange("p h (c n) -> p (h c) n", n=CHUNK).bitcast(F32)]
        gate = sb("gate", [P, 3, CHUNK])
        gated = sb("gated", [P, 3, CHUNK])
        hid = sb("hid", [P, 3, CHUNK])
        hid_hi = sb("hid_hi", [P, 3, CHUNK], F32R)
        hid_lo = sb("hid_lo", [P, 3, CHUNK], F32R)
        ffnT = sb("ffnT", [P, CHUNK])
        result = sb("result", [P, TILES, C])

        in_x = [sem(f"in_x{k}") for k in range(len(NORM_GROUPS))]
        in_small = sem("in_small")
        in_q_bias = sem("in_q_bias")
        in_k_bias = sem("in_k_bias")
        in_ctx = sem("in_ctx")
        in_w_ck = sem("in_w_ck")
        in_w_cv = sem("in_w_cv")
        in_w_kq = sem("in_w_kq")
        in_w_cqv = sem("in_w_cqv")
        in_w_p = sem("in_w_p")
        in_wide = sem("in_wide")
        in_bp = sem("in_bp")
        in_router = sem("in_router")
        in_down_bias = sem("in_down_bias")
        in_ffn = [sem(f"in_ffn{k}") for k in range(SLOTS)]
        placed_q = [sem(f"placed_q{k}") for k in range(2)]
        wrote_k = [sem(f"wrote_k{n}") for n in range(len(WRITES))]
        wrote_ck = sem("wrote_ck")
        wrote_q = [sem(f"wrote_q{n}") for n in range(len(WRITES))]
        placed_k = [sem(f"placed_k{s}") for s in range(2)]
        placed_ck = sem("placed_ck")
        stored = sem("stored")
        zeroed = sem("zeroed")
        have_ident = sem("have_ident")
        have_causal = sem("have_causal")
        have_key_const = sem("have_key_const")
        have_spread = sem("have_spread")
        g_chain = sem("g_chain")
        have_rstd = sem("have_rstd")
        have_x_bp = sem("have_x_bp")
        late_x_normed = sem("late_x_normed")
        selected = sem("selected")
        y_added = sem("y_added")
        ffn_lo = sem("ffn_lo")
        pool_lo_done = sem("pool_lo_done")
        v_chain = sem("v_chain")
        var_ready = sem("var_ready")
        x_normed = sem("x_normed")
        have_idents = sem("have_idents")
        w_qkv_split = sem("w_qkv_split")
        qkc_bias_stacked = sem("qkc_bias_stacked")
        have_bias_cols = sem("have_bias_cols")
        have_ffn_bias = sem("have_ffn_bias")
        have_ctxT = sem("have_ctxT")
        have_w_ck = sem("have_w_ck")
        ck_split = sem("ck_split")
        xT_split = sem("xT_split")
        qkc_split = sem("qkc_split")
        have_value = sem("have_value")
        have_cvalue = sem("have_cvalue")
        key_blocks_set = sem("key_blocks_set")
        key_blocks1_set = sem("key_blocks1_set")
        ckey_blocks_set = sem("ckey_blocks_set")
        out_zeroed = sem("out_zeroed")
        max_done = sem("max_done")
        normalized = sem("normalized")
        yT_split = sem("yT_split")
        x1_ready = sem("x1_ready")
        var2_ready = sem("var2_ready")
        x2_normed = sem("x2_normed")
        x2T_split = sem("x2T_split")
        w_r_split = sem("w_r_split")
        b_down_split = sem("b_down_split")
        logits_ready = sem("logits_ready")
        route_ready = sem("route_ready")
        gated_done = sem("gated_done")
        hid_done = sem("hid_done")
        hid_lo_done = sem("hid_lo_done")
        last_hid = sem("last_hid")
        last_lo = sem("last_lo")
        result_ready = sem("result_ready")
        have_ctxT2 = sem("have_ctxT2")
        w_qkv_rounded = sem("w_qkv_rounded")
        ck_rounded = sem("ck_rounded")
        xT_rounded = sem("xT_rounded")
        qkc_rounded = sem("qkc_rounded")
        w_r_rounded = sem("w_r_rounded")
        b_down_rounded = sem("b_down_rounded")
        spread_copied = sem("spread_copied")
        ffn_rounded = sem("ffn_rounded")
        shift_placed = sem("shift_placed")
        exp_done = sem("exp_done")
        o_copied = sem("o_copied")
        yT_rounded = sem("yT_rounded")
        x2T_rounded = sem("x2T_rounded")
        exp_neg_ready = sem("exp_neg_ready")
        routeT_ready = sem("routeT_ready")
        gate_done = sem("gate_done")
        hid_rounded = sem("hid_rounded")
        last_hi = sem("last_hi")
        ffnT_copied = sem("ffnT_copied")
        t_bias = sem("t_bias")
        t_ffn_bias = sem("t_ffn_bias")
        t_ctx = sem("t_ctx")
        m_ck = sem("m_ck")
        m_cv = sem("m_cv")
        t_x = sem("t_x")
        m_qkc = sem("m_qkc")
        m_v = sem("m_v")
        m_nat = sem("m_nat")
        t_max = sem("t_max")
        m_st = sem("m_st")
        m_out = sem("m_out")
        t_out = sem("t_out")
        t_y = sem("t_y")
        m_proj = sem("m_proj")
        t_x2 = sem("t_x2")
        m_router = sem("m_router")
        t_route = sem("t_route")
        m_gate = sem("m_gate")
        m_up = sem("m_up")
        m_wide = sem("m_wide")
        m_down = sem("m_down")
        t_ffn = sem("t_ffn")

        x_t = x.rearrange("a s c -> (a s) c").rearrange("(t p) c -> p t c", p=P)
        out_t = out.rearrange("a s c -> (a s) c").rearrange("(t p) c -> p t c", p=P)

        def row(v):
            return v.rearrange("(o n) -> o n", o=1)

        def bank(n, cols=CHUNK):
            return psum[:, n, 0:cols]

        def grouped(v):
            return v.rearrange("p (g j d) -> p j d g", j=GROUP, d=D)

        def stacked(v):
            return v.rearrange("p (j d g) -> p j d g", j=GROUP, d=D)

        def tokens(b, tile=None):
            lo = b * SEQ + (tile or 0) * P
            return slice(lo, lo + (SEQ if tile is None else P))

        TAIL = ("y_turn", "project", "x2_turn", "router")
        tail_at = {2: [("ffn_bias", 0)]}
        late_at = {}
        between_at = {}
        for b in range(BATCH - 1):
            for n, name in enumerate(TAIL):
                tail_at.setdefault(4 * b + 6 + n, []).append((name, b))
            between_at[4 * b + 8] = [("norm", b)]
            late_at[4 * b + 11] = [("route_turn", b)]
        beside = {(0, "A"): ("attend", STEPS - 1),
                  (0, "B"): ("turn_out", STEPS - 2),
                  (1, "A"): ("x2_turn", BATCH - 2),
                  (1, "B"): ("router", BATCH - 2),
                  (1, "C"): ("turn_out", STEPS - 1),
                  (2, "A"): ("y_turn", BATCH - 1),
                  (2, "B"): ("project", BATCH - 1),
                  (3, "A"): ("route_turn", BATCH - 2),
                  (4, "A"): ("x2_turn", BATCH - 1),
                  (4, "B"): ("router", BATCH - 1),
                  (6, "A"): ("route_turn", BATCH - 1)}
        v_beside = {(0, "B"): ("norm", BATCH - 2),
                    (1, "C"): ("router", BATCH - 2),
                    (2, "A"): ("weights", BATCH - 2),
                    (2, "C"): ("project", BATCH - 1),
                    (3, "B"): ("norm", BATCH - 1),
                    (4, "C"): ("router", BATCH - 1),
                    (5, "A"): ("weights", BATCH - 1)}
        assert max(beside) <= (LEAD, "A")
        LAST_ITEM = ITEMS - 1
        POOL_LO = [*range(8)]
        VECTOR_LO = [n for n in range(LAST_ITEM) if n not in POOL_LO]

        def projected(b, n, half):
            if n == 0:
                return keys[:, half, tokens(b)]
            return queries[:, half, n - 1, tokens(b)]

        def lo_done(n):
            if n in POOL_LO:
                return pool_lo_done, POOL_LO.index(n) + 1
            return hid_lo_done, VECTOR_LO.index(n) + 1

        def routed(n):
            return sum(u != SHARED for u, _ in WORK[:n])

        def rows_of(n):
            return slice(INNER if WORK[n][0] == SHARED else 0, P)

        HALF = CHUNK // 2
        HALVES = (slice(0, HALF), slice(HALF, CHUNK))
        block = stack.enter_context(nc.Block())

        def write_keys(sp, dram, parts, rounded, split, done):
            sp.wait_ge(*rounded)
            for part, half in enumerate(KEY_PARTS):
                if half:
                    sp.wait_ge(*split)
                sp.dma_start(dram[:, D * part:D * (part + 1), :, :].rearrange("j d g n -> j (d g) n"),
                             parts[:, half, :].bitcast(F32)).then_inc(done, 16)

        def write_token_keys(sp, n):
            first, end = WRITES[n]
            cols = slice(first * SEQ, end * SEQ)
            write_keys(sp, key_dram[:, :, :, cols], keys[:, :, cols], (qkc_rounded, 3 * end - 2),
                       (qkc_split, 3 * end - 2), wrote_k[n])

        def write_queries(sp, n):
            first, end = WRITES[n]
            cols = slice(first * SEQ, end * SEQ)
            sp.wait_ge(qkc_rounded, 3 * end)
            for part in (0, 2, 1):
                half = QUERY_PARTS[part]
                if half:
                    sp.wait_ge(qkc_split, 3 * end)
                sp.dma_start(query_dram[:, D * part:D * (part + 1), :, :, cols].rearrange("j d g s n -> j (d g) s n"),
                             queries[:, half, :, cols].bitcast(F32)).then_inc(wrote_q[n], 16)

        def read_keys(sp, b):
            if b == 0:
                sp.wait_ge(key_blocks_set, 1)
            if b == 1:
                sp.wait_ge(key_blocks1_set, GROUPS)
            if b >= 2:
                sp.wait_ge(m_st, 16 * (b - 1))
            sp.wait_ge(wrote_k[min(b, 2)], 48)
            for j in range(GROUP):
                sp.dma_start(key_blocks[24 * j:24 * (j + 1), b % 2, :, j, :].bitcast(F32),
                             key_dram[j][:, :, tokens(b)]).then_inc(placed_k[b % 2], 16)

        def read_queries(sp, b):
            sp.wait_ge(wrote_q[min(b, 2)], 48)
            sp.dma_start(query_rows[0:SHIFT_ROW, b % 2, :, :, :].rearrange("p g s n -> p (g s) n").bitcast(F32),
                         query_dram.rearrange("j r g s n -> (j r) (g s) n")[:, :, tokens(b)]
                         ).then_inc(placed_q[b % 2], 16)

        def load_unit(sp, u):
            slot = u % SLOTS
            if u >= SLOTS:
                sp.wait_ge(ffn_lo, u - SLOTS + 1)
            if u == SHARED:
                sp.dma_start(w_ffn[:, slot, 0, 0:INNER], w["Wg_s"]).then_inc(in_ffn[slot], 16)
                sp.dma_start(w_ffn[:, slot, 0, INNER:P], w["Wu_s"]).then_inc(in_ffn[slot], 16)
                sp.dma_start(w_ffn[INNER:P, slot, 2, :], w["Wd_s"]).then_inc(in_ffn[slot], 16)
                return
            for n, name in enumerate(("Wg", "Wu")):
                sp.dma_start(w_ffn[:, slot, n, :].rearrange("h (e i) -> h e i", e=2),
                             w[name][2 * u:2 * u + 2].rearrange("e h i -> h e i")).then_inc(in_ffn[slot], 16)
            sp.dma_start(w_ffn[:, slot, 2, :],
                         w["Wd"][2 * u:2 * u + 2].rearrange("e i h -> (e i) h")).then_inc(in_ffn[slot], 16)

        @block.sync
        def _(sp):
            def load_x(k):
                lo, hi = NORM_GROUPS[k]
                sp.dma_start(x_sb[:, lo:hi, :], x_t[:, lo:hi, :]).then_inc(in_x[k], 16)

            load_x(0)
            sp.dma_start(w_qkv[:, 1, :], w["Wk"]).then_inc(in_w_kq, 16)
            load_x(1)
            sp.dma_start(w_qkv[:, 0, :], w["Wq"]).then_inc(in_w_kq, 16)
            for name, r0 in (("bk", BIAS_K), ("bck", BIAS_CK)):
                sp.dma_start(qkc_bias[r0 - BIAS_Q:r0 - BIAS_Q + 1, 0, :], row(w[name])).then_inc(in_k_bias, 16)
            sp.dma_start(w_qkv[:, 2, :], w["Wcq"]).then_inc(in_w_cqv, 16)
            sp.dma_start(w_qkv[:, 3, :], w["Wv"]).then_inc(in_w_cqv, 16)
            load_x(2)
            sp.dma_start(w_ctx[:, 1, :], w["Wcv"]).then_inc(in_w_cv, 16)
            for n, name in enumerate(("bv", "bcv")):
                sp.dma_start(b_wide[:, n, :], row(w[name]).to_broadcast([P, C])).then_inc(in_wide, 16)
            write_token_keys(sp, 0)
            write_queries(sp, 0)
            read_keys(sp, 0)
            read_queries(sp, 0)
            sp.wait_ge(ckey_blocks_set, 2)
            sp.wait_ge(wrote_ck, 48)
            for j in range(GROUP):
                sp.dma_start(ckey_blocks[24 * j:24 * (j + 1), :, :, j, :].rearrange("r g b k -> r (g b) k").bitcast(F32),
                             ckey_dram[j].rearrange("r g (b k) -> r (g b) k", b=BATCH)).then_inc(placed_ck, 16)
            for n in (1, 2):
                write_token_keys(sp, n)
                write_queries(sp, n)
            read_keys(sp, 1)
            read_queries(sp, 1)
            sp.dma_start(b_wide[:, 2, :], row(w["bp"]).to_broadcast([P, C])).then_inc(in_bp, 16)
            sp.dma_start(w_qkv[:, 4, :], w["Wp"]).then_inc(in_w_p, 16)
            sp.wait_ge(zeroed, 4)
            for name, r0 in (("bg", BIAS_GATE), ("bu", BIAS_UP)):
                sp.dma_start(bias_rows[r0:r0 + PAIRS, :],
                              w[name].rearrange("(p e) i -> p (e i)", e=2)).then_inc(in_small, 16)
            sp.dma_start(bias_rows[PAIRS:PAIRS + 1, 0:INNER], row(w["bg_s"])).then_inc(in_small, 16)
            sp.dma_start(bias_rows[BIAS_UP + PAIRS:BIAS_UP + UNITS, INNER:P], row(w["bu_s"])).then_inc(in_small, 16)
            sp.dma_start(w_r[:, :], w["Wr"]).then_inc(in_router, 16)
            sp.dma_start(b_r[:, :], row(w["br"]).to_broadcast([P, EXPERTS])).then_inc(in_router, 16)
            sp.wait_ge(zeroed, 5)
            sp.dma_start(b_down[0:EXPERTS, :], w["bd"]).then_inc(in_down_bias, 16)
            sp.dma_start(b_down[EXPERTS:2 * EXPERTS, :], w["bd"]).then_inc(in_down_bias, 16)
            sp.dma_start(b_down[2 * EXPERTS:2 * EXPERTS + 1, :], row(w["bd_s"])).then_inc(in_down_bias, 16)
            for u in range(SLOTS):
                load_unit(sp, u)
            read_keys(sp, 2)
            read_queries(sp, 2)
            read_keys(sp, 3)
            read_queries(sp, 3)
            for u in range(SLOTS, UNITS):
                load_unit(sp, u)
            for n, (first, end) in enumerate(((0, 4), (4, 6), (6, 8))):
                sp.wait_ge(result_ready, n + 1)
                sp.dma_start(out_t[:, first:end, :], result[:, first:end, :]).then_inc(stored, 16)
            sp.wait_ge(stored, 16 * 3)

        @block.gpsimd
        def _(pool):
            chained = [0]

            def chain(ins):
                chained[0] += 1
                ins.then_inc(g_chain, 1)
                pool.wait_ge(g_chain, chained[0])

            chain(pool.memset(key_const[:, :, :], 0.0))
            pool.affine_select(out=key_const[:, :, :], in_=key_const[:, :, :], compare_op=ALU.not_equal,
                               fill=-1.0, base=-SHIFT_ROW, pattern=[[-1, GROUP], [0, CTX]],
                               channel_multiplier=1).then_inc(have_key_const, 1)
            chain(pool.memset(ident[:, :], 0.0))
            pool.affine_select(out=ident[:, :], in_=ident[:, :], compare_op=ALU.not_equal, fill=1.0, base=0,
                               pattern=[[-1, P]], channel_multiplier=1).then_inc(have_ident, 1)
            chain(pool.memset(minus_half[:, :], -0.5))
            for name, r0 in (("bq", BIAS_Q), ("bcq", BIAS_CQ)):
                pool.dma_start(qkc_bias[r0 - BIAS_Q:r0 - BIAS_Q + 1, 0, :], row(w[name])).then_inc(in_q_bias, 16)

            def first_rstd(k):
                lo, hi = NORM_GROUPS[k]
                pool.wait_ge(var_ready, k + 1)
                pool.tensor_tensor(rstd[:, lo:hi], var_eps[:, lo:hi], minus_half[:, 0:hi - lo],
                                   ALU.pow).then_inc(have_rstd, 1)

            first_rstd(0)
            pool.memset(value[:, :, :, :], 1.0).then_inc(zeroed, 1)
            pool.memset(cvalue[:, :, :, :], 0.0).then_inc(g_chain, 1)
            chained[0] += 1
            pool.wait_ge(g_chain, chained[0])
            pool.memset(cvalue[0:CTX, :, :, D:D + 1], 1.0).then_inc(zeroed, 1)
            pool.wait_ge(zeroed, 2)
            pool.memset(cvalue[CTX:P, :, :, 32 + D:32 + D + 1], 1.0).then_inc(zeroed, 1)
            pool.wait_ge(zeroed, 3)
            first_rstd(1)
            write_keys(pool, ckey_dram, ckeys, (ck_rounded, 1), (ck_split, 1), wrote_ck)
            first_rstd(2)
            pool.wait_ge(have_rstd, 3)
            for t in range(*NORM_GROUPS[2]):
                pool.tensor_scalar(x1[:, t, :], x_sb[:, t, :], moments[:, t, 0:1], rstd[:, t:t + 1],
                                   ALU.subtract, ALU.mult).then_inc(late_x_normed, 1)
            chain(pool.memset(causal[:, :, :], 0.0))
            pool.affine_select(out=causal[:, :, :], in_=causal[:, :, :], compare_op=ALU.is_ge, fill=MASKED, base=0,
                               pattern=[[0, GROUP], [-1, P]], channel_multiplier=1).then_inc(have_causal, 1)
            pool.wait_ge(zeroed, 3)
            pool.memset(bias_rows[:, :], 0.0).then_inc(zeroed, 1)
            pool.memset(b_down[:, :], 0.0).then_inc(zeroed, 1)
            chain(pool.memset(route[:, :, :, :], 0.0))
            pool.memset(route[:, :, :, 2 * EXPERTS:2 * EXPERTS + 1], 1.0).then_inc(zeroed, 1)

            def add_bp(b):
                for t in (2 * b, 2 * b + 1):
                    ins = pool.tensor_tensor(x_sb[:, t, :], x_sb[:, t, :], b_wide[:, 2, :], ALU.add)
                ins.then_inc(have_x_bp, 1)

            def make_spread(k):
                if k:
                    pool.wait_ge(spread_copied, k)
                body = spread_f[:, :, :].rearrange("p u (e i) -> p u e i", e=2)
                chain(pool.memset(spread_f[:, :, :], 0.0))
                for half in range(2):
                    ins = pool.affine_select(out=body, in_=body, compare_op=ALU.not_equal, fill=1.0,
                                             base=-EXPERTS * half - 2 * SPREAD_UNITS * k,
                                             pattern=[[-2, SPREAD_UNITS], [-1, 2], [0, INNER]],
                                             channel_multiplier=1)
                    if half == 0:
                        chain(ins)
                ins.then_inc(have_spread, 1)

            def split_unit(u):
                k = u % SLOTS
                pool.wait_ge(ffn_rounded, u + 1)
                ins = pool.tensor_tensor(w_ffn_lo[:, k, :, :], w_ffn[:, k, :, :], w_ffn_hi[:, k, :, :].bitcast(F32),
                                         ALU.subtract).then_inc(ffn_lo, 1)

            def add_y(i):
                b, g = divmod(i, GROUPS)
                pool.wait_ge(normalized, i + 1)
                if g == 0 and b >= 2:
                    pool.wait_ge(t_y, b - 1)
                pool.tensor_tensor(y_nat[:, b % 2, :, PART * g:PART * (g + 1)],
                                   o_norm[:, i % 2, 0:2 * PART].rearrange("p (t c) -> p t c", t=2),
                                   o_norm[:, i % 2, 2 * PART:4 * PART].rearrange("p (t c) -> p t c", t=2),
                                   ALU.add).then_inc(y_added, 1)

            def tail(name, b):
                if name == "project":
                    pool.wait_ge(var2_ready, b + 1)
                    pool.tensor_tensor(rstd[:, 2 * b:2 * b + 2], var_eps[:, 2 * b:2 * b + 2], minus_half[:, 0:2],
                                       ALU.pow).then_inc(have_rstd, 1)

            for i in range(STEPS):
                pool.wait_ge(exp_done, 4 * i + 2)
                for_k0 = probs[i % 2][:, 0:2, :].rearrange("p c (j q) -> p (c j) q", j=2)[:, :, 0:P]
                pool.affine_select(out=for_k0, in_=for_k0, compare_op=ALU.is_ge, fill=0.0, base=0,
                                   pattern=[[0, GROUP], [1, P]], channel_multiplier=-1).then_inc(selected, 1)
                pool.wait_ge(exp_done, 4 * i + 3)
                for_k1 = probs[i % 2][:, 2, :].rearrange("p (j q) -> p j q", j=GROUP)
                pool.affine_select(out=for_k1, in_=for_k1, compare_op=ALU.is_ge, fill=0.0, base=0,
                                   pattern=[[0, GROUP], [1, P]], channel_multiplier=-1).then_inc(selected, 1)
                if i >= 2:
                    add_y(i - 2)
                for name, b in tail_at.get(i, ()):
                    tail(name, b)
                if i < BATCH:
                    if i == 0:
                        pool.wait_ge(in_bp, 16)
                        pool.wait_ge(x_normed, NORM_GROUPS[2][0])
                        pool.wait_ge(late_x_normed, TILES - NORM_GROUPS[2][0])
                    add_bp(i)
                elif i % 2 and i // 2 - 2 < SPREADS:
                    make_spread(i // 2 - 2)
                if ROUND_STEP <= i < ROUND_STEP + SLOTS:
                    split_unit(i - ROUND_STEP)
            add_y(STEPS - 2)
            add_y(STEPS - 1)

            def lower_half(n):
                pool.wait_ge(hid_rounded, n + 1)
                if n >= 3:
                    pool.wait_ge(m_down, n - 2)
                pool.tensor_tensor(hid_lo[:, n % 3, :], hid[:, n % 3, :], hid_hi[:, n % 3, :].bitcast(F32),
                                   ALU.subtract).then_inc(pool_lo_done, 1)

            for n in POOL_LO:
                if ("project", BATCH - 1) in [beside.get((n, slot)) for slot in "ABC"]:
                    tail("project", BATCH - 1)
                lower_half(n)
            for u in range(SLOTS, UNITS):
                split_unit(u)

        @block.scalar
        def _(act):
            act.dma_start(ctx_sb[:, :, :], ctx.rearrange("(h a) k c -> (a k) h c", a=2)).then_inc(in_ctx, 16)
            act.dma_start(w_ctx[:, 0, :], w["Wck"]).then_inc(in_w_ck, 16)

            def blocks_const(g):
                act.copy(key_blocks[:, 1, g, :, :].rearrange("p j (r k) -> p j r k", k=CTX),
                         key_const[:, :, :].unsqueeze(2).to_broadcast([P, GROUP, SEQ // CTX, CTX])
                         ).then_inc(key_blocks1_set, 1)

            def copy_hi(dst, src, done):
                act.copy(dst, src).then_inc(done, 1)

            def ckey_const(g):
                return act.copy(ckey_blocks[:, g, :, :, :],
                                key_const[:, :, :].unsqueeze(1).to_broadcast([P, BATCH, GROUP, CTX]))

            act.wait_ge(have_key_const, 1)
            ckey_const(0)
            act.wait_ge(t_ctx, 1)
            act.copy(ctxT[:, :, 1, :], psum[0:CTX_C, B_VALUE, 0:CTX_KEYS]
                     .rearrange("p (b k) -> p b k", b=BATCH)).then_inc(have_ctxT2, 1)
            act.wait_ge(in_w_kq, 32)
            for n in (1, 0):
                ins = act.copy(stacked(w_qkv_hi[:, n, :]), grouped(w_qkv[:, n, :]))
            ins.then_inc(w_qkv_rounded, 1)

            def round_x(b):
                act.wait_ge(t_x, b + 1)
                copy_hi(xT_hi[:, tokens(b)], bank(b % 2, SEQ), xT_rounded)

            round_x(0)
            for b in range(BATCH):
                if b == 0:
                    act.wait_ge(in_w_cqv, 32)
                    act.copy(stacked(w_qkv_hi[:, 2, :]), grouped(w_qkv[:, 2, :]))
                    act.copy(w_qkv_hi[:, 3, :], w_qkv[:, 3, :]).then_inc(w_qkv_rounded, 1)
                    act.wait_ge(have_bias_cols, 1)
                    act.wait_ge(m_ck, 1)
                    act.activation(ckeys[:, 0, :], bank(B_CK, CTX_KEYS), ACT.Identity,
                                   bias=bias_cols[:, BIAS_CK:BIAS_CK + 1]).then_inc(ck_rounded, 1)
                for n, (tensor, bias) in enumerate(ORDER):
                    act.wait_ge(m_qkc, 3 * b + n + 1)
                    act.activation(projected(b, n, 0), bank(B_QKC + n, SEQ), ACT.Identity,
                                   bias=bias_cols[:, bias:bias + 1]).then_inc(qkc_rounded, 1)
                if b == 0:
                    round_x(1)
                    for g in range(1, 2):
                        ins = ckey_const(g)
                    ins.then_inc(ckey_blocks_set, 1)
                if b == 1:
                    round_x(2)
                    round_x(3)

            def shift(i):
                b, g = divmod(i, GROUPS)
                act.wait_ge(t_max, i + 1)
                act.copy(query_rows[SHIFT_ROW:ROWS, b % 2, g, :, :],
                         psum[0:GROUP, B_MISC, :].rearrange("p (s n) -> p s n", s=2)).then_inc(shift_placed, 1)

            def exps(i, parts):
                if i == 1:
                    for done in wrote_k:
                        act.wait_ge(done, 48)
                if i >= 2:
                    act.wait_ge(m_out, i - 1)
                for c in parts:
                    act.wait_ge(m_st, 4 * i + c + 1)
                    act.activation(probs[i % 2][:, c, :], bank(B_ST + c % 2), ACT.Exp,
                                   scale=SCALE).then_inc(exp_done, 1)

            def copy_out(i):
                act.wait_ge(m_out, i + 1)
                if i >= 2:
                    act.wait_ge(t_out, i - 1)
                act.copy(o_sb[:, i % 2, :], bank(B_OUT)).then_inc(o_copied, 1)

            def round_unit(u):
                k = u % SLOTS
                act.wait_ge(in_ffn[k], 48 * (u // SLOTS + 1))
                if u >= SLOTS:
                    act.wait_ge(m_down, LAST_USE[u - SLOTS] + 1)
                act.copy(w_ffn_hi[:, k, :, :], w_ffn[:, k, :, :]).then_inc(ffn_rounded, 1)

            def tail(name, b):
                if name == "y_turn":
                    act.wait_ge(t_y, b + 1)
                    copy_hi(yT_hi[:, :], bank(B_MISC, SEQ), yT_rounded)
                if name == "x2_turn":
                    act.wait_ge(t_x2, b + 1)
                    copy_hi(xT_hi[:, tokens(b)], bank(B_MISC, SEQ), x2T_rounded)
                if name == "route_turn":
                    act.wait_ge(t_route, b + 1)
                    act.copy(routeT[:, tokens(b)], bank(B_MISC, SEQ)).then_inc(routeT_ready, 1)

            def tail_rest(name, b):
                if name == "router":
                    act.wait_ge(logits_ready, b + 1)
                    act.activation(exp_neg[:, :, :], logits[:, :, :], ACT.Exp, scale=-1.0).then_inc(exp_neg_ready, 1)

            blocks_const(0)
            blocks_const(1)
            shift(0)
            blocks_const(2)
            for i in range(STEPS):
                exps(i, (0,))
                if i + 1 < STEPS:
                    shift(i + 1)
                exps(i, (1,))
                if i == 2:
                    act.wait_ge(in_w_p, 16)
                    act.copy(w_qkv_hi[:, 4, :], w_qkv[:, 4, :]).then_inc(w_qkv_rounded, 1)
                    act.wait_ge(in_router, 32)
                    copy_hi(w_r_hi[:, :], w_r[:, :], w_r_rounded)
                    act.wait_ge(in_down_bias, 48)
                    copy_hi(b_down_hi[:, :], b_down[:, :], b_down_rounded)
                if ROUND_STEP <= i < ROUND_STEP + SLOTS:
                    round_unit(i - ROUND_STEP)
                if i % 2 and 0 <= i // 2 - 3 < SPREADS:
                    k = i // 2 - 3
                    act.wait_ge(have_spread, k + 1)
                    act.copy(spread[:, SPREAD_UNITS * k:SPREAD_UNITS * (k + 1), :],
                             spread_f[:, :, :]).then_inc(spread_copied, 1)
                exps(i, (2, 3))
                for name, b in tail_at.get(i, ()):
                    tail(name, b)
                if i:
                    copy_out(i - 1)
                for name, b in tail_at.get(i, ()):
                    tail_rest(name, b)
                for name, b in late_at.get(i, ()):
                    tail(name, b)

            def left_over(n, slot):
                name, b = beside.get((n, slot), ("", 0))
                if name == "attend":
                    copy_out(b)
                tail(name, b)
                name, b = v_beside.get((n, slot), ("", 0))
                if name == "router":
                    tail_rest(name, b)

            act.wait_ge(have_ffn_bias, 1)
            for done in wrote_q:
                act.wait_ge(done, 48)
            act.wait_ge(wrote_ck, 48)
            for n in range(ITEMS + 1):
                if n < ITEMS:
                    u, _ = WORK[n]
                    act.wait_ge(m_gate, n + 1)
                    if n >= 3:
                        if WORK[n - 3][0] == SHARED:
                            act.wait_ge(hid_done, n - 2)
                        else:
                            act.wait_ge(gated_done, routed(n - 2))
                    of = slice(0, INNER if u == SHARED else P)
                    for part in (slice(0, CHUNK),) if n < LAST_ITEM else HALVES:
                        act.activation(gate[rows_of(n), n % 3, part], psum[of, B_GATE + n % 2, part], ACT.Silu,
                                       bias=bias_cols[of, BIAS_GATE + u:BIAS_GATE + u + 1]).then_inc(gate_done, 1)
                left_over(n, "A")
                if 1 <= n <= LAST_ITEM:
                    act.wait_ge(hid_done, n)
                    if n >= 4:
                        act.wait_ge(m_down, n - 3)
                    act.copy(hid_hi[rows_of(n - 1), (n - 1) % 3, :],
                             hid[rows_of(n - 1), (n - 1) % 3, :]).then_inc(hid_rounded, 1)
                left_over(n, "B")
                left_over(n, "C")
                if n in SPLIT_AT:
                    round_unit(SPLIT_AT[n])
                if n == CHUNK_DONE[0] + 3:
                    act.wait_ge(m_down, CHUNK_DONE[0] + 1)
                    act.copy(ffnT[:, :], bank(6)).then_inc(ffnT_copied, 1)
            for h, part in enumerate(HALVES):
                act.wait_ge(last_hid, h + 1)
                if h == 0:
                    act.wait_ge(m_down, LAST_ITEM - 2)
                act.copy(hid_hi[INNER:P, LAST_ITEM % 3, part],
                         hid[INNER:P, LAST_ITEM % 3, part]).then_inc(last_hi, 1)
            act.wait_ge(m_down, ITEMS)
            act.wait_ge(t_ffn, 1)
            for part in HALVES:
                act.copy(ffnT[:, part], bank(7)[:, part]).then_inc(ffnT_copied, 1)

        @block.vector
        def _(dve):
            chained = [0]

            def chain(ins):
                chained[0] += 1
                ins.then_inc(v_chain, 1)
                dve.wait_ge(v_chain, chained[0])

            def norm_stats(src, tiles, done):
                for k in range(tiles.start, tiles.stop):
                    ins = dve.bn_stats(stats[:, k, :], src[:, k, :])
                chain(ins)
                for k in range(tiles.start, tiles.stop):
                    ins = dve.bn_aggr(moments[:, k, :], stats[:, k, :])
                chain(ins)
                dve.tensor_scalar(var_eps[:, tiles], moments[:, tiles, 1], LN_EPS, None, ALU.add).then_inc(done, 1)

            def lo_half(dst, src, hi, done):
                return dve.tensor_tensor(dst, src, hi.bitcast(F32), ALU.subtract).then_inc(done, 1)

            def stats_of(k):
                dve.wait_ge(in_x[k], 16)
                norm_stats(x_sb, slice(*NORM_GROUPS[k]), var_ready)

            def norm(k):
                dve.wait_ge(have_rstd, k + 1)
                for t in range(*NORM_GROUPS[k]):
                    dve.tensor_scalar(x1[:, t, :], x_sb[:, t, :], moments[:, t, 0:1], rstd[:, t:t + 1],
                                      ALU.subtract, ALU.mult).then_inc(x_normed, 1)

            def blocks_const(g, copy=0):
                return dve.tensor_copy(key_blocks[:, copy, g, :, :].rearrange("p j (r k) -> p j r k", k=CTX),
                                       key_const[:, :, :].unsqueeze(2).to_broadcast([P, GROUP, SEQ // CTX, CTX]))

            def ckey_const(g):
                return dve.tensor_copy(ckey_blocks[:, g, :, :, :],
                                       key_const[:, :, :].unsqueeze(1).to_broadcast([P, BATCH, GROUP, CTX]))

            def lo_weights(n):
                return dve.tensor_tensor(stacked(w_qkv_lo[:, n, :]), grouped(w_qkv[:, n, :]),
                                         stacked(w_qkv_hi[:, n, :]).bitcast(F32), ALU.subtract)

            dve.memset(bank(B_OUT), 0.0).then_inc(out_zeroed, 1)
            dve.wait_ge(have_key_const, 1)
            for g in range(2):
                blocks_const(g)
            stats_of(0)
            blocks_const(2)
            norm(0)
            dve.wait_ge(have_ctxT2, 1)
            dve.tensor_copy(ctxT[:, :, 0, :],
                            psum[0:CTX_C, B_VALUE, 0:CTX_KEYS].rearrange("p (b k) -> p b k", b=BATCH)
                            ).then_inc(have_ctxT, 1)
            dve.wait_ge(in_w_ck, 16)
            dve.tensor_copy(stacked(w_ctx[:, 2, :]), grouped(w_ctx[:, 0, :])).then_inc(have_w_ck, 1)
            dve.wait_ge(w_qkv_rounded, 1)
            lo_weights(1)
            lo_weights(0).then_inc(w_qkv_split, 1)
            dve.wait_ge(in_q_bias, 32)
            dve.wait_ge(in_k_bias, 32)
            dve.tensor_copy(stacked(qkc_bias[:, 1, :]), grouped(qkc_bias[:, 0, :])).then_inc(qkc_bias_stacked, 1)

            def value_add(dst, src, which, done):
                dve.tensor_tensor(dst, src, which, ALU.add).then_inc(done, 1)

            def split_x(b):
                dve.wait_ge(xT_rounded, b + 1)
                lo_half(xT_lo[:, tokens(b)], bank(b % 2, SEQ), xT_hi[:, tokens(b)], xT_split)

            def split_qkc(b, n):
                bias = ORDER[n][1]
                dve.wait_ge(qkc_rounded, 3 * b + n + 1)
                dve.scalar_tensor_tensor(out=projected(b, n, 1), in0=bank(B_QKC + n, SEQ),
                                         scalar=bias_cols[:, bias:bias + 1],
                                         in1=projected(b, n, 0).bitcast(F32),
                                         op0=ALU.add, op1=ALU.subtract).then_inc(qkc_split, 1)

            def values(b):
                dve.wait_ge(m_v, b + 1)
                if b == 0:
                    dve.wait_ge(in_wide, 32)
                    dve.wait_ge(zeroed, 1)
                value_add(value[:, 2 * b:2 * b + 2, :, 0:D],
                          bank(B_VALUE, SEQ).rearrange("p (t h d) -> p t h d", t=2, h=HEADS),
                          b_wide[:, 0, :].rearrange("p (h d) -> p h d", h=HEADS).unsqueeze(1)
                          .to_broadcast([P, 2, HEADS, D]), have_value)

            split_x(0)
            stats_of(1)
            dve.wait_ge(t_bias, 1)
            dve.tensor_copy(bias_cols[:, BIAS_Q:BIAS_ROWS],
                            bank(B_CV, 4)).then_inc(have_bias_cols, 1)
            dve.wait_ge(w_qkv_rounded, 2)
            lo_weights(2)
            lo_half(w_qkv_lo[:, 3, :], w_qkv[:, 3, :], w_qkv_hi[:, 3, :], w_qkv_split)
            dve.wait_ge(ck_rounded, 1)
            dve.scalar_tensor_tensor(out=ckeys[:, 1, :], in0=bank(B_CK, CTX_KEYS),
                                     scalar=bias_cols[:, BIAS_CK:BIAS_CK + 1], in1=ckeys[:, 0, :].bitcast(F32),
                                     op0=ALU.add, op1=ALU.subtract).then_inc(ck_split, 1)
            split_qkc(0, 0)
            split_qkc(0, 1)
            stats_of(2)
            norm(1)
            split_qkc(0, 2)
            blocks_const(3).then_inc(key_blocks_set, 1)
            split_x(1)
            values(0)
            dve.tensor_copy(ident_bf[:, :], ident[:, :])
            dve.tensor_copy(ident_r[:, :], ident[:, :]).then_inc(have_idents, 1)
            for g in range(2, GROUPS):
                ins = ckey_const(g)
            ins.then_inc(ckey_blocks_set, 1)
            for n in range(3):
                split_qkc(1, n)
            split_x(2)
            split_x(3)
            values(1)
            dve.wait_ge(m_cv, 1)
            dve.wait_ge(zeroed, 3)
            for h in range(2):
                rows = slice(CTX * h, CTX * (h + 1))
                src = psum[rows, B_CV, :].rearrange("p (b q e d) -> p b q e d", b=BATCH, e=2, d=D)[:, :, :, h, :]
                wide = b_wide[rows, 1, :].rearrange("p (q e d) -> p q e d", e=2, d=D)[:, :, h, :]
                value_add(cvalue[rows, :, :, 32 * h:32 * h + D], src,
                          wide.unsqueeze(1).to_broadcast([CTX, BATCH, HEADS // 2, D]), have_cvalue)

            def maxima(i, outputs=-1):
                to = row_max[:, i % 2, :, :]
                if i >= 2:
                    dve.wait_ge(t_max, i - 1)

                def tile_0():
                    dve.tensor_reduce(to[:, 0, :], bank(B_NAT0).rearrange("p (j k) -> p j k", j=GROUP),
                                      AX.X, ALU.max).then_inc(max_done, 1)

                def tile_1():
                    dve.tensor_reduce(to[:, 1, :],
                                      psum[:, B_NAT1:B_NAT1 + 2, :].rearrange("p k (j c) -> p j k c", j=GROUP),
                                      AX.XY, ALU.max).then_inc(max_done, 1)

                def context():
                    dve.tensor_reduce(to[:, 2:4, :],
                                      bank(B_NATC).rearrange("p (t j k) -> p t j k", t=2, j=GROUP),
                                      AX.X, ALU.max).then_inc(max_done, 1)

                dve.wait_ge(m_nat, 3 * i + 1)
                tile_0()
                if i == 0:
                    dve.wait_ge(m_nat, 2)
                    tile_1()
                    split_qkc(BATCH - 1, 0)
                    values(BATCH - 1)
                    dve.wait_ge(m_nat, 3)
                    context()
                    split_qkc(BATCH - 1, 1)
                    split_qkc(BATCH - 1, 2)
                    return
                dve.wait_ge(m_nat, 3 * i + 2)
                context()
                for name, b in between_at.get(i - 2, ()):
                    long_part(name, b)
                if outputs >= 0:
                    normalize(outputs)
                dve.wait_ge(m_nat, 3 * i + 3)
                tile_1()

            def normalize(i):
                turned = bank(B_MISC).rearrange("p (j d) -> p j d", d=32)
                dve.wait_ge(t_out, i + 1)
                chain(dve.reciprocal(r_den[:, :].unsqueeze(2), turned[:, :, D:D + 1]))
                if i >= 2:
                    dve.wait_ge(y_added, i - 1)
                dve.tensor_tensor(o_norm[:, i % 2, :].rearrange("p (j d) -> p j d", d=D), turned[:, :, 0:D],
                                  r_den[:, :].unsqueeze(2).to_broadcast([P, 16, D]), ALU.mult)\
                   .then_inc(normalized, 1)

            def tail(name, b):
                mine = slice(2 * b, 2 * b + 2)
                if name == "ffn_bias":
                    dve.wait_ge(t_ffn_bias, 1)
                    dve.tensor_copy(bias_cols[:, 0:2 * UNITS], bank(B_MISC, 2 * UNITS)).then_inc(have_ffn_bias, 1)
                if name == "y_turn":
                    dve.wait_ge(yT_rounded, b + 1)
                    lo_half(yT_lo[:, :], bank(B_MISC, SEQ), yT_hi[:, :], yT_split)
                if name == "project":
                    dve.wait_ge(m_proj, b + 1)
                    dve.wait_ge(have_x_bp, b + 1)
                    dve.tensor_tensor(x1[:, mine, :], bank(B_MISC, SEQ).rearrange("p (t c) -> p t c", t=2),
                                      x_sb[:, mine, :], ALU.add).then_inc(x1_ready, 1)
                if name == "x2_turn":
                    dve.wait_ge(x2T_rounded, b + 1)
                    lo_half(xT_lo[:, tokens(b)], bank(B_MISC, SEQ), xT_hi[:, tokens(b)],
                            x2T_split)
                if name == "router":
                    dve.wait_ge(m_router, b + 1)
                    dve.tensor_tensor(logits[:, :, :], bank(B_MISC, 2 * EXPERTS).rearrange("p (t e) -> p t e", t=2),
                                      b_r[:, :].unsqueeze(1).to_broadcast([P, 2, EXPERTS]),
                                      ALU.add).then_inc(logits_ready, 1)

            def tail_rest(name, b):
                mine = slice(2 * b, 2 * b + 2)
                if name == "project":
                    dve.wait_ge(x1_ready, b + 1)
                    norm_stats(x1, mine, var2_ready)

                if name == "router":
                    dve.wait_ge(exp_neg_ready, b + 1)
                    chain(dve.tensor_scalar(exp_neg[:, :, :], exp_neg[:, :, :], 1.0, None, ALU.add))
                    chain(dve.reciprocal(affinity[:, :, :], exp_neg[:, :, :]))
                    for t in range(2):
                        ins = dve.max(top[:, t, :], affinity[:, t, :])
                    chain(ins)
                    for t in range(2):
                        dve.match_replace(not_top[:, t, :], top[:, t, :], affinity[:, t, :], -1.0)

            def long_part(name, b):
                mine = slice(2 * b, 2 * b + 2)
                if name == "norm":
                    dve.wait_ge(have_rstd, len(NORM_GROUPS) + b + 1)
                    for t in range(2):
                        k = 2 * b + t
                        dve.tensor_scalar(x2_norm[:, t, :], x1[:, k, :], moments[:, k, 0:1], rstd[:, k:k + 1],
                                          ALU.subtract, ALU.mult).then_inc(x2_normed, 1)
                if name == "weights":
                    chain(dve.tensor_reduce(top_sum[:, :], top[:, :, :], AX.X, ALU.add))
                    dve.scalar_tensor_tensor(out=affinity[:, :, :], in0=not_top[:, :, :], scalar=0.0,
                                             in1=affinity[:, :, :], op0=ALU.is_lt, op1=ALU.mult)
                    chain(dve.tensor_scalar(top_sum[:, :], top_sum[:, :], 1e-9, None, ALU.add))
                    chain(dve.reciprocal(r_top[:, :], top_sum[:, :]))
                    chain(dve.tensor_tensor(affinity[:, :, :], affinity[:, :, :],
                                            r_top[:, :].unsqueeze(2).to_broadcast([P, 2, EXPERTS]), ALU.mult))
                    if b >= 2:
                        dve.wait_ge(t_route, b - 1)
                    if b == 0:
                        dve.wait_ge(zeroed, 6)
                    to = route[:, b % 2, :, :]
                    chain(dve.tensor_copy(to[:, :, 0:EXPERTS].bitcast(F32R), affinity[:, :, :]))
                    dve.tensor_tensor(to[:, :, EXPERTS:2 * EXPERTS], affinity[:, :, :], to[:, :, 0:EXPERTS],
                                      ALU.subtract).then_inc(route_ready, 1)

            for n in range(3):
                split_qkc(2, n)
            values(2)
            maxima(0)
            blocks_const(3, copy=1).then_inc(key_blocks1_set, 1)
            maxima(1)
            for i in range(STEPS):
                if i + 2 < STEPS:
                    maxima(i + 2, i - 2)
                else:
                    normalize(i - 2)
                    for name, b in between_at.get(i, ()):
                        long_part(name, b)
                for name, b in tail_at.get(i, ()):
                    tail(name, b)
                if ("router", (i - 10) // 4) in tail_at.get(i - 1, ()):
                    long_part("weights", (i - 10) // 4)
                for name, b in tail_at.get(i, ()):
                    tail_rest(name, b)
                if i == 2:
                    dve.wait_ge(w_qkv_rounded, 3)
                    lo_half(w_qkv_lo[:, 4, :], w_qkv[:, 4, :], w_qkv_hi[:, 4, :], w_qkv_split)
                    dve.wait_ge(w_r_rounded, 1)
                    lo_half(w_r_lo[:, :], w_r[:, :], w_r_hi[:, :], w_r_split)
                    dve.wait_ge(b_down_rounded, 1)
                    lo_half(b_down_lo[:, :], b_down[:, :], b_down_hi[:, :], b_down_split)

            def residual(c, part, turned, done):
                first = (CHUNK * c + part.start) // P
                tiles = slice(first, first + (part.stop - part.start) // P)
                dve.wait_ge(t_ffn, done)
                dve.tensor_tensor(result[:, tiles, :], turned.rearrange("p (t h) -> p t h", h=C),
                                  x1[:, tiles, :], ALU.add).then_inc(result_ready, 1)

            def left_over(n, slot):
                name, b = v_beside.get((n, slot), ("", 0))
                if name == "norm":
                    long_part(name, b)
                name, b = beside.get((n, slot), ("", 0))
                if name == "turn_out":
                    normalize(b)
                tail(name, b)
                name, b = v_beside.get((n, slot), ("", 0))
                if name == "weights":
                    long_part(name, b)
                tail_rest(name, b)

            def lower_half(n):
                dve.wait_ge(hid_rounded, n + 1)
                dve.wait_ge(m_down, n - 2)
                k, rows = n % 3, rows_of(n)
                lo_half(hid_lo[rows, k, :], hid[rows, k, :], hid_hi[rows, k, :], hid_lo_done)

            for n in range(ITEMS):
                left_over(n, "A")
                if n == 0:
                    left_over(n, "B")
                u, _ = WORK[n]
                if u != SHARED:
                    dve.wait_ge(m_up, routed(n + 1))
                    dve.wait_ge(gate_done, n + 1)
                    dve.scalar_tensor_tensor(out=gated[:, n % 3, :], in0=bank(B_UP + n % 2),
                                             scalar=bias_cols[:, BIAS_UP + u:BIAS_UP + u + 1],
                                             in1=gate[:, n % 3, :], op0=ALU.add, op1=ALU.mult).then_inc(gated_done, 1)
                if n:
                    left_over(n, "B")
                if n - 1 in VECTOR_LO and n < LAST_ITEM:
                    lower_half(n - 1)
                if n >= 3:
                    dve.wait_ge(hid_rounded, n - 2)
                    dve.wait_ge(*lo_done(n - 3))
                if u != SHARED:
                    dve.wait_ge(m_wide, routed(n + 1))
                    dve.wait_ge(gated_done, routed(n + 1))
                    dve.tensor_tensor(hid[:, n % 3, :], gated[:, n % 3, :], bank(B_WIDE + n % 2),
                                      ALU.mult).then_inc(hid_done, 1)
                else:
                    for h, part in enumerate((slice(0, CHUNK),) if n < LAST_ITEM else HALVES):
                        dve.wait_ge(gate_done, n + 1 + h)
                        dve.scalar_tensor_tensor(out=hid[INNER:P, n % 3, part],
                                                 in0=psum[INNER:P, B_GATE + n % 2, part],
                                                 scalar=bias_cols[INNER:P, BIAS_UP + u:BIAS_UP + u + 1],
                                                 in1=gate[INNER:P, n % 3, part], op0=ALU.add, op1=ALU.mult
                                                 ).then_inc(hid_done if n < LAST_ITEM else last_hid, 1)
                left_over(n, "C")
            lower_half(LAST_ITEM - 1)
            k = LAST_ITEM % 3
            for h, part in enumerate(HALVES):
                dve.wait_ge(last_hi, h + 1)
                if h == 0:
                    dve.wait_ge(m_down, LAST_ITEM - 2)
                lo_half(hid_lo[INNER:P, k, part], hid[INNER:P, k, part], hid_hi[INNER:P, k, part], last_lo)
            residual(0, slice(0, CHUNK), bank(6), 1)
            for h, part in enumerate(HALVES):
                residual(1, part, bank(h, HALF), 2 + h)

        def turn_ffn(pe, part, to, nth):
            pe.wait_ge(ffnT_copied, nth)
            for k in range((part.stop - part.start) // P):
                ins = pe.transpose(to[:, P * k:P * (k + 1)], ffnT[:, part.start + P * k:part.start + P * (k + 1)],
                                   ident[:, :])
            ins.then_inc(t_ffn, 1)

        @block.tensor
        def _(pe):
            misc_read = []

            def take_misc(reader, count):
                if misc_read:
                    pe.wait_ge(*misc_read.pop())
                if reader:
                    misc_read.append((reader, count))

            def product3(dst, w_hi, w_lo, x_hi, x_lo, start=True, stop=True):
                pe.matmul(dst, w_hi, x_hi, start=start, stop=False, skip_group_check=True)
                pe.matmul(dst, w_hi, x_lo, start=False, stop=False, skip_group_check=True)
                return pe.matmul(dst, w_lo, x_hi, start=False, stop=stop, skip_group_check=True)

            def turn_x(b):
                if b >= 2:
                    pe.wait_ge(xT_split, b - 1)
                for k in range(2):
                    if b < 2:
                        pe.wait_ge(x_normed, 2 * b + k + 1)
                    else:
                        pe.wait_ge(late_x_normed, 2 * (b - 2) + k + 1)
                    ins = pe.transpose(psum[:, b % 2, P * k:P * (k + 1)], x1[:, 2 * b + k, :], ident[:, :])
                ins.then_inc(t_x, 1)

            def project(b):
                pe.wait_ge(xT_split, b + 1)
                if b == 0:
                    pe.wait_ge(w_qkv_split, 1)
                for n, (tensor, _) in enumerate(ORDER):
                    if b:
                        pe.wait_ge(qkc_split, 3 * (b - 1) + n + 1)
                    if b == 0 and n == 2:
                        pe.wait_ge(w_qkv_split, 2)
                    product3(bank(B_QKC + n, SEQ), w_qkv_hi[:, tensor, :], w_qkv_lo[:, tensor, :],
                             xT_hi[:, tokens(b)], xT_lo[:, tokens(b)]).then_inc(m_qkc, 1)
                if b:
                    pe.wait_ge(have_value, b)
                for k in range(2):
                    t = tokens(b, k)
                    ins = product3(psum[:, B_VALUE, P * k:P * (k + 1)], xT_hi[:, t], xT_lo[:, t], w_qkv_hi[:, 3, :],
                                   w_qkv_lo[:, 3, :])
                ins.then_inc(m_v, 1)

            pe.wait_ge(have_ident, 1)
            pe.wait_ge(in_ctx, 16)
            for h in range(2):
                ins = pe.transpose(psum[0:CTX_C, B_VALUE, P * h:P * (h + 1)], ctx_sb[:, h, :], ident[:, :])
            ins.then_inc(t_ctx, 1)
            turn_x(0)
            pe.wait_ge(have_ctxT, 1)
            pe.wait_ge(have_w_ck, 1)
            pe.matmul(bank(B_CK, CTX_KEYS), w_ctx[:, 2, :], ctxT[:, :, 0, :], start=True,
                      stop=True).then_inc(m_ck, 1)
            pe.wait_ge(qkc_bias_stacked, 1)
            pe.transpose(bank(B_CV, 4), qkc_bias[:, 1, :], ident[0:4, 0:4]).then_inc(t_bias, 1)
            pe.wait_ge(out_zeroed, 1)
            project(0)
            turn_x(1)
            pe.wait_ge(in_w_cv, 16)
            pe.wait_ge(have_bias_cols, 1)
            for b in range(BATCH):
                ins = pe.matmul(psum[:, B_CV, C * b:C * (b + 1)], ctxT[:, b, :, :], w_ctx[:, 1, :], start=True,
                                stop=True)
            ins.then_inc(m_cv, 1)
            project(1)
            turn_x(2)
            turn_x(3)

            def natural(i):
                b, g = divmod(i, GROUPS)
                KR = SHIFT_ROW
                if i:
                    pe.wait_ge(max_done, 3 * i)
                else:
                    pe.wait_ge(xT_split, BATCH)
                    pe.wait_ge(have_cvalue, 2)
                    pe.wait_ge(ck_split, 1)
                    pe.wait_ge(have_causal, 1)
                    pe.wait_ge(have_idents, 1)
                if g == 0:
                    pe.wait_ge(placed_k[b % 2], 64 * (b // 2 + 1))
                    pe.wait_ge(placed_q[b % 2], 16 * (b // 2 + 1))
                blocks = key_blocks[0:KR, b % 2, g, :, :]

                def masked(to, q, k):
                    diagonal = q == k
                    if diagonal:
                        pe.matmul(to, ident_bf[:, :], causal[:, :, :], start=True, stop=False, skip_group_check=True)
                    return pe.matmul(to, query_rows[0:KR, b % 2, g, 0, P * q:P * (q + 1)],
                                     blocks[:, :, P * k:P * (k + 1)],
                                     start=not diagonal, stop=True, skip_group_check=True)

                def tile_1():
                    masked(bank(B_NAT1), 1, 0)
                    masked(bank(B_NAT1 + 1), 1, 1).then_inc(m_nat, 1)

                masked(bank(B_NAT0), 0, 0).then_inc(m_nat, 1)
                if i == 0:
                    tile_1()
                    project(BATCH - 1)
                    pe.wait_ge(placed_ck, 64)
                for t in range(2):
                    ins = pe.matmul(psum[:, B_NATC, SEQ * t:SEQ * (t + 1)],
                                    query_rows[0:KR, b % 2, g, 1, P * t:P * (t + 1)],
                                    ckey_blocks[0:KR, g, b, :, :], start=True, stop=True)
                ins.then_inc(m_nat, 1)
                if i:
                    tile_1()

            def turn_max(i):
                pe.wait_ge(max_done, 3 * i + 3)
                take_misc(shift_placed, i + 1)
                for n in range(4):
                    ins = pe.matmul(psum[0:GROUP, B_MISC, P * n:P * (n + 1)], row_max[:, i % 2, n, :],
                                    ident_r[:, :], start=True, stop=True)
                ins.then_inc(t_max, 1)

            def scores(i, c):
                b, g = divmod(i, GROUPS)
                if c == 0:
                    pe.wait_ge(shift_placed, i + 1)
                if i or c >= 2:
                    pe.wait_ge(exp_done, 4 * i + c - 1)
                to = B_ST + c % 2
                if c < 2:
                    for j in range(2):
                        ins = pe.matmul(psum[:, to, SEQ * j:SEQ * (j + 1)],
                                        key_blocks[0:ROWS, b % 2, g, 2 * c + j, 0:P],
                                        query_rows[0:ROWS, b % 2, g, 0, :], start=True, stop=True)
                if c == 2:
                    for j in range(GROUP):
                        ins = pe.matmul(psum[:, to, P * j:P * (j + 1)], key_blocks[0:ROWS, b % 2, g, j, P:SEQ],
                                        query_rows[0:ROWS, b % 2, g, 0, P:SEQ], start=True, stop=True)
                if c == 3:
                    for j in range(2):
                        ins = pe.matmul(psum[:, to, SEQ * j:SEQ * (j + 1)],
                                        ckey_blocks[0:ROWS, g, b, 2 * j:2 * j + 2, :].rearrange("p j k -> p (j k)"),
                                        query_rows[0:ROWS, b % 2, g, 1, :], start=True, stop=True)
                ins.then_inc(m_st, 1)

            def attend_self(i):
                b, g = divmod(i, GROUPS)
                if i:
                    pe.wait_ge(o_copied, i)
                else:
                    pe.wait_ge(out_zeroed, 1)
                pe.wait_ge(selected, 2 * i + 1)
                for j in range(GROUP):
                    pe.matmul(psum[32 * j:32 * j + D + 1, B_OUT, 0:SEQ], value[:, 2 * b, GROUP * g + j, :],
                              probs[i % 2][:, j // 2, SEQ * (j % 2):SEQ * (j % 2 + 1)], start=True, stop=False,
                              skip_group_check=True)
                pe.wait_ge(selected, 2 * i + 2)
                for j in range(GROUP):
                    pe.matmul(psum[32 * j:32 * j + D + 1, B_OUT, P:SEQ], value[:, 2 * b + 1, GROUP * g + j, :],
                              probs[i % 2][:, 2, P * j:P * (j + 1)], start=False, stop=True, skip_group_check=True)

            def attend_context(i):
                b, g = divmod(i, GROUPS)
                pe.wait_ge(exp_done, 4 * i + 4)
                for j in range(2):
                    ins = pe.matmul(psum[64 * j:64 * j + 32 + D + 1, B_OUT, SEQ:2 * SEQ],
                                    cvalue[:, b, 2 * g + j, :], probs[i % 2][:, 3, SEQ * j:SEQ * (j + 1)],
                                    start=False, stop=True, skip_group_check=True)
                ins.then_inc(m_out, 1)

            def turn_out(i):
                pe.wait_ge(o_copied, i + 1)
                take_misc(normalized, i + 1)
                for n in range(4):
                    ins = pe.transpose(psum[:, B_MISC, P * n:P * (n + 1)], o_sb[:, i % 2, P * n:P * (n + 1)],
                                       ident[:, :])
                ins.then_inc(t_out, 1)

            def tail(name, b):
                take_misc({"ffn_bias": have_ffn_bias, "y_turn": yT_split, "project": x1_ready, "x2_turn": x2T_split,
                           "router": logits_ready,
                           "route_turn": routeT_ready}[name], b + 1)
                if name == "ffn_bias":
                    pe.wait_ge(in_small, 64)
                    pe.transpose(bank(B_MISC, 2 * UNITS), bias_rows[:, :],
                                 ident[0:2 * UNITS, 0:2 * UNITS]).then_inc(t_ffn_bias, 1)
                if name == "y_turn":
                    pe.wait_ge(y_added, 4 * b + 4)
                    for t in range(2):
                        ins = pe.transpose(psum[:, B_MISC, P * t:P * (t + 1)], y_nat[:, b % 2, t, :], ident[:, :])
                    ins.then_inc(t_y, 1)
                if name == "project":
                    pe.wait_ge(yT_split, b + 1)
                    pe.wait_ge(w_qkv_split, 3)
                    for t in range(2):
                        mine = slice(P * t, P * (t + 1))
                        ins = product3(psum[:, B_MISC, mine], yT_hi[:, mine], yT_lo[:, mine], w_qkv_hi[:, 4, :],
                                       w_qkv_lo[:, 4, :])
                    ins.then_inc(m_proj, 1)
                if name == "x2_turn":
                    pe.wait_ge(x2_normed, 2 * b + 2)
                    for t in range(2):
                        ins = pe.transpose(psum[:, B_MISC, P * t:P * (t + 1)], x2_norm[:, t, :], ident[:, :])
                    ins.then_inc(t_x2, 1)
                if name == "router":
                    pe.wait_ge(x2T_split, b + 1)
                    pe.wait_ge(w_r_split, 1)
                    for t in range(2):
                        ins = product3(psum[:, B_MISC, EXPERTS * t:EXPERTS * (t + 1)], xT_hi[:, tokens(b, t)],
                                       xT_lo[:, tokens(b, t)], w_r_hi[:, :], w_r_lo[:, :])
                    ins.then_inc(m_router, 1)
                if name == "route_turn":
                    pe.wait_ge(route_ready, b + 1)
                    for t in range(2):
                        ins = pe.transpose(psum[:, B_MISC, P * t:P * (t + 1)], route[:, b % 2, t, :], ident[:, :])
                    ins.then_inc(t_route, 1)

            project(2)
            natural(0)
            pe.wait_ge(have_value, BATCH)
            turn_max(0)
            natural(1)
            pe.wait_ge(qkc_split, 3 * BATCH)
            for i in range(STEPS):
                scores(i, 0)
                scores(i, 1)
                if i + 1 < STEPS:
                    turn_max(i + 1)
                if i + 2 < STEPS:
                    natural(i + 2)
                    scores(i, 2)
                    if i >= 2:
                        turn_out(i - 2)
                    scores(i, 3)
                    if i:
                        attend_self(i - 1)
                else:
                    attend_self(i - 1)
                    turn_out(i - 2)
                    scores(i, 2)
                    scores(i, 3)
                for name, b in tail_at.get(i, ()):
                    tail(name, b)
                if i:
                    attend_context(i - 1)
                for name, b in late_at.get(i, ()):
                    tail(name, b)

            def left_over(n, slot):
                name, b = beside.get((n, slot), ("", 0))
                if name == "attend":
                    attend_self(b)
                    attend_context(b)
                elif name == "turn_out":
                    turn_out(b)
                elif name:
                    tail(name, b)

            pe.wait_ge(b_down_split, 1)
            for n in range(ITEMS + 2):
                if n < ITEMS:
                    u, c = WORK[n]
                    k = u % SLOTS
                    cols = slice(c * CHUNK, (c + 1) * CHUNK)
                    if u == 0:
                        pe.wait_ge(x2T_split, 2 * c + 2)
                    pe.wait_ge(ffn_lo, u + 1)
                    if n >= 2:
                        pe.wait_ge(gate_done, n - 1)
                        if WORK[n - 2][0] == SHARED:
                            pe.wait_ge(hid_done, n - 1)
                    product3(bank(B_GATE + n % 2), w_ffn_hi[:, k, 0, :], w_ffn_lo[:, k, 0, :], xT_hi[:, cols],
                             xT_lo[:, cols]).then_inc(m_gate, 1)
                    left_over(n, "A")
                    if u != SHARED:
                        if n >= 2:
                            pe.wait_ge(gated_done, routed(n - 1))
                        product3(bank(B_UP + n % 2), w_ffn_hi[:, k, 1, :], w_ffn_lo[:, k, 1, :], xT_hi[:, cols],
                                 xT_lo[:, cols]).then_inc(m_up, 1)
                    left_over(n, "B")
                    if u == 0:
                        pe.wait_ge(routeT_ready, 2 * c + 2)
                    if u != SHARED:
                        if n >= 2:
                            pe.wait_ge(hid_done, n - 1)
                        pe.matmul(bank(B_WIDE + n % 2), spread[:, u, :], routeT[:, cols], start=True,
                                  stop=True).then_inc(m_wide, 1)
                if n >= 2:
                    m = n - 2
                    u, c = WORK[m]
                    k = u % SLOTS
                    cols = slice(c * CHUNK, (c + 1) * CHUNK)
                    y = bank(6 + c)
                    rows = rows_of(m)
                    if u == 0:
                        if c:
                            take_misc(None, 0)
                        pe.matmul(y, b_down_hi[:, :], routeT[:, cols], start=True, stop=False, skip_group_check=True)
                        pe.matmul(y, b_down_lo[:, :], routeT[:, cols], start=False, stop=False, skip_group_check=True)
                    if m < LAST_ITEM:
                        pe.wait_ge(*lo_done(m))
                        product3(y, w_ffn_hi[rows, k, 2, :], w_ffn_lo[rows, k, 2, :], hid_hi[rows, m % 3, :],
                                 hid_lo[rows, m % 3, :], start=False, stop=u == UNITS - 1).then_inc(m_down, 1)
                    else:
                        for h, part in enumerate(HALVES):
                            pe.wait_ge(last_lo, h + 1)
                            ins = product3(y[:, part], w_ffn_hi[rows, k, 2, :], w_ffn_lo[rows, k, 2, :],
                                           hid_hi[rows, m % 3, part], hid_lo[rows, m % 3, part], start=False)
                        ins.then_inc(m_down, 1)
                left_over(n, "C")
                if n == CHUNK_DONE[0] + 4:
                    turn_ffn(pe, slice(0, CHUNK), bank(6), 1)
            for h, part in enumerate(HALVES):
                turn_ffn(pe, part, bank(h), 2 + h)


NAMES = {
    "L0_xattn_": ("Wk", "bk", "Wq", "bq", "Wv", "bv", "Wck", "bck", "Wcq", "bcq", "Wcv", "bcv", "Wp", "bp"),
    "L0_ffn_": ("Wr", "br", "Wg_s", "bg_s", "Wu_s", "bu_s", "Wd_s", "bd_s", "Wg", "bg", "Wu", "bu", "Wd", "bd"),
}


def kernel(**inputs):
    import concourse.bacc as bacc
    import numpy as np
    from concourse.bass_utils import run_bass_kernel_spmd

    nc = bacc.Bacc("TRN2", target_bir_lowering=False, num_devices=1)
    arrays = {}

    def declare(name):
        a = np.ascontiguousarray(inputs[name])
        arrays[f"in_{name}"] = a
        return nc.dram_tensor(f"in_{name}", a.shape, mybir.dt.from_np(a.dtype), kind="ExternalInput").ap()

    x = declare("x")
    ctx = declare("ctx_512")
    w = {short: declare(prefix + short) for prefix, shorts in NAMES.items() for short in shorts}
    out = nc.dram_tensor("out_x", (BATCH, SEQ, C), F32, kind="ExternalOutput").ap()
    build(nc, x, ctx, w, out)
    r = run_bass_kernel_spmd(nc, [arrays], core_ids=[0])
    return r.results[0]["out_x"]
```
